# Optimizing a Trainium2 kernel written in Bass

```python
import numpy as np
import jax
import jax.numpy as jnp

def _softmax(x, axis=-1):
    return jax.nn.softmax(x, axis=axis)

def _gelu(x):
    return jax.nn.gelu(x, approximate=True)

def _silu(x):
    return jax.nn.silu(x)

def _sigmoid(x):
    return jax.nn.sigmoid(x)

def _layernorm(x, axis=-1, eps=1e-05):
    m = jnp.mean(x, axis=axis, keepdims=True)
    v = jnp.var(x, axis=axis, keepdims=True)
    return (x - m) / jnp.sqrt(v + eps)

def _scatter_add(tgt, idx, src, axis=0):
    return tgt.at[idx].add(src)

def _segment_sum(src, seg, n):
    return jax.ops.segment_sum(src, seg, n)
kernel_name = 'mk_lm_tower_d2_tok_ids1024_r4_16020e'

def setup_inputs(seed: int=0):
    np.random.seed(seed)
    _w = jnp.asarray

    def _rec_inputs():
        import jax
        import jax.numpy as jnp
        _rk = jax.random.key(seed)
        x = jax.random.randint(jax.random.fold_in(_rk, 1), (16, 256), 0, 12564, jnp.int32)
        return x
    x = _rec_inputs()

    def _L0_tok_setup():
        import math
        import jax, jax.numpy as jnp
        import numpy as np
        D_VOCAB = 50257
        D_MODEL = 256
        key = jax.random.key(seed)
        k_tok, k_w = jax.random.split(key)
        tokens = jax.random.randint(k_tok, (8, 512), 0, D_VOCAB)
        W_E = jax.random.normal(k_w, (D_VOCAB, D_MODEL), dtype=jnp.float32)
        return {'tokens': tokens, 'W_E': W_E}
    _L0_tok_all = _L0_tok_setup()
    _L0_tok_in = {k: v for k, v in _L0_tok_all.items() if k in ('W_E',)}
    del _L0_tok_all

    def _L0_attn_setup():
        import jax, jax.numpy as jnp
        import numpy as np
        LN_EPS = 1e-05
        WKV_EPS = 1e-08

        def _layernorm(x, g, b):
            mu = jnp.mean(x, axis=-1, keepdims=True)
            var = jnp.mean((x - mu) ** 2, axis=-1, keepdims=True)
            return (x - mu) * jax.lax.rsqrt(var + LN_EPS) * g + b

        def _time_mix(xn, Wr, Ww, Wk, Wv, Wo, time_decay):
            r = jax.nn.sigmoid(jnp.einsum('bsd,ed->bse', xn, Wr))
            w = -jnp.exp(jnp.einsum('bsd,ed->bse', xn, Ww))
            k = jnp.einsum('bsd,ed->bse', xn, Wk)
            v = jnp.einsum('bsd,ed->bse', xn, Wv)
            ewk = jnp.exp(w + k)
            decay = jnp.exp(time_decay)

            def step(carry, inp):
                num, den = carry
                e, vt = inp
                num = decay * num + e * vt
                den = decay * den + e
                wkv = num / (den + WKV_EPS)
                return ((num, den), wkv)
            B, S, D = xn.shape
            init = (jnp.zeros((B, D), xn.dtype), jnp.zeros((B, D), xn.dtype))
            (num_f, den_f), wkv = jax.lax.scan(step, init, (jnp.swapaxes(ewk, 0, 1), jnp.swapaxes(v, 0, 1)))
            wkv = jnp.swapaxes(wkv, 0, 1)
            out = jnp.einsum('bsd,ed->bse', r * wkv, Wo)
            final_state = jnp.stack([num_f, den_f], axis=1)
            return (out, final_state)

        def _channel_mix(xn, Wkey, Wval, Wrec):
            k = jnp.einsum('bsd,fd->bsf', xn, Wkey)
            k = jnp.square(jax.nn.relu(k))
            v = jnp.einsum('bsf,df->bsd', k, Wval)
            r = jax.nn.sigmoid(jnp.einsum('bsd,ed->bse', xn, Wrec))
            return r * v

        def _reference_tuple_inner(x, ln1_g, ln1_b, ln2_g, ln2_b, Wr, Ww, Wk, Wv, Wo, time_decay, time_first, Wkey, Wval, Wrec):
            tm, new_state = _time_mix(_layernorm(x, ln1_g, ln1_b), Wr, Ww, Wk, Wv, Wo, time_decay)
            x = x + tm
            x = x + _channel_mix(_layernorm(x, ln2_g, ln2_b), Wkey, Wval, Wrec)
            return (x, new_state)
        key = jax.random.key(seed)
        ks = jax.random.split(key, 16)
        B, S, D, F = (4, 512, 256, 1024)
        xavier_d = float(np.sqrt(6.0 / (D + D)))
        xavier_df = float(np.sqrt(6.0 / (D + F)))
        u = lambda k, sh, s: jax.random.uniform(k, sh, jnp.float32, -s, s)
        return {'x': jax.random.normal(ks[0], (B, S, D), jnp.float32), 'ln1_g': jnp.ones((D,), jnp.float32), 'ln1_b': jnp.zeros((D,), jnp.float32), 'ln2_g': jnp.ones((D,), jnp.float32), 'ln2_b': jnp.zeros((D,), jnp.float32), 'Wr': u(ks[1], (D, D), xavier_d), 'Ww': u(ks[2], (D, D), xavier_d), 'Wk': u(ks[3], (D, D), xavier_d), 'Wv': u(ks[4], (D, D), xavier_d), 'Wo': u(ks[5], (D, D), xavier_d), 'time_decay': jax.random.uniform(ks[6], (D,), jnp.float32, -1.0, 0.0), 'time_first': jax.random.uniform(ks[7], (D,), jnp.float32, -1.0, 1.0), 'Wkey': u(ks[8], (F, D), xavier_df), 'Wval': u(ks[9], (D, F), xavier_df), 'Wrec': u(ks[10], (D, D), xavier_d)}
    _L0_attn_all = _L0_attn_setup()
    _L0_attn_in = {k: v for k, v in _L0_attn_all.items() if k in ('ln1_g', 'ln1_b', 'ln2_g', 'ln2_b', 'Wr', 'Ww', 'Wk', 'Wv', 'Wo', 'time_decay', 'time_first', 'Wkey', 'Wval', 'Wrec')}
    del _L0_attn_all

    def _L0_ffn_setup():
        import jax, jax.numpy as jnp
        import numpy as np
        from jax import lax
        D = 256
        H = 1024
        E = 8
        TOPK = 2
        key = jax.random.key(seed)
        ks = jax.random.split(key, 7)
        s = 0.02
        return {'x': jax.random.normal(ks[0], (2, 512, D), dtype=jnp.float32), 'W1': jax.random.normal(ks[1], (E, D, H), dtype=jnp.float32) * s, 'b1': jnp.zeros((E, H), dtype=jnp.float32), 'W2': jax.random.normal(ks[2], (E, H, D), dtype=jnp.float32) * s, 'b2': jnp.zeros((E, D), dtype=jnp.float32), 'Wr': jax.random.normal(ks[3], (D, E), dtype=jnp.float32) * s, 'br': jnp.zeros((E,), dtype=jnp.float32)}
    _L0_ffn_all = _L0_ffn_setup()
    _L0_ffn_in = {k: v for k, v in _L0_ffn_all.items() if k in ('W1', 'b1', 'W2', 'b2', 'Wr', 'br')}
    del _L0_ffn_all

    def _L1_attn_setup():
        import jax, jax.numpy as jnp
        import numpy as np
        import math
        NEG_INF = -1e+38

        def wkv_scan(w, u, k, v):
            B, T, C = k.shape

            def step(carry, kv_t):
                a, b, pp = carry
                kt, vt = kv_t
                ww = u + kt
                q = jnp.maximum(pp, ww)
                e1 = jnp.exp(pp - q)
                e2 = jnp.exp(ww - q)
                y = (e1 * a + e2 * vt) / (e1 * b + e2)
                ww2 = pp + w
                q2 = jnp.maximum(ww2, kt)
                e1b = jnp.exp(ww2 - q2)
                e2b = jnp.exp(kt - q2)
                return ((e1b * a + e2b * vt, e1b * b + e2b, q2), y)
            init = (jnp.zeros((B, C), k.dtype), jnp.zeros((B, C), k.dtype), jnp.full((B, C), NEG_INF, k.dtype))
            kT = jnp.swapaxes(k, 0, 1)
            vT = jnp.swapaxes(v, 0, 1)
            _, ys = jax.lax.scan(step, init, (kT, vT))
            return jnp.swapaxes(ys, 0, 1)
        key = jax.random.key(seed)
        B, T, C = (16, 256, 256)
        k1, k2, k3, k4 = jax.random.split(key, 4)
        x = jax.random.normal(k1, (B, T, C), dtype=jnp.float32)
        scale = 0.02
        Wk = jax.random.normal(k2, (C, C), dtype=jnp.float32) * scale
        Wr = jax.random.normal(k3, (C, C), dtype=jnp.float32) * scale
        Wo = jax.random.normal(k4, (C, C), dtype=jnp.float32) * scale
        h = np.arange(C, dtype=np.float64)
        decay_speed = -5.0 + 8.0 * (h / (C - 1)) ** (0.7 + 1.3 * 1)
        zigzag = ((np.arange(C) + 1) % 3 - 1) * 0.5
        time_first = np.ones(C) * math.log(0.3) + zigzag
        return {'x': x, 'Wk': Wk, 'Wr': Wr, 'Wo': Wo, 'time_decay': jnp.asarray(decay_speed, dtype=jnp.float32), 'time_first': jnp.asarray(time_first, dtype=jnp.float32)}
    _L1_attn_all = _L1_attn_setup()
    _L1_attn_in = {k: v for k, v in _L1_attn_all.items() if k in ('Wk', 'Wr', 'Wo', 'time_decay', 'time_first')}
    del _L1_attn_all

    def _L1_ffn_setup():
        import jax, jax.numpy as jnp
        import numpy as np
        DIM = 256
        HEADS = 16
        HD = DIM // HEADS
        M = 64
        E = 4
        K = 2
        HID = 512
        MID = 512
        LB = 0.01
        EPS = 1.1920929e-07

        def _rms(x, w):
            return x * jax.lax.rsqrt(jnp.mean(x * x, axis=-1, keepdims=True) + EPS) * w

        def _gelu(x):
            return jax.nn.gelu(x, approximate=False)
        key = jax.random.key(seed)
        ks = jax.random.split(key, 20)
        d = DIM
        w = lambda k, s: jax.random.normal(k, s, jnp.float32) * 0.02
        return {'x': jax.random.normal(ks[0], (4, 256, d), jnp.float32), 'n1_w': jnp.ones((d,), jnp.float32), 'n2_w': jnp.ones((d,), jnp.float32), 'wq': w(ks[1], (d, d)), 'wk': w(ks[2], (d, d)), 'wv': w(ks[3], (d, d)), 'wo': w(ks[4], (d, d)), 'qn_w': jnp.ones((HD,), jnp.float32), 'kn_w': jnp.ones((HD,), jnp.float32), 'gate_w': w(ks[5], (E, d)), 'e0_up': w(ks[6], (HID, d)), 'e0_down': w(ks[7], (d, HID)), 'e1_w1': w(ks[8], (HID, d)), 'e1_w2': w(ks[9], (HID, d)), 'e1_down': w(ks[10], (d, HID)), 'e2_l1': w(ks[11], (MID, d)), 'e2_l2': w(ks[12], (HID, MID)), 'e2_l3': w(ks[13], (MID, HID)), 'e2_l4': w(ks[14], (d, MID)), 'e3_down': w(ks[15], (d, d)), 'e3_up': w(ks[16], (HID, d)), 'e3_out': w(ks[17], (d, HID))}
    _L1_ffn_all = _L1_ffn_setup()
    _L1_ffn_in = {k: v for k, v in _L1_ffn_all.items() if k in ('n1_w', 'n2_w', 'wq', 'wk', 'wv', 'wo', 'qn_w', 'kn_w', 'gate_w', 'e0_up', 'e0_down', 'e1_w1', 'e1_w2', 'e1_down', 'e2_l1', 'e2_l2', 'e2_l3', 'e2_l4', 'e3_down', 'e3_up', 'e3_out')}
    del _L1_ffn_all
    return {'x': x, 'L0_tok_W_E': _L0_tok_in['W_E'], 'L0_attn_ln1_g': _L0_attn_in['ln1_g'], 'L0_attn_ln1_b': _L0_attn_in['ln1_b'], 'L0_attn_ln2_g': _L0_attn_in['ln2_g'], 'L0_attn_ln2_b': _L0_attn_in['ln2_b'], 'L0_attn_Wr': _L0_attn_in['Wr'], 'L0_attn_Ww': _L0_attn_in['Ww'], 'L0_attn_Wk': _L0_attn_in['Wk'], 'L0_attn_Wv': _L0_attn_in['Wv'], 'L0_attn_Wo': _L0_attn_in['Wo'], 'L0_attn_time_decay': _L0_attn_in['time_decay'], 'L0_attn_time_first': _L0_attn_in['time_first'], 'L0_attn_Wkey': _L0_attn_in['Wkey'], 'L0_attn_Wval': _L0_attn_in['Wval'], 'L0_attn_Wrec': _L0_attn_in['Wrec'], 'L0_ffn_W1': _L0_ffn_in['W1'], 'L0_ffn_b1': _L0_ffn_in['b1'], 'L0_ffn_W2': _L0_ffn_in['W2'], 'L0_ffn_b2': _L0_ffn_in['b2'], 'L0_ffn_Wr': _L0_ffn_in['Wr'], 'L0_ffn_br': _L0_ffn_in['br'], 'L1_attn_Wk': _L1_attn_in['Wk'], 'L1_attn_Wr': _L1_attn_in['Wr'], 'L1_attn_Wo': _L1_attn_in['Wo'], 'L1_attn_time_decay': _L1_attn_in['time_decay'], 'L1_attn_time_first': _L1_attn_in['time_first'], 'L1_ffn_n1_w': _L1_ffn_in['n1_w'], 'L1_ffn_n2_w': _L1_ffn_in['n2_w'], 'L1_ffn_wq': _L1_ffn_in['wq'], 'L1_ffn_wk': _L1_ffn_in['wk'], 'L1_ffn_wv': _L1_ffn_in['wv'], 'L1_ffn_wo': _L1_ffn_in['wo'], 'L1_ffn_qn_w': _L1_ffn_in['qn_w'], 'L1_ffn_kn_w': _L1_ffn_in['kn_w'], 'L1_ffn_gate_w': _L1_ffn_in['gate_w'], 'L1_ffn_e0_up': _L1_ffn_in['e0_up'], 'L1_ffn_e0_down': _L1_ffn_in['e0_down'], 'L1_ffn_e1_w1': _L1_ffn_in['e1_w1'], 'L1_ffn_e1_w2': _L1_ffn_in['e1_w2'], 'L1_ffn_e1_down': _L1_ffn_in['e1_down'], 'L1_ffn_e2_l1': _L1_ffn_in['e2_l1'], 'L1_ffn_e2_l2': _L1_ffn_in['e2_l2'], 'L1_ffn_e2_l3': _L1_ffn_in['e2_l3'], 'L1_ffn_e2_l4': _L1_ffn_in['e2_l4'], 'L1_ffn_e3_down': _L1_ffn_in['e3_down'], 'L1_ffn_e3_up': _L1_ffn_in['e3_up'], 'L1_ffn_e3_out': _L1_ffn_in['e3_out']}

def reference(x, L0_tok_W_E, L0_attn_ln1_g, L0_attn_ln1_b, L0_attn_ln2_g, L0_attn_ln2_b, L0_attn_Wr, L0_attn_Ww, L0_attn_Wk, L0_attn_Wv, L0_attn_Wo, L0_attn_time_decay, L0_attn_time_first, L0_attn_Wkey, L0_attn_Wval, L0_attn_Wrec, L0_ffn_W1, L0_ffn_b1, L0_ffn_W2, L0_ffn_b2, L0_ffn_Wr, L0_ffn_br, L1_attn_Wk, L1_attn_Wr, L1_attn_Wo, L1_attn_time_decay, L1_attn_time_first, L1_ffn_n1_w, L1_ffn_n2_w, L1_ffn_wq, L1_ffn_wk, L1_ffn_wv, L1_ffn_wo, L1_ffn_qn_w, L1_ffn_kn_w, L1_ffn_gate_w, L1_ffn_e0_up, L1_ffn_e0_down, L1_ffn_e1_w1, L1_ffn_e1_w2, L1_ffn_e1_down, L1_ffn_e2_l1, L1_ffn_e2_l2, L1_ffn_e2_l3, L1_ffn_e2_l4, L1_ffn_e3_down, L1_ffn_e3_up, L1_ffn_e3_out):
    import jax
    import jax.numpy as jnp

    def _L0_tok_ref(tokens, W_E):
        import math
        import jax, jax.numpy as jnp
        import numpy as np
        D_VOCAB = 50257
        D_MODEL = 256
        scale = jnp.asarray(math.sqrt(W_E.shape[1]), dtype=W_E.dtype)
        return jnp.take(W_E, tokens, axis=0) * scale

    def _L0_attn_ref(x, ln1_g, ln1_b, ln2_g, ln2_b, Wr, Ww, Wk, Wv, Wo, time_decay, time_first, Wkey, Wval, Wrec):
        import jax, jax.numpy as jnp
        import numpy as np
        LN_EPS = 1e-05
        WKV_EPS = 1e-08

        def _layernorm(x, g, b):
            mu = jnp.mean(x, axis=-1, keepdims=True)
            var = jnp.mean((x - mu) ** 2, axis=-1, keepdims=True)
            return (x - mu) * jax.lax.rsqrt(var + LN_EPS) * g + b

        def _time_mix(xn, Wr, Ww, Wk, Wv, Wo, time_decay):
            r = jax.nn.sigmoid(jnp.einsum('bsd,ed->bse', xn, Wr))
            w = -jnp.exp(jnp.einsum('bsd,ed->bse', xn, Ww))
            k = jnp.einsum('bsd,ed->bse', xn, Wk)
            v = jnp.einsum('bsd,ed->bse', xn, Wv)
            ewk = jnp.exp(w + k)
            decay = jnp.exp(time_decay)

            def step(carry, inp):
                num, den = carry
                e, vt = inp
                num = decay * num + e * vt
                den = decay * den + e
                wkv = num / (den + WKV_EPS)
                return ((num, den), wkv)
            B, S, D = xn.shape
            init = (jnp.zeros((B, D), xn.dtype), jnp.zeros((B, D), xn.dtype))
            (num_f, den_f), wkv = jax.lax.scan(step, init, (jnp.swapaxes(ewk, 0, 1), jnp.swapaxes(v, 0, 1)))
            wkv = jnp.swapaxes(wkv, 0, 1)
            out = jnp.einsum('bsd,ed->bse', r * wkv, Wo)
            final_state = jnp.stack([num_f, den_f], axis=1)
            return (out, final_state)

        def _channel_mix(xn, Wkey, Wval, Wrec):
            k = jnp.einsum('bsd,fd->bsf', xn, Wkey)
            k = jnp.square(jax.nn.relu(k))
            v = jnp.einsum('bsf,df->bsd', k, Wval)
            r = jax.nn.sigmoid(jnp.einsum('bsd,ed->bse', xn, Wrec))
            return r * v

        def _reference_tuple_inner(x, ln1_g, ln1_b, ln2_g, ln2_b, Wr, Ww, Wk, Wv, Wo, time_decay, time_first, Wkey, Wval, Wrec):
            tm, new_state = _time_mix(_layernorm(x, ln1_g, ln1_b), Wr, Ww, Wk, Wv, Wo, time_decay)
            x = x + tm
            x = x + _channel_mix(_layernorm(x, ln2_g, ln2_b), Wkey, Wval, Wrec)
            return (x, new_state)
        return _reference_tuple_inner(x, ln1_g, ln1_b, ln2_g, ln2_b, Wr, Ww, Wk, Wv, Wo, time_decay, time_first, Wkey, Wval, Wrec)[0]

    def _L0_ffn_ref(x, W1, b1, W2, b2, Wr, br):
        import jax, jax.numpy as jnp
        import numpy as np
        from jax import lax
        D = 256
        H = 1024
        E = 8
        TOPK = 2
        B, S, _ = x.shape
        xf = x.reshape(-1, D)
        logits = xf @ Wr + br
        topv, _ = lax.top_k(logits, TOPK)
        thresh = topv[:, TOPK - 1:TOPK]
        masked = jnp.where(logits >= thresh, logits, -jnp.inf)
        weights = jax.nn.softmax(masked, axis=-1)
        h = jax.nn.gelu(jnp.einsum('td,edh->eth', xf, W1) + b1[:, None, :], approximate=False)
        expert_out = jnp.einsum('eth,ehd->etd', h, W2) + b2[:, None, :]
        out = jnp.einsum('etd,te->td', expert_out, weights)
        return out.reshape(B, S, D)

    def _L1_attn_ref(x, Wk, Wr, Wo, time_decay, time_first):
        import jax, jax.numpy as jnp
        import numpy as np
        import math
        NEG_INF = -1e+38

        def wkv_scan(w, u, k, v):
            B, T, C = k.shape

            def step(carry, kv_t):
                a, b, pp = carry
                kt, vt = kv_t
                ww = u + kt
                q = jnp.maximum(pp, ww)
                e1 = jnp.exp(pp - q)
                e2 = jnp.exp(ww - q)
                y = (e1 * a + e2 * vt) / (e1 * b + e2)
                ww2 = pp + w
                q2 = jnp.maximum(ww2, kt)
                e1b = jnp.exp(ww2 - q2)
                e2b = jnp.exp(kt - q2)
                return ((e1b * a + e2b * vt, e1b * b + e2b, q2), y)
            init = (jnp.zeros((B, C), k.dtype), jnp.zeros((B, C), k.dtype), jnp.full((B, C), NEG_INF, k.dtype))
            kT = jnp.swapaxes(k, 0, 1)
            vT = jnp.swapaxes(v, 0, 1)
            _, ys = jax.lax.scan(step, init, (kT, vT))
            return jnp.swapaxes(ys, 0, 1)
        k = jnp.einsum('btc,hc->bth', x, Wk)
        r = jnp.einsum('btc,hc->bth', x, Wr)
        v = r
        w = -jnp.exp(time_decay)
        y = wkv_scan(w, time_first, k, v)
        out = jax.nn.sigmoid(r) * y
        return jnp.einsum('bth,ch->btc', out, Wo)

    def _L1_ffn_ref(x, n1_w, n2_w, wq, wk, wv, wo, qn_w, kn_w, gate_w, e0_up, e0_down, e1_w1, e1_w2, e1_down, e2_l1, e2_l2, e2_l3, e2_l4, e3_down, e3_up, e3_out):
        import jax, jax.numpy as jnp
        import numpy as np
        DIM = 256
        HEADS = 16
        HD = DIM // HEADS
        M = 64
        E = 4
        K = 2
        HID = 512
        MID = 512
        LB = 0.01
        EPS = 1.1920929e-07

        def _rms(x, w):
            return x * jax.lax.rsqrt(jnp.mean(x * x, axis=-1, keepdims=True) + EPS) * w

        def _gelu(x):
            return jax.nn.gelu(x, approximate=False)
        B, T, C = x.shape
        h = _rms(x, n1_w)
        heads = lambda w_: (h @ w_.T).reshape(B, T, HEADS, HD).transpose(0, 2, 1, 3)
        q = _rms(heads(wq), qn_w)
        k = _rms(heads(wk), kn_w)
        v = heads(wv)
        scores = jnp.einsum('bhqd,bhkd->bhqk', q, k) * HD ** (-0.5)
        causal = jnp.tril(jnp.ones((T, T), bool))
        scores = jnp.where(causal[None, None], scores, -jnp.inf)
        attn = jax.nn.softmax(scores, axis=-1)
        ao = jnp.einsum('bhqk,bhkd->bhqd', attn, v).transpose(0, 2, 1, 3).reshape(B, T, C) @ wo.T
        ao = ao.at[:, :, :M].set(0.0)
        x = x + ao
        xf = _rms(x, n2_w).reshape(-1, C)
        N = xf.shape[0]
        logits = jnp.nan_to_num(xf @ gate_w.T)
        probs = jax.nn.softmax(logits, axis=-1)
        topv, topi = jax.lax.top_k(probs, K)
        topv = topv / (topv.sum(-1, keepdims=True) + 1e-08)
        wts = jnp.zeros((N, E), x.dtype).at[jnp.arange(N)[:, None], topi].add(topv)
        o0 = _gelu(xf @ e0_up.T) @ e0_down.T
        o1 = jax.nn.silu(xf @ e1_w1.T) * (xf @ e1_w2.T) @ e1_down.T
        o2 = _gelu(_gelu(_gelu(xf @ e2_l1.T) @ e2_l2.T) @ e2_l3.T) @ e2_l4.T
        o3 = _gelu(_gelu(xf @ e3_down.T) @ e3_up.T) @ e3_out.T
        moe = wts[:, 0:1] * o0 + wts[:, 1:2] * o1 + wts[:, 2:3] * o2 + wts[:, 3:4] * o3
        moe = moe.reshape(B, T, C).at[:, :, :M].set(0.0)
        return x + moe
    h = _L0_tok_ref(x, L0_tok_W_E)
    h = h + _L0_attn_ref(_layernorm(h, axis=-1), L0_attn_ln1_g, L0_attn_ln1_b, L0_attn_ln2_g, L0_attn_ln2_b, L0_attn_Wr, L0_attn_Ww, L0_attn_Wk, L0_attn_Wv, L0_attn_Wo, L0_attn_time_decay, L0_attn_time_first, L0_attn_Wkey, L0_attn_Wval, L0_attn_Wrec)
    h = h + _L0_ffn_ref(_layernorm(h, axis=-1), L0_ffn_W1, L0_ffn_b1, L0_ffn_W2, L0_ffn_b2, L0_ffn_Wr, L0_ffn_br)
    h = h + _L1_attn_ref(_layernorm(h, axis=-1), L1_attn_Wk, L1_attn_Wr, L1_attn_Wo, L1_attn_time_decay, L1_attn_time_first)
    h = h + _L1_ffn_ref(_layernorm(h, axis=-1), L1_ffn_n1_w, L1_ffn_n2_w, L1_ffn_wq, L1_ffn_wk, L1_ffn_wv, L1_ffn_wo, L1_ffn_qn_w, L1_ffn_kn_w, L1_ffn_gate_w, L1_ffn_e0_up, L1_ffn_e0_down, L1_ffn_e1_w1, L1_ffn_e1_w2, L1_ffn_e1_down, L1_ffn_e2_l1, L1_ffn_e2_l2, L1_ffn_e2_l3, L1_ffn_e2_l4, L1_ffn_e3_down, L1_ffn_e3_up, L1_ffn_e3_out)
    return h

_drawn_inputs = setup_inputs


def setup_inputs(seed=0):
    import zlib

    import numpy as np

    out = dict(_drawn_inputs(seed))
    spreads = {'L0_attn_ln1_g': (1.0, 0.6),
     'L0_attn_ln1_b': (0.0, 0.8),
     'L0_attn_ln2_g': (1.0, 0.6),
     'L0_attn_ln2_b': (0.0, 0.8),
     'L0_ffn_b1': (0.0, 0.8),
     'L0_ffn_b2': (0.0, 0.8),
     'L0_ffn_br': (0.0, 0.8),
     'L1_ffn_n1_w': (1.0, 0.6),
     'L1_ffn_n2_w': (1.0, 0.6),
     'L1_ffn_qn_w': (1.0, 0.6),
     'L1_ffn_kn_w': (1.0, 0.6)}
    factors = {'L0_attn_Wr': 6.704,
     'L0_attn_Ww': 5.297,
     'L0_attn_Wk': 4.905,
     'L0_attn_time_decay': 6.499,
     'L0_attn_Wkey': 2.806,
     'L0_attn_Wrec': 6.499,
     'L0_ffn_W1': 8.0,
     'L0_ffn_W2': 8.0,
     'L0_ffn_Wr': 8.0,
     'L1_attn_Wk': 8.0,
     'L1_attn_Wr': 8.0,
     'L1_attn_Wo': 8.0,
     'L1_attn_time_decay': 8.0,
     'L1_attn_time_first': 8.0,
     'L1_ffn_wq': 8.0,
     'L1_ffn_wk': 8.0,
     'L1_ffn_wv': 8.0,
     'L1_ffn_wo': 8.0,
     'L1_ffn_gate_w': 8.0,
     'L1_ffn_e0_up': 8.0,
     'L1_ffn_e0_down': 8.0,
     'L1_ffn_e1_w1': 8.0,
     'L1_ffn_e1_w2': 8.0,
     'L1_ffn_e1_down': 8.0,
     'L1_ffn_e2_l1': 8.0,
     'L1_ffn_e2_l2': 8.0,
     'L1_ffn_e2_l3': 8.0,
     'L1_ffn_e2_l4': 8.0,
     'L1_ffn_e3_down': 8.0,
     'L1_ffn_e3_up': 8.0,
     'L1_ffn_e3_out': 8.0}
    for name, (base, spread) in spreads.items():
        noise = np.random.default_rng([zlib.crc32(name.encode()), seed]).standard_normal(out[name].shape)
        drawn = base * np.exp(spread * noise) if base else spread * noise
        out[name] = jnp.asarray(drawn.astype(out[name].dtype))
    for name, factor in factors.items():
        out[name] = (out[name] * factor).astype(out[name].dtype)
    return out
```

```python
import concourse.bass as bass
from concourse import mybir
from contextlib import ExitStack

F32 = mybir.dt.float32
BF16 = mybir.dt.bfloat16
I32 = mybir.dt.int32
U32 = mybir.dt.uint32
ALU = mybir.AluOpType
ACT = mybir.ActivationFunctionType
AX = mybir.AxisListType

P = 128
BATCH, SEQ, D = 16, 256, 256
N = BATCH * SEQ
KC = D // P
TT = 512
TILES = N // TT
SUB = TT // P
SEQS = TT // SEQ
VOCAB = 50257
EMB_SCALE = float(D) ** 0.5
LN_EPS, WKV_EPS = 1e-5, 1e-8

F0 = 1024
OFF_A = {}
_at = 0
for _name, _k, _n in (("Ww", D, D), ("Wk", D, D), ("Wv", D, D), ("Wr", D, D), ("Wo", D, D),
                      ("Wrec", D, D), ("Wkey", D, F0), ("Wval", F0, D)):
    OFF_A[_name] = (_at, _n)
    _at += _k // P * _n
COLS_A = _at

E0, H0 = 8, 1024
HC0 = H0 // P
COLS_E = KC * H0 + HC0 * D

HEADS, HD = 16, 16
ZERO = 64
DZ = D - ZERO
E1, HID = 4, 512
OFF_C = {}
_at = 0
for _name, _k, _n in (("Wk", D, D), ("Wr", D, D), ("Wo", D, D),
                      ("wqk", D, 2 * D), ("wv", D, D), ("wo", D, DZ),
                      ("e0_up", D, HID), ("e0_down", HID, DZ),
                      ("e1_w1", D, HID), ("e1_w2", D, HID), ("e1_down", HID, DZ),
                      ("e2_l1", D, HID), ("e2_l2", HID, HID), ("e2_l3", HID, HID), ("e2_l4", HID, DZ),
                      ("e3_down", D, D), ("e3_up", D, HID), ("e3_out", HID, DZ)):
    OFF_C[_name] = (_at, _n)
    _at += _k // P * _n
COLS_C = _at


PIECES = E0 * TILES
PIECE_E, PIECE_C = COLS_E // TILES, COLS_C // PIECES
assert PIECE_C * PIECES == COLS_C

VEC = {n: 2 * i for i, n in enumerate(("ln1_g", "ln1_b", "ln2_g", "ln2_b", "decay0",
                                       "decay1", "first1", "n1_w", "n2_w"))}
NVEC = 2 * len(VEC)


class Count:

    def __init__(self, sem, per):
        self.sem, self.per = sem, per

    def at(self, t, n=None):
        return t * self.per + (self.per if n is None else n)


class Steps:

    def __init__(self, eng, count):
        self.eng, self.count = eng, count

    def begin(self, t):
        self.t, self.n = t, 0

    def done(self, ins):
        ins.then_inc(self.count.sem, 1)
        self.n += 1

    def settle(self):
        self.eng.wait_ge(self.count.sem, self.count.at(self.t, self.n))

    def end(self):
        assert self.n == self.count.per, (self.n, self.count.per)


class Chip:
    pass


def split_weights(nc, ctx, jobs, tag, engines, free=None):
    pass


def phase_load(nc, c):
    CH = 1024
    NCH = COLS_A // CH
    with ExitStack() as x:
        stage = x.enter_context(nc.sbuf_tensor("stage_a", [P, NCH, CH], F32))
        s_w = [x.enter_context(nc.semaphore(f"ld_weights{k}")) for k in range(NCH)]
        s_v = x.enter_context(nc.semaphore("ld_vectors"))
        s_hi = x.enter_context(nc.semaphore("ld_high"))
        s_lo = x.enter_context(nc.semaphore("ld_low"))
        s_c = x.enter_context(nc.semaphore("ld_constants"))
        s_d = x.enter_context(nc.semaphore("ld_decay"))
        block = x.enter_context(nc.Block())

        @block.sync
        def _(sp):
            for dst, src in ((c.tok, c.i["tok"]), (c.vec, c.i["vec"]), (c.b1, c.i["b1"]), (c.b2, c.i["b2"]),
                             (c.Wrt, c.i["Wrt"]), (c.br, c.i["br"]), (c.gate, c.i["gate"]),
                             (c.qkw[:, 0:HD], c.i["qn"].partition_broadcast(P)),
                             (c.qkw[:, HD:2 * HD], c.i["kn"].partition_broadcast(P))):
                sp.dma_start(dst[:, :] if dst is not c.qkw else dst, src).then_inc(s_v, 16)
            for k in range(NCH):
                sp.dma_start(stage[:, k, :], c.i["WA"][:, k * CH:(k + 1) * CH]).then_inc(s_w[k], 16)
            sp.wait_ge(s_v, 9 * 16)

        @block.scalar
        def _(act):
            act.wait_ge(s_v, 9 * 16)
            act.activation(c.dec[:, 0:4], c.vec[:, VEC["decay0"]:VEC["decay0"] + 4], ACT.Exp).then_inc(s_d, 1)
            for k in range(NCH):
                act.wait_ge(s_w[k], 16)
                act.activation(c.WA_hi[:, k * CH:(k + 1) * CH], stage[:, k, :], ACT.Copy).then_inc(s_hi, 1)

        @block.vector
        def _(dve):
            dve.memset(c.ones[:, :], 1.0).then_inc(s_c, 1)
            dve.memset(c.scr[:, :], 0.0).then_inc(s_c, 1)
            dve.memset(c.eps[:, 0:4], LN_EPS).then_inc(s_c, 1)
            dve.memset(c.eps[:, 4:8], -0.5).then_inc(s_c, 1)
            dve.memset(c.eps[:, 8:12], 1.1920929e-07).then_inc(s_c, 1)
            dve.memset(c.eps[:, 12:13], 1.0 / HD).then_inc(s_c, 1)
            dve.wait_ge(s_d, 1)
            dve.tensor_scalar(c.dec[:, 4:6], c.dec[:, 2:4], -1.0, None, ALU.mult).then_inc(s_c, 1)
            dve.wait_ge(s_v, 9 * 16)
            dve.tensor_scalar(c.qkw2[:, 0:HD], c.qkw[:, 0:HD], float(HD) ** -0.5, None, ALU.mult).then_inc(s_c, 1)
            dve.tensor_copy(c.qkw2[:, HD:2 * HD], c.qkw[:, HD:2 * HD]).then_inc(s_c, 1)
            for k in range(NCH):
                dve.wait_ge(s_hi, k + 1)
                dve.tensor_tensor(c.WA_lo[:, k * CH:(k + 1) * CH], stage[:, k, :],
                                  c.WA_hi[:, k * CH:(k + 1) * CH], ALU.subtract).then_inc(s_lo, 1)

        @block.gpsimd
        def _(pool):
            pool.memset(c.ident[:, :], 0.0).then_inc(s_c, 1)
            pool.memset(c.identb[:, :], 0.0).then_inc(s_c, 1)
            pool.memset(c.mask[:, :], 0.0).then_inc(s_c, 1)
            pool.memset(c.sel[:, :, :], 0.0).then_inc(s_c, 1)
            pool.memset(c.zero_i[:, :], 0).then_inc(s_c, 1)
            pool.wait_ge(s_c, 14)
            for m in (c.ident, c.identb):
                pool.affine_select(out=m[:, :], in_=m[:, :], compare_op=ALU.not_equal, fill=1.0, base=0,
                                   pattern=[[-1, P]], channel_multiplier=1).then_inc(s_c, 1)
            pool.affine_select(out=c.mask[:, 0:P], in_=c.mask[:, 0:P], compare_op=ALU.is_ge, fill=-1e30, base=0,
                               pattern=[[-1, P]], channel_multiplier=1).then_inc(s_c, 1)
            pool.affine_select(out=c.mask[:, P:2 * P], in_=c.mask[:, P:2 * P], compare_op=ALU.is_ge, fill=-1e30,
                               base=0, pattern=[[1, P]], channel_multiplier=-1).then_inc(s_c, 1)
            for j in range(3):
                pool.wait_ge(s_c, 18 + j)
                pool.affine_select(out=c.sel[:, :, :], in_=c.sel[:, :, :], compare_op=ALU.not_equal, fill=1.0,
                                   base=-j, pattern=[[-3, HEADS], [0, P]], channel_multiplier=1).then_inc(s_c, 1)


def phase_a(nc, c):
    KF, KB = 32, 30
    with ExitStack() as x:
        def sb(name, shape, dt=F32):
            return x.enter_context(nc.sbuf_tensor("a_" + name, shape, dt))

        def count(name, per):
            return Count(x.enter_context(nc.semaphore("a_" + name)), per)

        fb = [x.enter_context(nc.psum_tensor(f"a_front{k}", [P, TT], F32)) for k in range(4)]
        bb = [x.enter_context(nc.psum_tensor(f"a_back{k}", [P, TT], F32)) for k in range(4)]

        emb, h0, x1, xn = (sb(n, [P, SUB * D]) for n in ("emb", "h0", "x1", "xn"))
        fst, bst = sb("fst", [P, SUB, 6]), sb("bst", [P, SUB, 6])
        fmv, bmv = sb("fmv", [P, SUB, 2]), sb("bmv", [P, SUB, 2])
        frs, brs = sb("frs", [P, 2, SUB]), sb("brs", [P, 2, SUB])
        xf, xhi, xlo = sb("xf", [P, KC, TT]), sb("xhi", [P, KC, TT], BF16), sb("xlo", [P, KC, TT], BF16)
        ew, kw, ek, ev, num, den, tr = (sb(n, [P, KC, TT]) for n in ("ew", "kw", "ek", "ev", "num", "den", "tr"))
        z = ew
        zhi, zlo = sb("zhi", [P, KC, TT], BF16), sb("zlo", [P, KC, TT], BF16)
        x2, xn2, tr2, mix = (sb(n, [P, SUB * D]) for n in ("x2", "xn2", "tr2", "mix"))
        hs = xn2
        yf, yhi, ylo = sb("yf", [P, KC, TT]), sb("yhi", [P, KC, TT], BF16), sb("ylo", [P, KC, TT], BF16)
        u, sq = sb("u", [P, 2, TT]), sb("sq", [P, 2, TT])
        khi, klo = sb("khi", [P, HC0, TT], BF16), sb("klo", [P, HC0, TT], BF16)
        lg, ex, sel, wsel = (sb(n, [P, SUB, E0]) for n in ("lg", "ex", "sel", "wsel"))
        m8, rsum = sb("m8", [P, SUB, 8]), sb("rsum", [P, 2, SUB])
        wT = u[:, 0, :]
        xmf = yf

        emb_in = count("emb_in", 16 * SUB)
        emb_used = count("emb_used", 1)
        f_var, f_rstd = count("f_var", 2), count("f_rstd", 2)
        b_var, b_rstd = count("b_var", 2), count("b_rstd", 2)
        f_pool, b_pool = count("f_pool", 2), count("b_pool", 2)
        xn_ready, xnT = count("xn_ready", 1), count("xnT", KC)
        x_hi, x_lo = count("x_hi", KC), count("x_lo", KC)
        w_ps, k_ps, v_ps, r_ps = (count(n, KC) for n in ("w_ps", "k_ps", "v_ps", "r_ps"))
        ew_ready, kw_ready, ek_ready, ev_ready = (count(n, KC) for n in ("ew_ready", "kw_ready", "ek_ready", "ev_ready"))
        tr_ready, z_ready, z_hi, z_lo = (count(n, KC) for n in ("tr_ready", "z_ready", "z_hi", "z_lo"))
        o_ps, xn2_ready, xn2T = count("o_ps", 2), count("xn2_ready", 1), count("xn2T", KC)
        x2_ready = count("x2_ready", 2)
        y_hi, y_lo = count("y_hi", KC), count("y_lo", KC)
        rec_ps, tr2_ready = count("rec_ps", 2), count("tr2_ready", 2)
        up_ps, u_ready, sq_ready, k_hi, k_lo = (count(n, HC0) for n in ("up_ps", "u_ready", "sq_ready", "k_hi", "k_lo"))
        val_ps, val_used = count("val_ps", 1), count("val_used", 2)
        xm_ready, xmT, xm_f = count("xm_ready", 1), count("xmT", KC), count("xm_f", KC)
        lg_ps, lg_used, lg_shift, lg_exp = (count(n, 1) for n in ("lg_ps", "lg_used", "lg_shift", "lg_exp"))
        w_ready, wT_ps, wT_ready = (count(n, 1) for n in ("w_ready", "wT_ps", "wT_ready"))
        b2_ps, h_ready = count("b2_ps", 2), count("h_ready", 2)
        f_steps, b_steps = count("f_steps", KF), count("b_steps", KB)

        W = {n: (o, w) for n, (o, w) in OFF_A.items()}

        def wslice(part, name, kc, lo, n):
            o, w = W[name]
            return part[:, o + kc * w + lo:o + kc * w + lo + n]

        def braid(front, back):
            order = "b0 f0 b1 f1 b2 f2 b3 f3 b4 f4 b5 f5 b6 b7".split()
            for o in order:
                part = (front if o[0] == "f" else back)
                if part and int(o[1]) in part:
                    part[int(o[1])]()

        def run(eng, front, back):
            braid(front(0), None)
            with eng.Fori(0, TILES - 1) as t:
                braid(front(t + 1), back(t))
            braid(None, back(TILES - 1))

        block = x.enter_context(nc.Block())

        @block.gpsimd
        def _(pool):
            def rstd(mv, rs, var, ready, own, t, n):
                pool.wait_ge(var.sem, var.at(t, n + 1))
                pool.tensor_tensor(rs[:, 0, :], mv[:, :, 1], c.eps[:, 0:SUB], ALU.add).then_inc(own.sem, 1)
                pool.wait_ge(own.sem, own.at(t, n + 1))
                pool.tensor_tensor(rs[:, 1, :], rs[:, 0, :], c.eps[:, 4:4 + SUB], ALU.pow).then_inc(ready.sem, 1)

            def gather(t):
                for s in range(SUB):
                    pool.indirect_dma_start(emb[:, s * D:(s + 1) * D], None, c.i["emb"],
                                            bass.IndirectOffsetOnAxis(ap=c.idx[:, s:s + 1].bitcast(U32), axis=0)
                                            ).then_inc(emb_in.sem, 16)

            def front(t):
                def f0():
                    if isinstance(t, int):
                        pool.tensor_copy(c.idx[:, :], c.tok[:, 0:SUB]).then_inc(c.idx_ready, 1)
                        pool.wait_ge(c.idx_ready, 1)
                    else:
                        pool.wait_ge(emb_used.sem, emb_used.at(t, 0))
                        pool.tensor_tensor(c.idx[:, :], c.tok[:, bass.ds(t * SUB, SUB)],
                                           c.zero_i[:, :], ALU.add).then_inc(c.idx_ready, 1)
                        pool.wait_ge(c.idx_ready, t + 1)
                        pool.tensor_tensor(c.zero_j[:, :], c.zero_i[:, 0:1], c.zero_i[:, 0:1], ALU.add)
                    gather(t)
                    rstd(fmv, frs, f_var, f_rstd, f_pool, t, 0)
                    rstd(fmv, frs, f_var, f_rstd, f_pool, t, 1)

                def f1():
                    for k in range(KC):
                        pool.wait_ge(x_hi.sem, x_hi.at(t, k + 1))
                        pool.tensor_tensor(xlo[:, k, :], xf[:, k, :], xhi[:, k, :], ALU.subtract).then_inc(x_lo.sem, 1)

                def fz(k):
                    def f():
                        pool.wait_ge(z_hi.sem, z_hi.at(t, k + 1))
                        pool.tensor_tensor(zlo[:, k, :], z[:, k, :], zhi[:, k, :], ALU.subtract).then_inc(z_lo.sem, 1)
                    return f
                return {0: f0, 1: f1, 4: fz(0), 5: fz(1)}

            def back(t):
                def b0():
                    rstd(bmv, brs, b_var, b_rstd, b_pool, t, 0)

                def b1():
                    for k in range(KC):
                        pool.wait_ge(y_hi.sem, y_hi.at(t, k + 1))
                        pool.tensor_tensor(ylo[:, k, :], yf[:, k, :], yhi[:, k, :], ALU.subtract).then_inc(y_lo.sem, 1)

                def low(*ks):
                    def f():
                        for k in ks:
                            pool.wait_ge(sq_ready.sem, sq_ready.at(t, k + 1))
                            pool.wait_ge(k_hi.sem, k_hi.at(t, k + 1))
                            pool.tensor_tensor(klo[:, k, :], sq[:, k % 2, :], khi[:, k, :],
                                               ALU.subtract).then_inc(k_lo.sem, 1)
                    return f

                def b6():
                    rstd(bmv, brs, b_var, b_rstd, b_pool, t, 1)
                return {0: b0, 1: b1, 2: low(0, 1), 3: low(2, 3), 4: low(4, 5), 5: low(6, 7), 6: b6}
            run(pool, front, back)

        @block.scalar
        def _(act):
            def affine(src, f, hi, g, b, psum_ready, ready, low_done, t):
                for k in range(KC):
                    act.wait_ge(psum_ready.sem, psum_ready.at(t, k + 1))
                    act.wait_ge(low_done.sem, low_done.at(t, 0))
                    act.activation(f[:, k, :], src[k][:, :], ACT.Identity, bias=c.vec[:, b + k:b + k + 1],
                                   scale=c.vec[:, g + k:g + k + 1])
                    act.activation(hi[:, k, :], src[k][:, :], ACT.Identity, bias=c.vec[:, b + k:b + k + 1],
                                   scale=c.vec[:, g + k:g + k + 1]).then_inc(ready.sem, 1)

            def front(t):
                def f1():
                    affine(fb, xf, xhi, VEC["ln1_g"], VEC["ln1_b"], xnT, x_hi, x_lo, t)

                def exps(k):
                    def f():
                        act.wait_ge(w_ps.sem, w_ps.at(t, k + 1))
                        act.activation(ew[:, k, :], (fb[2], fb[1])[k][:, :], ACT.Exp).then_inc(ew_ready.sem, 1)
                        act.wait_ge(kw_ready.sem, kw_ready.at(t, k + 1))
                        act.activation(ek[:, k, :], kw[:, k, :], ACT.Exp).then_inc(ek_ready.sem, 1)
                    return f

                def fz(k):
                    def f():
                        if k == 0:
                            for j in range(KC):
                                act.wait_ge(r_ps.sem, r_ps.at(t, j + 1))
                                act.activation(tr[:, j, :], fb[j][:, :], ACT.Tanh, scale=0.5).then_inc(tr_ready.sem, 1)
                        act.wait_ge(z_ready.sem, z_ready.at(t, k + 1))
                        act.activation(zhi[:, k, :], z[:, k, :], ACT.Copy).then_inc(z_hi.sem, 1)
                    return f
                return {1: f1, 2: exps(0), 3: exps(1), 4: fz(0), 5: fz(1)}

            def back(t):
                def b1():
                    affine(bb[2:4], yf, yhi, VEC["ln2_g"], VEC["ln2_b"], xn2T, y_hi, y_lo, t)

                def relus(*ks):
                    def f():
                        if ks[0] == 0:
                            for j in range(2):
                                act.wait_ge(rec_ps.sem, rec_ps.at(t, j + 1))
                                act.activation(tr2[:, j * TT:(j + 1) * TT], bb[j][:, :], ACT.Tanh,
                                               scale=0.5).then_inc(tr2_ready.sem, 1)
                        for k in ks:
                            act.wait_ge(up_ps.sem, up_ps.at(t, k + 1))
                            act.wait_ge(sq_ready.sem, sq_ready.at(t, max(k - 1, 0)))
                            act.activation(u[:, k % 2, :], bb[2 + k % 2][:, :], ACT.Relu).then_inc(u_ready.sem, 1)
                            act.wait_ge(u_ready.sem, u_ready.at(t, k + 1))
                            act.activation(khi[:, k, :], u[:, k % 2, :], ACT.Square).then_inc(k_hi.sem, 1)
                    return f

                def b7():
                    for k in range(KC):
                        act.wait_ge(xmT.sem, xmT.at(t, k + 1))
                        act.activation(xmf[:, k, :], bb[2 + k][:, :], ACT.Copy)
                        act.activation(c.xT_hi[:, bass.ds(t * TT + k * N, TT)], bb[2 + k][:, :],
                                       ACT.Copy).then_inc(xm_f.sem, 1)
                    act.wait_ge(lg_shift.sem, lg_shift.at(t))
                    act.activation(ex[:, :, :], lg[:, :, :], ACT.Exp).then_inc(lg_exp.sem, 1)
                    act.wait_ge(wT_ps.sem, wT_ps.at(t))
                    act.activation(wT[0:E0, :], bb[1][0:E0, :], ACT.Copy).then_inc(wT_ready.sem, 1)
                return {1: b1, 2: relus(0, 1), 3: relus(2, 3), 4: relus(4, 5), 5: relus(6, 7), 7: b7}
            run(act, front, back)

        @block.vector
        def _(dve):
            F, B = Steps(dve, f_steps), Steps(dve, b_steps)

            def norm(S, src, dst, st, mv, rs, var, rstd, t, n, ready=None):
                S.settle()
                for s in range(SUB):
                    S.done(dve.bn_stats(st[:, s, :], src[:, s * D:(s + 1) * D]))
                S.settle()
                S.done(dve.tensor_copy(c.scr[:, 0:1], c.scr[:, 1:2]))
                for s in range(SUB):
                    i = dve.bn_aggr(mv[:, s, :], st[:, s, :])
                i.then_inc(var.sem, 1)
                dve.wait_ge(rstd.sem, rstd.at(t, n + 1))
                for s in range(SUB):
                    i = dve.tensor_scalar(dst[:, s * D:(s + 1) * D], src[:, s * D:(s + 1) * D], mv[:, s, 0:1],
                                          rs[:, 1, s:s + 1], ALU.subtract, ALU.mult)
                    if ready is None or s < SUB - 1:
                        S.done(i)
                if ready is not None:
                    i.then_inc(ready.sem, 1)

            def front(t):
                def f0():
                    F.begin(t)
                    dve.wait_ge(emb_in.sem, emb_in.at(t))
                    F.done(dve.tensor_scalar(h0[:, :], emb[:, :], EMB_SCALE, None, ALU.mult))
                    dve.tensor_scalar(c.h[:, bass.ds(t * SUB * D, SUB * D)], emb[:, :], EMB_SCALE, None,
                                      ALU.mult).then_inc(emb_used.sem, 1)
                    norm(F, h0, x1, fst, fmv, frs, f_var, f_rstd, t, 0)
                    norm(F, x1, xn, fst, fmv, frs, f_var, f_rstd, t, 1, xn_ready)

                def recur(k):
                    def f():
                        dve.wait_ge(ew_ready.sem, ew_ready.at(t, k + 1))
                        dve.wait_ge(k_ps.sem, k_ps.at(t, k + 1))
                        dve.tensor_tensor(kw[:, k, :], (fb[3], fb[2])[k][:, :], ew[:, k, :],
                                          ALU.subtract).then_inc(kw_ready.sem, 1)
                        dve.wait_ge(ek_ready.sem, ek_ready.at(t, k + 1))
                        dve.wait_ge(v_ps.sem, v_ps.at(t, k + 1))
                        dve.tensor_tensor(ev[:, k, :], (fb[0], fb[3])[k][:, :], ek[:, k, :],
                                          ALU.mult).then_inc(ev_ready.sem, 1)
                        decay = c.dec[:, k:k + 1].to_broadcast([P, SEQ])
                        for b in range(SEQS):
                            q = slice(b * SEQ, (b + 1) * SEQ)
                            F.done(dve.tensor_tensor_scan(den[:, k, q], decay, ek[:, k, q], 0.0, ALU.mult, ALU.add))
                        dve.wait_ge(ev_ready.sem, ev_ready.at(t, k + 1))
                        for b in range(SEQS):
                            q = slice(b * SEQ, (b + 1) * SEQ)
                            F.done(dve.tensor_tensor_scan(num[:, k, q], decay, ev[:, k, q], 0.0, ALU.mult, ALU.add))
                        F.settle()
                        F.done(dve.tensor_scalar(ew[:, k, :], den[:, k, :], 2.0, 2 * WKV_EPS, ALU.mult, ALU.add))
                    return f

                def fz(k):
                    def f():
                        F.settle()
                        F.done(dve.reciprocal(den[:, k, :], ew[:, k, :]))
                        F.settle()
                        F.done(dve.tensor_tensor(kw[:, k, :], num[:, k, :], den[:, k, :], ALU.mult))
                        F.settle()
                        dve.wait_ge(tr_ready.sem, tr_ready.at(t, k + 1))
                        dve.scalar_tensor_tensor(z[:, k, :], tr[:, k, :], 1.0, kw[:, k, :], ALU.add,
                                                 ALU.mult).then_inc(z_ready.sem, 1)
                        if k == KC - 1:
                            F.end()
                    return f
                return {0: f0, 2: recur(0), 3: recur(1), 4: fz(0), 5: fz(1)}

            def back(t):
                def b0():
                    B.begin(t)
                    for j in range(2):
                        q = slice(j * TT, (j + 1) * TT)
                        dve.wait_ge(o_ps.sem, o_ps.at(t, j + 1))
                        dve.tensor_tensor(x2[:, q], x1[:, q], bb[j][:, :], ALU.add).then_inc(x2_ready.sem, 1)
                    dve.wait_ge(x2_ready.sem, x2_ready.at(t))
                    norm(B, x2, xn2, bst, bmv, brs, b_var, b_rstd, t, 0, xn2_ready)

                def squares(*ks):
                    def f():
                        for k in ks:
                            dve.wait_ge(u_ready.sem, u_ready.at(t, k + 1))
                            dve.wait_ge(k_lo.sem, k_lo.at(t, max(k - 1, 0)))
                            dve.tensor_tensor(sq[:, k % 2, :], u[:, k % 2, :], u[:, k % 2, :],
                                              ALU.mult).then_inc(sq_ready.sem, 1)
                    return f

                def b6():
                    dve.wait_ge(tr2_ready.sem, tr2_ready.at(t))
                    dve.wait_ge(val_ps.sem, val_ps.at(t))
                    for j in range(2):
                        q = slice(j * TT, (j + 1) * TT)
                        dve.scalar_tensor_tensor(mix[:, q], tr2[:, q], 1.0, bb[j][:, :], ALU.add,
                                                 ALU.mult).then_inc(val_used.sem, 1)
                    dve.wait_ge(val_used.sem, val_used.at(t))
                    B.done(dve.scalar_tensor_tensor(hs[:, :], mix[:, :], 0.5, x2[:, :], ALU.mult, ALU.add))
                    B.settle()
                    B.done(dve.tensor_tensor(hs[:, :], hs[:, :], c.h[:, bass.ds(t * SUB * D, SUB * D)], ALU.add))
                    norm(B, hs, mix, bst, bmv, brs, b_var, b_rstd, t, 1, xm_ready)

                def b7():
                    for k in range(KC):
                        at = bass.ds(t * TT + k * N, TT)
                        dve.wait_ge(xm_f.sem, xm_f.at(t, k + 1))
                        B.done(dve.tensor_tensor(c.xT_lo[:, at], xmf[:, k, :], c.xT_hi[:, at], ALU.subtract))
                    dve.wait_ge(lg_ps.sem, lg_ps.at(t))
                    dve.tensor_copy(lg[:, :, :], bb[0][:, 0:SUB * E0].rearrange("p (s e) -> p s e", s=SUB)
                                    ).then_inc(lg_used.sem, 1)
                    dve.wait_ge(lg_used.sem, lg_used.at(t))
                    B.done(dve.tensor_copy(c.scr[:, 0:1], c.scr[:, 1:2]))
                    for s in range(SUB):
                        B.done(dve.max(m8[:, s, :], lg[:, s, :]))
                    B.settle()
                    B.done(dve.tensor_tensor(sel[:, :, :], lg[:, :, :], m8[:, :, 1:2].to_broadcast([P, SUB, E0]),
                                             ALU.is_ge))
                    B.settle()
                    dve.tensor_tensor(lg[:, :, :], lg[:, :, :], m8[:, :, 0:1].to_broadcast([P, SUB, E0]),
                                      ALU.subtract).then_inc(lg_shift.sem, 1)
                    dve.wait_ge(lg_exp.sem, lg_exp.at(t))
                    B.done(dve.tensor_tensor(sel[:, :, :], ex[:, :, :], sel[:, :, :], ALU.mult))
                    B.settle()
                    B.done(dve.tensor_reduce(rsum[:, 0, :], sel[:, :, :], AX.X, ALU.add))
                    B.settle()
                    B.done(dve.reciprocal(rsum[:, 1, :], rsum[:, 0, :]))
                    B.settle()
                    weights = rsum[:, 1, :].unsqueeze(2).to_broadcast([P, SUB, E0])
                    dve.tensor_tensor(wsel[:, :, :], sel[:, :, :], weights, ALU.mult).then_inc(w_ready.sem, 1)
                    dve.wait_ge(w_ready.sem, w_ready.at(t))
                    B.done(dve.tensor_copy(c.w0[:, bass.ds(t * SUB * E0, SUB * E0)],
                                           wsel[:, :, :].rearrange("p s e -> p (s e)")))
                    for j in range(2):
                        dve.wait_ge(b2_ps.sem, b2_ps.at(t, j + 1))
                        dve.tensor_tensor(c.h[:, bass.ds(t * SUB * D + j * TT, TT)], hs[:, j * TT:(j + 1) * TT],
                                          bb[2 + j][:, :], ALU.add).then_inc(h_ready.sem, 1)
                    B.end()
                return {0: b0, 2: squares(0, 1), 3: squares(2, 3), 4: squares(4, 5), 5: squares(6, 7), 6: b6, 7: b7}
            run(dve, front, back)

        @block.tensor
        def _(pe):
            def feature_major(out, name, e, hi, lo, ready, lo_sem, lo_at):
                cols = e * P
                for j, (wp, xp) in enumerate(((c.WA_hi, hi), (c.WA_lo, hi), (c.WA_hi, lo))):
                    if j == 2 and lo_sem is not None:
                        pe.wait_ge(lo_sem, lo_at)
                    for k in range(KC):
                        m = pe.matmul(out[:, :], wslice(wp, name, k, cols, P), xp[:, k, :],
                                      start=(j == 0 and k == 0), stop=(j == 2 and k == KC - 1))
                m.then_inc(ready.sem, 1)

            def token_major(out, name, s, hi, lo):
                for j, (wp, xp) in enumerate(((c.WA_hi, hi), (c.WA_lo, hi), (c.WA_hi, lo))):
                    for k in range(KC):
                        m = pe.matmul(out, xp[:, k, s * P:(s + 1) * P], wslice(wp, name, k, 0, D),
                                      start=(j == 0 and k == 0), stop=(j == 2 and k == KC - 1))
                return m

            def transposes(src, banks, ready):
                for k in range(KC):
                    for s in range(SUB):
                        m = pe.transpose(banks[k][:, s * P:(s + 1) * P], src[:, s * D + k * P:s * D + (k + 1) * P],
                                         c.ident[:, :])
                    m.then_inc(ready.sem, 1)

            def front(t):
                def f1():
                    pe.wait_ge(xn_ready.sem, xn_ready.at(t))
                    pe.wait_ge(tr_ready.sem, tr_ready.at(t, 0))
                    transposes(xn, fb, xnT)

                def f2():
                    pe.wait_ge(x_hi.sem, x_hi.at(t))
                    pe.wait_ge(kw_ready.sem, kw_ready.at(t, 0))
                    feature_major(fb[2], "Ww", 0, xhi, xlo, w_ps, x_lo.sem, x_lo.at(t))
                    pe.wait_ge(ev_ready.sem, ev_ready.at(t, 0))
                    feature_major(fb[3], "Wk", 0, xhi, xlo, k_ps, None, None)
                    feature_major(fb[0], "Wv", 0, xhi, xlo, v_ps, None, None)

                def f3():
                    feature_major(fb[1], "Ww", 1, xhi, xlo, w_ps, None, None)
                    pe.wait_ge(ew_ready.sem, ew_ready.at(t, 1))
                    feature_major(fb[2], "Wk", 1, xhi, xlo, k_ps, None, None)
                    pe.wait_ge(kw_ready.sem, kw_ready.at(t, 1))
                    feature_major(fb[3], "Wv", 1, xhi, xlo, v_ps, None, None)

                def f4():
                    pe.wait_ge(ev_ready.sem, ev_ready.at(t, 1))
                    feature_major(fb[0], "Wr", 0, xhi, xlo, r_ps, None, None)
                    pe.wait_ge(ew_ready.sem, ew_ready.at(t, 2))
                    feature_major(fb[1], "Wr", 1, xhi, xlo, r_ps, None, None)
                return {1: f1, 2: f2, 3: f3, 4: f4}

            def back(t):
                def b0():
                    pe.wait_ge(z_lo.sem, z_lo.at(t))
                    pe.wait_ge(z_hi.sem, z_hi.at(t))
                    pe.wait_ge(lg_used.sem, lg_used.at(t, 0))
                    pe.wait_ge(wT_ready.sem, wT_ready.at(t, 0))
                    for s in range(SUB):
                        m = token_major(bb[s // 2][:, (s % 2) * D:(s % 2 + 1) * D], "Wo", s, zhi, zlo)
                        if s % 2:
                            m.then_inc(o_ps.sem, 1)

                def b1():
                    pe.wait_ge(xn2_ready.sem, xn2_ready.at(t))
                    pe.wait_ge(h_ready.sem, h_ready.at(t, 0))
                    transposes(xn2, bb[2:4], xn2T)

                def up(k):
                    if k >= 2:
                        pe.wait_ge(u_ready.sem, u_ready.at(t, k - 1))
                    feature_major(bb[2 + k % 2], "Wkey", k, yhi, ylo, up_ps, None, None)

                def down(k):
                    if k == 0:
                        pe.wait_ge(tr2_ready.sem, tr2_ready.at(t))
                    pe.wait_ge(k_hi.sem, k_hi.at(t, k + 1))
                    pe.wait_ge(k_lo.sem, k_lo.at(t, k + 1))
                    o, w = W["Wval"]
                    for s in range(SUB):
                        for j, (wp, xp) in enumerate(((c.WA_hi, khi), (c.WA_lo, khi), (c.WA_hi, klo))):
                            m = pe.matmul(bb[s // 2][:, (s % 2) * D:(s % 2 + 1) * D], xp[:, k, s * P:(s + 1) * P],
                                          wp[:, o + k * w:o + (k + 1) * w],
                                          start=(k == 0 and j == 0 and s % 2 == 0), stop=(k == HC0 - 1 and j == 2),
                                          skip_group_check=True)
                    if k == HC0 - 1:
                        m.then_inc(val_ps.sem, 1)

                def b2():
                    pe.wait_ge(y_hi.sem, y_hi.at(t))
                    pe.wait_ge(y_lo.sem, y_lo.at(t))
                    pe.wait_ge(x2_ready.sem, x2_ready.at(t))
                    for s in range(SUB):
                        m = token_major(bb[s // 2][:, (s % 2) * D:(s % 2 + 1) * D], "Wrec", s, yhi, ylo)
                        if s % 2:
                            m.then_inc(rec_ps.sem, 1)
                    up(0)
                    up(1)

                def pairs(k):
                    def f():
                        down(k)
                        up(k + 2)
                        down(k + 1)
                        up(k + 3)
                    return f

                def b6():
                    down(6)
                    down(7)

                def b7():
                    pe.wait_ge(xm_ready.sem, xm_ready.at(t))
                    pe.wait_ge(u_ready.sem, u_ready.at(t))
                    transposes(mix, bb[2:4], xmT)
                    pe.wait_ge(xm_f.sem, xm_f.at(t))
                    for s in range(SUB):
                        out = bb[0][:, s * E0:(s + 1) * E0]
                        for k in range(KC):
                            pe.matmul(out, xmf[:, k, s * P:(s + 1) * P], c.Wrt[:, k * E0:(k + 1) * E0],
                                      start=(k == 0), stop=False)
                        m = pe.matmul(out, c.ones[0:1, :], c.br[0:1, :], start=False, stop=True)
                    m.then_inc(lg_ps.sem, 1)
                    pe.wait_ge(w_ready.sem, w_ready.at(t))
                    for s in range(SUB):
                        m = pe.transpose(bb[1][0:E0, s * P:(s + 1) * P], wsel[:, s, :], c.ident[:, :])
                    m.then_inc(wT_ps.sem, 1)
                    pe.wait_ge(wT_ready.sem, wT_ready.at(t))
                    for s in range(SUB):
                        m = pe.matmul(bb[2 + s // 2][:, (s % 2) * D:(s % 2 + 1) * D], wT[0:E0, s * P:(s + 1) * P],
                                      c.b2[0:E0, :], start=True, stop=True)
                        if s % 2:
                            m.then_inc(b2_ps.sem, 1)
                return {0: b0, 1: b1, 2: b2, 3: pairs(0), 4: pairs(2), 5: pairs(4), 6: b6, 7: b7}
            run(pe, front, back)


def phase_b(nc, c):
    with ExitStack() as x:
        def sb(name, shape, dt=F32):
            return x.enter_context(nc.sbuf_tensor("b_" + name, shape, dt))

        def count(name, per):
            return Count(x.enter_context(nc.semaphore("b_" + name)), per)

        ub = [x.enter_context(nc.psum_tensor(f"b_up{k}", [P, TT], F32)) for k in range(4)]
        ob = [x.enter_context(nc.psum_tensor(f"b_down{k}", [P, TT], F32)) for k in range(2)]
        W_hi, W_lo = ([sb(f"{n}{p}", [P, COLS_E], BF16) for p in range(2)] for n in ("W_hi", "W_lo"))
        stage = [sb(f"stage{j}", [P, PIECE_E + PIECE_C]) for j in range(2)]
        b1 = [sb(f"b1_{p}", [P, HC0]) for p in range(2)]
        f = sb("f", [P, 4, TT])
        ghi, glo = sb("ghi", [P, HC0, TT], BF16), sb("glo", [P, HC0, TT], BF16)

        up_ps, g_hi, g_lo = count("up_ps", HC0), count("g_hi", HC0), count("g_lo", HC0)
        out_ps, out_used = count("out_ps", 1), count("out_used", SUB)
        landed = [count(f"landed{j}", 16) for j in range(2)]
        w_hi, w_lo = count("w_hi", 1), count("w_lo", 1)
        b1_ready = count("b1_ready", 1)

        def run(eng, step, begin=None, last_begin=None):
            def expert(e, par, more):
                if begin:
                    begin(e, par)
                with eng.Fori(0, TILES // 2) as tp:
                    for j in range(2):
                        step(e, par, tp, j, more)
            with eng.Fori(0, E0 // 2 - 1) as pair:
                expert(pair * 2, 0, True)
                expert(pair * 2 + 1, 1, True)
            expert(E0 - 2, 0, True)
            expert(E0 - 1, 1, False)

        def split_at(piece):
            return piece * PIECE_E, piece * PIECE_C

        block = x.enter_context(nc.Block())

        @block.sync
        def _(sp):
            for p in range(TILES):
                if p >= 2:
                    sp.wait_ge(w_lo.sem, p - 1)
                sp.dma_start(stage[p % 2][:, :], c.i["WP"][p, :, :]).then_inc(landed[p % 2].sem, 16)

            def step(e, par, tp, j, more):
                if more:
                    g = e * TILES + tp * 2 + (TILES + j)
                    sp.wait_ge(w_lo.sem, g - 1)
                    sp.dma_start(stage[j][:, :], c.i["WP"][bass.ds(g, 1), :, :].rearrange("g p n -> (g p) n")
                                 ).then_inc(landed[j].sem, 16)
            run(sp, step)

        @block.scalar
        def _(act):
            def high(buf, j, piece, piece_c):
                act.activation(c.WC_hi[:, bass.ds(piece_c * PIECE_C, PIECE_C)], stage[j][:, PIECE_E:], ACT.Copy)
                act.activation(buf[:, bass.ds(piece * PIECE_E, PIECE_E)], stage[j][:, 0:PIECE_E],
                               ACT.Copy).then_inc(w_hi.sem, 1)
            for p in range(TILES):
                act.wait_ge(landed[p % 2].sem, 16 * (p // 2 + 1))
                high(W_hi[0], p % 2, p, p)

            def step(e, par, tp, j, more):
                g = e * TILES + tp * 2 + j
                for k in range(HC0):
                    act.wait_ge(up_ps.sem, up_ps.at(g, k + 1))
                    if k == 0 and j == 0:
                        act.wait_ge(b1_ready.sem, e + 1)
                    act.wait_ge(g_lo.sem, g_lo.at(g, max(k - 3, 0)))
                    if k == HC0 - 1 and more:
                        act.wait_ge(landed[j].sem, (e * (TILES // 2) + tp + (TILES // 2 + 1)) * 16)
                    act.activation(f[:, k % 4, :], ub[k % 4][:, :], ACT.Gelu, bias=b1[par][:, k:k + 1])
                    act.activation(ghi[:, k, :], ub[k % 4][:, :], ACT.Gelu,
                                   bias=b1[par][:, k:k + 1]).then_inc(g_hi.sem, 1)
                if more:
                    high(W_hi[1 - par], j, tp * 2 + j, g + TILES)
            run(act, step)

        @block.vector
        def _(dve):
            def low(hi, lo, j, piece, piece_c):
                q = bass.ds(piece_c * PIECE_C, PIECE_C)
                dve.tensor_tensor(c.WC_lo[:, q], stage[j][:, PIECE_E:], c.WC_hi[:, q], ALU.subtract)
                q = bass.ds(piece * PIECE_E, PIECE_E)
                dve.tensor_tensor(lo[:, q], stage[j][:, 0:PIECE_E], hi[:, q], ALU.subtract).then_inc(w_lo.sem, 1)
            for p in range(TILES):
                dve.wait_ge(w_hi.sem, p + 1)
                low(W_hi[0], W_lo[0], p % 2, p, p)

            def begin(e, par):
                dve.tensor_copy(b1[par][:, :], c.b1[:, bass.ds(e * HC0, HC0)]).then_inc(b1_ready.sem, 1)

            def step(e, par, tp, j, more):
                g = e * TILES + tp * 2 + j
                t = tp * 2 + j
                for k in range(HC0):
                    dve.wait_ge(g_hi.sem, g_hi.at(g, k + 1))
                    dve.tensor_tensor(glo[:, k, :], f[:, k % 4, :], ghi[:, k, :], ALU.subtract).then_inc(g_lo.sem, 1)
                if more:
                    dve.wait_ge(w_hi.sem, g + (TILES + 1))
                    low(W_hi[1 - par], W_lo[1 - par], j, tp * 2 + j, g + TILES)
                dve.wait_ge(out_ps.sem, out_ps.at(g))
                dve.wait_ge(out_used.sem, out_used.at(g, 0))
                for s in range(SUB):
                    at = bass.ds((t * SUB + s) * D, D)
                    dve.scalar_tensor_tensor(c.h[:, at], ob[s // 2][:, (s % 2) * D:(s % 2 + 1) * D],
                                             c.w0[:, bass.ds((t * SUB + s) * E0 + e, 1)], c.h[:, at],
                                             ALU.mult, ALU.add).then_inc(out_used.sem, 1)
            run(dve, step, begin)

        @block.tensor
        def _(pe):
            def step(e, par, tp, j, more):
                g = e * TILES + tp * 2 + j
                t = tp * 2 + j

                def up(k):
                    for n, (wp, xp) in enumerate(((W_hi, c.xT_hi), (W_lo, c.xT_hi), (W_hi, c.xT_lo))):
                        for q in range(KC):
                            m = pe.matmul(ub[k % 4][:, :], wp[par][:, q * H0 + k * P:q * H0 + (k + 1) * P],
                                          xp[:, bass.ds(t * TT + q * N, TT)], start=(n == 0 and q == 0),
                                          stop=(n == 2 and q == KC - 1))
                    m.then_inc(up_ps.sem, 1)

                def down(k):
                    pe.wait_ge(g_hi.sem, g_hi.at(g, k + 1))
                    pe.wait_ge(g_lo.sem, g_lo.at(g, k + 1))
                    if k == 0:
                        pe.wait_ge(out_used.sem, out_used.at(g, 0))
                    w = slice(KC * H0 + k * D, KC * H0 + (k + 1) * D)
                    for s in range(SUB):
                        for n, (wp, xp) in enumerate(((W_hi, ghi), (W_lo, ghi), (W_hi, glo))):
                            m = pe.matmul(ob[s // 2][:, (s % 2) * D:(s % 2 + 1) * D], xp[:, k, s * P:(s + 1) * P],
                                          wp[par][:, w], start=(k == 0 and n == 0 and s % 2 == 0),
                                          stop=(k == HC0 - 1 and n == 2), skip_group_check=True)
                    if k == HC0 - 1:
                        m.then_inc(out_ps.sem, 1)
                pe.wait_ge(w_lo.sem, (e + 1) * TILES)
                up(0)
                up(1)
                for k in range(2, HC0):
                    up(k)
                    down(k - 2)
                down(HC0 - 2)
                down(HC0 - 1)
            run(pe, step)


def phase_c(nc, c, out):
    KF, KB = 90, 28
    VW = HD + 1
    with ExitStack() as x:
        def sb(name, shape, dt=F32):
            return x.enter_context(nc.sbuf_tensor("c_" + name, shape, dt))

        def count(name, per):
            return Count(x.enter_context(nc.semaphore("c_" + name)), per)

        fb = [x.enter_context(nc.psum_tensor(f"c_front{k}", [P, TT], F32)) for k in range(4)]
        bb = [x.enter_context(nc.psum_tensor(f"c_back{k}", [P, TT], F32)) for k in range(4)]

        room = [c.xT_hi[:, :].bitcast(F32), c.xT_lo[:, :].bitcast(F32)]
        at = [0, 0]

        def reuse(n, which):
            at[which] += n
            assert at[which] <= KC * N // 2
            return room[which][:, at[which] - n:at[which]]

        h2 = sb("h2", [P, SUB * D])
        xn = sb("xn", [P, SUB * D])
        fst, fmv, frs = sb("fst", [P, SUB, 6]), sb("fmv", [P, SUB, 2]), sb("frs", [P, 5, SUB])
        bst, bmv, brs = sb("bst", [P, SUB, 6]), sb("bmv", [P, SUB, 2]), sb("brs", [P, 2, SUB])
        xf = reuse(KC * TT, 0).rearrange("p (k n) -> p k n", k=KC)
        xhi, xlo = sb("xhi", [P, KC, TT], BF16), sb("xlo", [P, KC, TT], BF16)
        kk, vv, tr = (reuse(KC * TT, 0).rearrange("p (k n) -> p k n", k=KC) for _ in range(3))
        T = reuse(5 * TT, 1).rearrange("p (k n) -> p k n", k=5)
        z = reuse(TT, 1)
        pp, av, bv = (sb(n, [P, SEQS, SEQ + 1]) for n in ("pp", "av", "bv"))
        qkr, qsq = reuse(TT, 1), reuse(TT, 1)
        T_ = T.rearrange("p k n -> p (k n)")
        used = [0]

        def in_T(n, dt=F32):
            o = used[0]
            used[0] += n // 2 if dt is BF16 else n
            assert used[0] <= 5 * TT
            return T_[:, o:used[0]] if dt is F32 else T_[:, o:used[0]].bitcast(BF16)
        vf = in_T(D)
        ss, qrs = sb("ss", [P, 2 * HEADS]), sb("qrs", [P, 2, 2 * HEADS])
        qs, ks = sb("qs", [P, HEADS, 64], BF16), sb("ks", [P, HEADS, 64], BF16)
        qT, kT = (a.rearrange("p k n -> p (k n)").bitcast(BF16).rearrange("p (h n) -> p h n", h=HEADS // 2)
                  for a in (kk, vv))
        vh, vl = sb("vh", [P, 2, HEADS, VW], BF16), sb("vl", [P, 2, HEADS, HD], BF16)
        mx, mr = sb("mx", [P, 2, HEADS]), sb("mr", [P, 2, 2, HEADS])
        nstack, negT = sb("nstack", [P, 2, P], BF16), sb("negT", [P, SEQ], BF16)
        npart = nstack[:, :, 0:3 * HEADS].rearrange("p q (h a) -> p q h a", h=HEADS)
        pf = in_T(2 * 3 * P).rearrange("p (b n) -> p b n", b=2)
        ph, pl = (in_T(2 * 3 * P, BF16).rearrange("p (b n) -> p b n", b=2) for _ in range(2))
        ou = in_T(2 * HEADS * VW).rearrange("p (q h d) -> p q h d", q=2, h=HEADS)
        den = sb("den", [P, 2, HEADS])
        yn, yf = sb("yn", [P, SUB * D]), sb("yf", [P, KC, TT])
        yhi, ylo = sb("yhi", [P, KC, TT], BF16), sb("ylo", [P, KC, TT], BF16)
        hid_hi = [sb(f"hid_hi{n}", [P, HID // P, TT], BF16) for n in range(3)]
        hid_lo = [sb(f"hid_lo{n}", [P, HID // P, TT], BF16) for n in range(3)]
        g = sb("g", [P, 2, TT])
        sl, sl2 = sb("sl", [P, TT]), sb("sl2", [P, TT])
        lg, pr, wt = (sb(n, [P, SUB, E1]) for n in ("lg", "pr", "wt"))
        gt, eq = sb("gt", [P, SUB, E1, E1]), sb("eq", [P, SUB, E1, E1])
        r1 = sb("r1", [P, 4, SUB])
        below = sb("below", [P, E1, E1])

        f_var, f_rstd, f_pool = count("f_var", 2), count("f_rstd", 2), count("f_pool", 6)
        b_var, b_rstd, b_pool = count("b_var", 1), count("b_rstd", 1), count("b_pool", 3)
        xn_ready, xnT, x_hi, x_lo = count("xn_ready", 3), count("xnT", 3 * KC), count("x_hi", 3 * KC), count("x_lo", 3 * KC)
        k_ps, r_ps, kv_ready, tr_ready = (count(n, KC) for n in ("k_ps", "r_ps", "kv_ready", "tr_ready"))
        arg_ready, exp_ready, z_ready, z_hi, z_lo = (count(n, KC) for n in ("arg_ready", "exp_ready", "z_ready", "z_hi", "z_lo"))
        o_ps, h2_ready = count("o_ps", 2), count("h2_ready", 2)
        qk_ps, v_ps, qk_sq, v_hi, v_lo, ss_ready, q_rstd, q_pool, q_stack, k_stack = (
            count(n, SUB * m) for n, m in (("qk_ps", 1), ("v_ps", 1), ("qk_sq", 1), ("v_hi", 1), ("v_lo", 1),
                                           ("ss_ready", 1), ("q_rstd", 1), ("q_pool", 2), ("q_stack", 1), ("k_stack", 1)))
        qkT_ps, qkT_ready = count("qkT_ps", 2 * SUB), count("qkT_ready", 2 * SUB)
        S_ps, mx_ready = count("S_ps", 12 * SEQS), count("mx_ready", 12 * SEQS)
        np_ready, negT_ps, negT_ready = (count(n, SEQS) for n in ("np_ready", "negT_ps", "negT_ready"))
        P_ps, p_f, p_hi, p_lo, pv_ps = (count(n, HEADS * SEQS) for n in ("P_ps", "p_f", "p_hi", "p_lo", "pv_ps"))
        ou_ready = count("ou_ready", 2 * SEQS)
        ao_ps, h3_ready = count("ao_ps", 2), count("h3_ready", 1)
        yn_ready, ynT, y_hi, y_lo = count("yn_ready", 1), count("ynT", KC), count("y_hi", KC), count("y_lo", KC)
        lg_ps, lg_ready, lg_shift, lg_exp = (count(n, 1) for n in ("lg_ps", "lg_ready", "lg_shift", "lg_exp"))
        f_steps, b_steps = count("f_steps", KF), count("b_steps", KB)
        stored, set_up = count("stored", 16), count("set_up", 1)

        HC = HID // P
        UPS = {}
        for n, (name, src, ks_, dst, cs) in enumerate((
                ("e2_l1", None, KC, 0, HC), ("e0_up", None, KC, 2, HC), ("e2_l2", 0, HC, 1, HC),
                ("e2_l3", 1, HC, 0, HC), ("e3_down", None, KC, 2, KC), ("e3_up", 2, KC, 1, HC))):
            UPS[name] = (src, ks_, dst, cs)
        WORK = [("up", "e2_l1"), ("up", "e0_up"), ("up", "e2_l2"), ("down", "e0_down", 0, 2),
                ("up", "e2_l3"), ("up", "e3_down"), ("down", "e2_l4", 2, 0), ("up", "e3_up"),
                ("gated", None), ("down", "e3_out", 3, 1), ("down", "e1_down", 1, 0)]
        SEGMENT = {2: WORK[0:2], 3: WORK[2:3], 4: WORK[3:5], 5: WORK[5:7], 6: WORK[7:8], 7: WORK[8:9], 8: WORK[9:11]}
        first_up, first_hid, first_down, nu, nh, nd = {}, {}, {}, 0, 0, 0
        hid_of = {}
        for w in WORK:
            if w[0] == "up":
                first_up[w[1]], first_hid[w[1]] = nu, nh
                nu, nh = nu + UPS[w[1]][3], nh + UPS[w[1]][3]
            elif w[0] == "gated":
                first_up["e1"], first_hid["e1"] = nu, nh
                nu, nh = nu + 2 * HC, nh + HC
            else:
                first_down[w[1]] = nd
                nd += 1
        NU, NH, ND = nu, nh, nd
        assert NU % 2 == 0
        maker = {"e0_down": "e0_up", "e2_l4": "e2_l3", "e3_out": "e3_up", "e1_down": "e1",
                 "e2_l2": "e2_l1", "e2_l3": "e2_l2", "e3_up": "e3_down"}
        up_ps = count("up_ps", NU)
        gate_th, gate_sl = count("gate_th", HC), count("gate_sl", HC)
        hi_ready, lo_ready = count("hi_ready", NH), count("lo_ready", NH)
        down_ps, down_used = count("down_ps", ND), count("down_used", ND * SUB)

        ORDER = "b0 f0 b1 f1 f2 b2 f3 b3 f4 b4 f5 b5 f6 b6 f7 f8 b7 f9 f10 b8 f11 f12 f13".split()

        def braid(front, back):
            for o in ORDER:
                part = front if o[0] == "f" else back
                if part and int(o[1:]) in part:
                    part[int(o[1:])]()

        def run(eng, front, back):
            braid(front(0), None)
            with eng.Fori(0, TILES - 1) as t:
                braid(front(t + 1), back(t))
            braid(None, back(TILES - 1))

        def group(n):
            if n < 8:
                return [4 * (n // 2) + n % 2 + 2 * j for j in range(2)]
            return [8 * ((n - 8) // 2) + n % 2 + 2 * j for j in range(4)]

        def W(part, name, k, lo, n):
            o, w = OFF_C[name]
            return part[:, o + k * w + lo:o + k * w + lo + n]

        block = x.enter_context(nc.Block())

        @block.sync
        def _(sp):
            with sp.Fori(0, TILES) as t:
                sp.wait_ge(down_used.sem, down_used.at(t))
                sp.dma_start(out[bass.ds(t * TT, TT), :].rearrange("(s p) d -> p s d", p=P),
                             c.h[:, bass.ds(t * SUB * D, SUB * D)].rearrange("p (s d) -> p s d", s=SUB)
                             ).then_inc(stored.sem, 16)
            sp.wait_ge(stored.sem, 16 * TILES)

        @block.gpsimd
        def _(pool):
            def rstd(mv, rs, var, ready, own, t, n, m, centred):
                pool.wait_ge(var.sem, var.at(t, n + 1))
                v = mv[:, :, 1]
                if not centred:
                    pool.tensor_tensor(rs[:, 0, :], mv[:, :, 0], mv[:, :, 0], ALU.mult).then_inc(own.sem, 1)
                    pool.wait_ge(own.sem, own.at(t, m + 1))
                    pool.tensor_tensor(rs[:, 1, :], rs[:, 0, :], v, ALU.add).then_inc(own.sem, 1)
                    pool.wait_ge(own.sem, own.at(t, m + 2))
                    v, m = rs[:, 1, :], m + 2
                pool.tensor_tensor(rs[:, 0, :], v, c.eps[:, 0:SUB] if centred else c.eps[:, 8:8 + SUB],
                                   ALU.add).then_inc(own.sem, 1)
                pool.wait_ge(own.sem, own.at(t, m + 1))
                pool.tensor_tensor(rs[:, 1, :], rs[:, 0, :], c.eps[:, 4:4 + SUB], ALU.pow).then_inc(ready.sem, 1)

            def front(t):
                def both_norms():
                    v, a, r1, b_, d_, r2 = (fmv[:, :, 1],) + tuple(frs[:, k, :] for k in range(5))
                    steps = ((a, v, c.eps[:, 0:SUB], ALU.add), (r1, a, c.eps[:, 4:4 + SUB], ALU.pow),
                             (b_, r1, r1, ALU.mult), (d_, b_, v, ALU.mult), (a, d_, c.eps[:, 8:8 + SUB], ALU.add))
                    pool.wait_ge(f_var.sem, f_var.at(t, 2))
                    for k, (o, p_, q, op) in enumerate(steps):
                        pool.tensor_tensor(o, p_, q, op).then_inc(f_pool.sem, 1)
                        pool.wait_ge(f_pool.sem, f_pool.at(t, k + 2))
                    pool.tensor_tensor(r2, a, c.eps[:, 4:4 + SUB], ALU.pow).then_inc(f_rstd.sem, 1)

                def low(n):
                    def f():
                        for k in range(KC):
                            pool.wait_ge(x_hi.sem, x_hi.at(t, n * KC + k + 1))
                            pool.tensor_tensor(xlo[:, k, :], xf[:, k, :], xhi[:, k, :],
                                               ALU.subtract).then_inc(x_lo.sem, 1)
                    return f

                def qnorm(s):
                    pool.wait_ge(ss_ready.sem, ss_ready.at(t, s + 1))
                    pool.tensor_tensor(qrs[:, 0, :], ss[:, :], c.eps[:, 12:13].to_broadcast([P, 2 * HEADS]),
                                       ALU.mult).then_inc(q_pool.sem, 1)
                    pool.wait_ge(q_pool.sem, q_pool.at(t, 2 * s + 1))
                    pool.tensor_tensor(qrs[:, 1, :], qrs[:, 0, :], c.eps[:, 8:9].to_broadcast([P, 2 * HEADS]),
                                       ALU.add).then_inc(q_pool.sem, 1)
                    pool.wait_ge(q_pool.sem, q_pool.at(t, 2 * s + 2))
                    pool.tensor_tensor(qrs[:, 0, :], qrs[:, 1, :], c.eps[:, 4:5].to_broadcast([P, 2 * HEADS]),
                                       ALU.pow).then_inc(q_rstd.sem, 1)

                def prep(*subs):
                    def f():
                        for s in subs:
                            qnorm(s)
                    return f

                def weights(b):
                    def f():
                        for h in range(HEADS):
                            n = b * HEADS + h
                            pool.wait_ge(p_hi.sem, p_hi.at(t, n + 1))
                            pool.tensor_tensor(pl[:, h % 2, :], pf[:, h % 2, :], ph[:, h % 2, :],
                                               ALU.subtract).then_inc(p_lo.sem, 1)
                    return f
                return {0: lambda: rstd(fmv, frs, f_var, f_rstd, f_pool, t, 0, 0, True), 1: low(0), 5: both_norms, 6: low(1), 7: prep(0, 1), 9: weights(0),
                        10: prep(2, 3), 12: weights(1), 13: low(2)}

            def back(t):
                def low(first, dsts):
                    for n, (dst, k) in enumerate(dsts):
                        m = first + n
                        pool.wait_ge(hi_ready.sem, hi_ready.at(t, m + 1))
                        pool.tensor_tensor(hid_lo[dst][:, k, :], g[:, m % 2, :], hid_hi[dst][:, k, :],
                                           ALU.subtract).then_inc(lo_ready.sem, 1)

                def b1():
                    for k in range(KC):
                        pool.wait_ge(y_hi.sem, y_hi.at(t, k + 1))
                        pool.tensor_tensor(ylo[:, k, :], yf[:, k, :], yhi[:, k, :], ALU.subtract).then_inc(y_lo.sem, 1)

                def segment(n):
                    def f():
                        for w in SEGMENT[n]:
                            if w[0] == "up":
                                _, _, dst, cs = UPS[w[1]]
                                low(first_hid[w[1]], [(dst, k) for k in range(cs)])
                            elif w[0] == "gated":
                                low(first_hid["e1"], [(0, k) for k in range(HC)])
                    return f
                return {0: lambda: rstd(bmv, brs, b_var, b_rstd, b_pool, t, 0, 0, False), 1: b1,
                        **{n: segment(n) for n in SEGMENT}}
            run(pool, front, back)

        @block.scalar
        def _(act):
            def halves(src, f, hi, gain, psum_ready, ready, low_done, t, n, at_low):
                for k in range(KC):
                    act.wait_ge(psum_ready.sem, psum_ready.at(t, n * KC + k + 1))
                    act.wait_ge(low_done.sem, low_done.at(t, at_low))
                    scale = 1.0 if gain is None else c.vec[:, gain + k:gain + k + 1]
                    act.activation(f[:, k, :], src[k][:, :], ACT.Identity, scale=scale)
                    act.activation(hi[:, k, :], src[k][:, :], ACT.Identity, scale=scale).then_inc(ready.sem, 1)

            def front(t):
                def split(n, gain):
                    return lambda: halves(fb, xf, xhi, gain, xnT, x_hi, x_lo, t, n, n * KC)

                def evacuate(k):
                    def f():
                        b = (fb[2], fb[3]) if k == 0 else (fb[0], fb[1])
                        act.wait_ge(k_ps.sem, k_ps.at(t, k + 1))
                        act.activation(kk[:, k, :], b[0][:, :], ACT.Copy)
                        act.wait_ge(r_ps.sem, r_ps.at(t, k + 1))
                        act.activation(vv[:, k, :], b[1][:, :], ACT.Copy).then_inc(kv_ready.sem, 1)
                        act.activation(tr[:, k, :], b[1][:, :], ACT.Tanh, scale=0.5).then_inc(tr_ready.sem, 1)
                    return f

                def exps(k):
                    def f():
                        act.wait_ge(arg_ready.sem, arg_ready.at(t, k + 1))
                        act.activation(T[:, 0:4, :], T[:, 0:4, :], ACT.Exp).then_inc(exp_ready.sem, 1)
                    return f

                def f2():
                    evacuate(0)()
                    evacuate(1)()

                def zsplit(k):
                    act.wait_ge(z_ready.sem, z_ready.at(t, k + 1))
                    act.activation(xhi[:, k, :], z, ACT.Copy).then_inc(z_hi.sem, 1)

                def f3():
                    exps(0)()
                    zsplit(0)

                def f4():
                    exps(1)()
                    zsplit(1)

                def prep(*subs):
                    def f():
                        for s in subs:
                            act.wait_ge(qk_ps.sem, qk_ps.at(t, s + 1))
                            act.activation(qkr, fb[2][:, :], ACT.Copy)
                            act.activation(qsq, fb[2][:, :], ACT.Square).then_inc(qk_sq.sem, 1)
                            act.wait_ge(v_ps.sem, v_ps.at(t, s + 1))
                            act.wait_ge(v_lo.sem, v_lo.at(t, s))
                            act.activation(vf, fb[3][:, 0:D], ACT.Copy)
                            act.activation(vh[:, s % 2, :, 0:HD], fb[3][:, 0:D].rearrange("p (h d) -> p h d", h=HEADS),
                                           ACT.Copy).then_inc(v_hi.sem, 1)
                            for j, dst in enumerate((qT, kT)):
                                act.wait_ge(qkT_ps.sem, qkT_ps.at(t, 2 * s + j + 1))
                                act.activation(dst[:, :, (s % 2) * P:(s % 2 + 1) * P],
                                               fb[j][:, :].bitcast(BF16).rearrange("p (h n) -> p h n", h=HEADS // 2),
                                               ACT.Copy).then_inc(qkT_ready.sem, 1)
                    return f

                def weights(b):
                    def f():
                        act.wait_ge(negT_ps.sem, negT_ps.at(t, b + 1))
                        act.activation(negT[:, :], fb[2][:, 0:P].bitcast(BF16), ACT.Copy).then_inc(negT_ready.sem, 1)
                        for h in range(HEADS):
                            n = b * HEADS + h
                            act.wait_ge(P_ps.sem, P_ps.at(t, n + 1))
                            act.wait_ge(p_lo.sem, p_lo.at(t, max(n - 1, 0)))
                            act.activation(pf[:, h % 2, :], fb[h % 2][:, 0:3 * P], ACT.Exp).then_inc(p_f.sem, 1)
                        for q in range(2):
                            act.wait_ge(pv_ps.sem, pv_ps.at(t, (b + 1) * HEADS))
                            act.activation(ou[:, q, :, :], fb[2 + q][:, 0:HEADS * VW].rearrange("p (h d) -> p h d", h=HEADS),
                                           ACT.Copy).then_inc(ou_ready.sem, 1)
                    return f
                return {1: split(0, None), 2: f2, 3: f3, 4: f4, 6: split(1, VEC["n1_w"]), 7: prep(0, 1),
                        9: weights(0), 10: prep(2, 3), 12: weights(1), 13: split(2, None)}

            def back(t):
                def b1():
                    halves(bb[2:4], yf, yhi, VEC["n2_w"], ynT, y_hi, y_lo, t, 0, 0)
                    act.wait_ge(lg_shift.sem, lg_shift.at(t))
                    act.activation(pr[:, :, :], lg[:, :, :], ACT.Exp).then_inc(lg_exp.sem, 1)

                def gelus(first_u, first_h, dst, cs):
                    for k in range(cs):
                        u, h = first_u + k, first_h + k
                        act.wait_ge(up_ps.sem, up_ps.at(t, u + 1))
                        act.wait_ge(lo_ready.sem, lo_ready.at(t, max(h - 1, 0)))
                        act.activation(g[:, h % 2, :], bb[2 + u % 2][:, :], ACT.Gelu)
                        act.activation(hid_hi[dst][:, k, :], bb[2 + u % 2][:, :], ACT.Gelu).then_inc(hi_ready.sem, 1)

                def segment(n):
                    def f():
                        for w in SEGMENT[n]:
                            if w[0] == "up":
                                _, _, dst, cs = UPS[w[1]]
                                gelus(first_up[w[1]], first_hid[w[1]], dst, cs)
                            elif w[0] == "gated":
                                for k in range(HC):
                                    u, h = first_up["e1"] + 2 * k, first_hid["e1"] + k
                                    act.wait_ge(up_ps.sem, up_ps.at(t, u + 1))
                                    act.activation(sl[:, :], bb[2][:, :], ACT.Tanh, scale=0.5).then_inc(gate_th.sem, 1)
                                    act.wait_ge(gate_sl.sem, gate_sl.at(t, k + 1))
                                    act.activation(hid_hi[0][:, k, :], g[:, h % 2, :], ACT.Copy).then_inc(hi_ready.sem, 1)
                    return f
                return {1: b1, **{n: segment(n) for n in SEGMENT}}
            run(act, front, back)

        @block.vector
        def _(dve):
            F, B = Steps(dve, f_steps), Steps(dve, b_steps)

            def norm(S, src, dst, st, mv, rs, var, rstd, t, n, centred, ready, own=None):
                S.settle()
                for s in range(SUB):
                    S.done(dve.bn_stats(st[:, s, :], src[:, s * D:(s + 1) * D]))
                S.settle()
                S.done(dve.tensor_copy(c.scr[:, 0:1], c.scr[:, 1:2]))
                for s in range(SUB):
                    i = dve.bn_aggr(mv[:, s, :], st[:, s, :])
                i.then_inc(var.sem, 1)
                dve.wait_ge(rstd.sem, rstd.at(t, n + 1))
                if own is not None:
                    for s in range(SUB):
                        q = slice(s * D, (s + 1) * D)
                        i = dve.tensor_scalar(src[:, q], src[:, q], mv[:, s, 0:1], rs[:, 1, s:s + 1],
                                              ALU.subtract, ALU.mult)
                    S.done(i)
                    S.settle()
                    rs = own
                for s in range(SUB):
                    a = (mv[:, s, 0:1], rs[:, 1, s:s + 1], ALU.subtract, ALU.mult) if centred else \
                        (rs[:, 1, s:s + 1], None, ALU.mult)
                    i = dve.tensor_scalar(dst[:, s * D:(s + 1) * D], src[:, s * D:(s + 1) * D], *a)
                i.then_inc(ready.sem, 1)

            dve.memset(pp[:, :, 0:1], -1e38).then_inc(set_up.sem, 1)
            dve.memset(av[:, :, 0:1], 0.0).then_inc(set_up.sem, 1)
            dve.memset(bv[:, :, 0:1], 0.0).then_inc(set_up.sem, 1)
            dve.memset(vh[:, :, :, HD:VW], 1.0).then_inc(set_up.sem, 1)
            dve.memset(qs[:, :, 3 * HD:], 0.0).then_inc(set_up.sem, 1)
            dve.memset(ks[:, :, 3 * HD:], 0.0).then_inc(set_up.sem, 1)
            dve.memset(below[:, :, :], 0.0).then_inc(set_up.sem, 1)
            dve.memset(nstack[:, :, :], 0.0).then_inc(set_up.sem, 1)
            dve.wait_ge(set_up.sem, 8)
            for e in range(1, E1):
                dve.memset(below[:, e, 0:e], 1.0).then_inc(set_up.sem, 1)
            dve.wait_ge(set_up.sem, 8 + E1 - 1)

            def front(t):
                here = bass.ds(t * SUB * D, SUB * D)

                def f0():
                    F.begin(t)
                    dve.wait_ge(yn_ready.sem, yn_ready.at(t, 0))
                    dve.tensor_copy(c.scr[:, 0:1], c.scr[:, 1:2])
                    F.done(dve.tensor_copy(h2[:, :], c.h[:, here]))
                    norm(F, h2, xn, fst, fmv, frs, f_var, f_rstd, t, 0, True, xn_ready)

                def seqs(a, n=SEQ):
                    return a.rearrange("p (b n) -> p b n", b=SEQS)

                def recur_args(k):
                    def f():
                        w, u = c.dec[:, 4 + k:5 + k], c.vec[:, VEC["first1"] + k:VEC["first1"] + k + 1]
                        dve.wait_ge(kv_ready.sem, kv_ready.at(t, k + 1))
                        for b in range(SEQS):
                            F.done(dve.tensor_tensor_scan(pp[:, b, 1:], w.to_broadcast([P, SEQ]),
                                                          kk[:, k, b * SEQ:(b + 1) * SEQ], -1e38, ALU.add, ALU.max))
                        F.settle()
                        before, now, K = pp[:, :, 0:SEQ], pp[:, :, 1:], seqs(kk[:, k, :])
                        F.done(dve.scalar_tensor_tensor(seqs(T[:, 0, :]), before, w, now, ALU.add, ALU.subtract))
                        F.done(dve.tensor_tensor(seqs(T[:, 1, :]), K, now, ALU.subtract))
                        F.done(dve.scalar_tensor_tensor(seqs(T[:, 4, :]), K, u, before, ALU.add, ALU.max))
                        F.settle()
                        F.done(dve.tensor_tensor(seqs(T[:, 2, :]), before, seqs(T[:, 4, :]), ALU.subtract))
                        dve.scalar_tensor_tensor(T[:, 3, :], kk[:, k, :], u, T[:, 4, :], ALU.add,
                                                 ALU.subtract).then_inc(arg_ready.sem, 1)
                    return f

                def recur(k):
                    def f():
                        V = vv[:, k, :]
                        dve.wait_ge(exp_ready.sem, exp_ready.at(t, k + 1))
                        F.done(dve.tensor_tensor(T[:, 4, :], T[:, 1, :], V, ALU.mult))
                        for b in range(SEQS):
                            q = slice(b * SEQ, (b + 1) * SEQ)
                            F.done(dve.tensor_tensor_scan(bv[:, b, 1:], T[:, 0, q], T[:, 1, q], 0.0, ALU.mult, ALU.add))
                        F.settle()
                        for b in range(SEQS):
                            q = slice(b * SEQ, (b + 1) * SEQ)
                            F.done(dve.tensor_tensor_scan(av[:, b, 1:], T[:, 0, q], T[:, 4, q], 0.0, ALU.mult, ALU.add))
                        F.settle()
                        F.done(dve.tensor_tensor(seqs(T[:, 0, :]), seqs(T[:, 2, :]), av[:, :, 0:SEQ], ALU.mult))
                        F.done(dve.tensor_tensor(T[:, 4, :], T[:, 3, :], V, ALU.mult))
                        F.done(dve.tensor_tensor(seqs(T[:, 1, :]), seqs(T[:, 2, :]), bv[:, :, 0:SEQ], ALU.mult))
                        F.settle()
                        F.done(dve.tensor_tensor(T[:, 0, :], T[:, 0, :], T[:, 4, :], ALU.add))
                        F.done(dve.tensor_tensor(T[:, 3, :], T[:, 1, :], T[:, 3, :], ALU.add))
                        F.settle()
                        F.done(dve.reciprocal(T[:, 2, :], T[:, 3, :]))
                        F.settle()
                        F.done(dve.scalar_tensor_tensor(T[:, 1, :], T[:, 0, :], 0.5, T[:, 2, :], ALU.mult, ALU.mult))
                        F.settle()
                        dve.wait_ge(tr_ready.sem, tr_ready.at(t, k + 1))
                        dve.scalar_tensor_tensor(z, tr[:, k, :], 1.0, T[:, 1, :], ALU.add,
                                                 ALU.mult).then_inc(z_ready.sem, 1)
                        dve.wait_ge(z_hi.sem, z_hi.at(t, k + 1))
                        dve.tensor_tensor(xlo[:, k, :], z, xhi[:, k, :], ALU.subtract).then_inc(z_lo.sem, 1)
                    return f

                def f2():
                    recur_args(0)()

                def f3():
                    recur(0)()
                    recur_args(1)()

                def f4():
                    recur(1)()

                def f5():
                    for j in range(2):
                        q = slice(j * TT, (j + 1) * TT)
                        dve.wait_ge(o_ps.sem, o_ps.at(t, j + 1))
                        dve.tensor_tensor(h2[:, q], h2[:, q], fb[2 + j][:, :], ALU.add).then_inc(h2_ready.sem, 1)
                    dve.wait_ge(h2_ready.sem, h2_ready.at(t))
                    dve.tensor_copy(c.scr[:, 0:1], c.scr[:, 1:2])
                    F.done(dve.tensor_copy(c.h[:, here], h2[:, :]))
                    norm(F, h2, xn, fst, fmv, frs, f_var, f_rstd, t, 1, False, xn_ready, frs[:, 3:5, :])

                def prep(*subs):
                    def f():
                        for s in subs:
                            heads = qkr.rearrange("p (h d) -> p h d", h=2 * HEADS)
                            dve.wait_ge(qk_sq.sem, qk_sq.at(t, s + 1))
                            dve.tensor_reduce(ss[:, :], qsq.rearrange("p (h d) -> p h d", h=2 * HEADS), AX.X,
                                              ALU.add).then_inc(ss_ready.sem, 1)
                            dve.wait_ge(v_hi.sem, v_hi.at(t, s + 1))
                            dve.tensor_tensor(vl[:, s % 2, :, :], vf.rearrange("p (h d) -> p h d", h=HEADS),
                                              vh[:, s % 2, :, 0:HD], ALU.subtract).then_inc(v_lo.sem, 1)
                            dve.wait_ge(q_rstd.sem, q_rstd.at(t, s + 1))
                            F.done(dve.tensor_tensor(heads, heads, qrs[:, 0, :].unsqueeze(2).to_broadcast(
                                [P, 2 * HEADS, HD]), ALU.mult))
                            F.settle()
                            for j in range(2):
                                part = heads[:, j * HEADS:(j + 1) * HEADS, :]
                                F.done(dve.tensor_tensor(part, part, c.qkw2[:, j * HD:(j + 1) * HD].unsqueeze(1)
                                                         .to_broadcast([P, HEADS, HD]), ALU.mult))
                            F.settle()
                            qh, kh = heads[:, 0:HEADS, :], heads[:, HEADS:, :]
                            F.done(dve.tensor_copy(qs[:, :, 0:HD], qh))
                            F.done(dve.tensor_copy(qs[:, :, HD:2 * HD], qh))
                            F.done(dve.tensor_copy(ks[:, :, 0:HD], kh))
                            F.done(dve.tensor_copy(ks[:, :, 2 * HD:3 * HD], kh))
                            F.settle()
                            dve.tensor_tensor(qs[:, :, 2 * HD:3 * HD], qh, qs[:, :, 0:HD],
                                              ALU.subtract).then_inc(q_stack.sem, 1)
                            dve.tensor_tensor(ks[:, :, HD:2 * HD], kh, ks[:, :, 0:HD],
                                              ALU.subtract).then_inc(k_stack.sem, 1)
                    return f

                def maxima(b):
                    def f():
                        for n in range(12):
                            m = b * 12 + n
                            dve.wait_ge(S_ps.sem, S_ps.at(t, m + 1))
                            if n < 8:
                                o, w = mx[:, 1, group(n)[0]:group(n)[-1] + 1:2], SEQ
                            else:
                                o, w = mx[:, 0, group(n)[0]:group(n)[-1] + 1:2], P
                            dve.tensor_reduce(o, fb[n % 2][:, :].rearrange("p (h k) -> p h k", k=w), AX.X,
                                              ALU.max).then_inc(mx_ready.sem, 1)
                        dve.wait_ge(mx_ready.sem, mx_ready.at(t, (b + 1) * 12))
                        F.done(dve.tensor_scalar(npart[:, :, :, 0], mx[:, :, :], -1.0, None, ALU.mult))
                        F.settle()
                        F.done(dve.scalar_tensor_tensor(mr[:, 0, :, :], mx[:, :, :], -1.0, npart[:, :, :, 0], ALU.mult,
                                                        ALU.subtract))
                        F.settle()
                        F.done(dve.tensor_copy(npart[:, :, :, 1], mr[:, 0, :, :]))
                        F.settle()
                        dve.tensor_tensor(npart[:, :, :, 2], mr[:, 0, :, :], npart[:, :, :, 1],
                                          ALU.subtract).then_inc(np_ready.sem, 1)
                    return f

                def weights(b):
                    def f():
                        for h in range(HEADS):
                            n = b * HEADS + h
                            dve.wait_ge(p_f.sem, p_f.at(t, n + 1))
                            dve.wait_ge(pv_ps.sem, pv_ps.at(t, max(n - 1, 0)))
                            dve.tensor_copy(ph[:, h % 2, :], pf[:, h % 2, :]).then_inc(p_hi.sem, 1)
                        dve.wait_ge(ou_ready.sem, ou_ready.at(t, 2 * (b + 1)))
                        F.done(dve.reciprocal(den[:, :, :], ou[:, :, :, HD]))
                        F.settle()
                        for q in range(2):
                            o = xn[:, (2 * b + q) * D:(2 * b + q + 1) * D].rearrange("p (h d) -> p h d", h=HEADS)
                            i = dve.tensor_tensor(o, ou[:, q, :, 0:HD], den[:, q, :].unsqueeze(2).to_broadcast(
                                [P, HEADS, HD]), ALU.mult)
                            if q == 0 or b == 0:
                                F.done(i)
                        if b == SEQS - 1:
                            i.then_inc(xn_ready.sem, 1)
                    return f

                def f13():
                    for j in range(2):
                        dve.wait_ge(ao_ps.sem, ao_ps.at(t, j + 1))
                        q = h2[:, j * TT:(j + 1) * TT].rearrange("p (s d) -> p s d", s=2)[:, :, ZERO:]
                        F.done(dve.tensor_tensor(q, q, fb[2 + j][:, :].rearrange("p (s d) -> p s d", s=2)[:, :, 0:DZ],
                                                 ALU.add))
                    F.settle()
                    dve.tensor_tensor(c.h[:, here], c.h[:, here], h2[:, :], ALU.add).then_inc(h3_ready.sem, 1)
                    F.end()
                return {0: f0, 2: f2, 3: f3, 4: f4, 5: f5, 7: prep(0, 1), 8: maxima(0), 9: weights(0),
                        10: prep(2, 3), 11: maxima(1), 12: weights(1), 13: f13}

            def back(t):
                def b0():
                    B.begin(t)
                    dve.wait_ge(h3_ready.sem, h3_ready.at(t))
                    norm(B, h2, yn, bst, bmv, brs, b_var, b_rstd, t, 0, False, yn_ready)

                def b1():
                    dve.wait_ge(lg_ps.sem, lg_ps.at(t))
                    dve.tensor_copy(pr[:, :, :], bb[0][:, 0:SUB * E1].rearrange("p (s e) -> p s e", s=SUB)
                                    ).then_inc(lg_ready.sem, 1)
                    dve.wait_ge(lg_ready.sem, lg_ready.at(t))
                    dve.wait_ge(down_used.sem, down_used.at(t, 0))
                    B.done(dve.memset(lg[:, :, :], 0.0))
                    B.settle()
                    B.done(dve.tensor_tensor(wt[:, :, :], pr[:, :, :], pr[:, :, :], ALU.is_equal))
                    B.settle()
                    B.done(dve.tensor_copy(c.scr[:, 0:1], c.scr[:, 1:2]))
                    B.done(dve.copy_predicated(lg[:, :, :], wt[:, :, :].bitcast(U32), pr[:, :, :]))
                    B.settle()
                    B.done(dve.tensor_scalar(lg[:, :, :], lg[:, :, :], -3.4028234e38, 3.4028234e38, ALU.max, ALU.min))
                    B.settle()
                    B.done(dve.tensor_reduce(r1[:, 0, :], lg[:, :, :], AX.X, ALU.max))
                    B.settle()

                    def over(n):
                        return r1[:, n, :].unsqueeze(2).to_broadcast([P, SUB, E1])
                    dve.tensor_tensor(lg[:, :, :], lg[:, :, :], over(0), ALU.subtract).then_inc(lg_shift.sem, 1)
                    dve.wait_ge(lg_exp.sem, lg_exp.at(t))
                    B.done(dve.tensor_reduce(r1[:, 1, :], pr[:, :, :], AX.X, ALU.add))
                    B.settle()
                    B.done(dve.reciprocal(r1[:, 2, :], r1[:, 1, :]))
                    B.settle()
                    B.done(dve.tensor_tensor(pr[:, :, :], pr[:, :, :], over(2), ALU.mult))
                    B.settle()
                    pj = pr[:, :, :].unsqueeze(2).to_broadcast([P, SUB, E1, E1])
                    pe_ = pr[:, :, :].unsqueeze(3).to_broadcast([P, SUB, E1, E1])
                    B.done(dve.tensor_tensor(gt[:, :, :, :], pj, pe_, ALU.is_gt))
                    B.done(dve.tensor_tensor(eq[:, :, :, :], pj, pe_, ALU.is_equal))
                    B.settle()
                    B.done(dve.tensor_tensor(eq[:, :, :, :], eq[:, :, :, :],
                                             below[:, :, :].unsqueeze(1).to_broadcast([P, SUB, E1, E1]), ALU.mult))
                    B.settle()
                    B.done(dve.tensor_tensor(gt[:, :, :, :], gt[:, :, :, :], eq[:, :, :, :], ALU.add))
                    B.settle()
                    B.done(dve.tensor_reduce(lg[:, :, :], gt[:, :, :, :], AX.X, ALU.add))
                    B.settle()
                    B.done(dve.scalar_tensor_tensor(wt[:, :, :], lg[:, :, :], 2.0, pr[:, :, :], ALU.is_lt, ALU.mult))
                    B.settle()
                    B.done(dve.tensor_reduce(r1[:, 0, :], wt[:, :, :], AX.X, ALU.add))
                    B.settle()
                    B.done(dve.tensor_scalar(r1[:, 1, :], r1[:, 0, :], 1e-8, None, ALU.add))
                    B.settle()
                    B.done(dve.reciprocal(r1[:, 3, :], r1[:, 1, :]))
                    B.settle()
                    B.done(dve.tensor_tensor(wt[:, :, :], wt[:, :, :], over(3), ALU.mult))
                    B.settle()

                def segment(n):
                    def f():
                        for w in SEGMENT[n]:
                            if w[0] == "gated":
                                for k in range(HC):
                                    h = first_hid["e1"] + k
                                    u = first_up["e1"] + 2 * k
                                    dve.wait_ge(gate_th.sem, gate_th.at(t, k + 1))
                                    B.done(dve.scalar_tensor_tensor(sl2[:, :], sl[:, :], 1.0, bb[2][:, :], ALU.add,
                                                                    ALU.mult))
                                    B.settle()
                                    dve.wait_ge(up_ps.sem, up_ps.at(t, u + 2))
                                    dve.wait_ge(lo_ready.sem, lo_ready.at(t, h - 1))
                                    dve.scalar_tensor_tensor(g[:, h % 2, :], sl2[:, :], 0.5, bb[3][:, :], ALU.mult,
                                                             ALU.mult).then_inc(gate_sl.sem, 1)
                            elif w[0] == "down":
                                d, e = first_down[w[1]], w[2]
                                dve.wait_ge(down_ps.sem, down_ps.at(t, d + 1))
                                dve.wait_ge(down_used.sem, down_used.at(t, d * SUB))
                                for s in range(SUB):
                                    q = bass.ds((t * SUB + s) * D + ZERO, DZ)
                                    dve.scalar_tensor_tensor(c.h[:, q], bb[s // 2][:, (s % 2) * D:(s % 2) * D + DZ],
                                                             wt[:, s, e:e + 1], c.h[:, q], ALU.mult,
                                                             ALU.add).then_inc(down_used.sem, 1)
                        if n == 8:
                            B.end()
                    return f
                return {0: b0, 1: b1, **{n: segment(n) for n in SEGMENT}}
            run(dve, front, back)

        @block.tensor
        def _(pe):
            PARTS = ((0, 0), (1, 0), (0, 1))
            WC = (c.WC_hi, c.WC_lo)

            def feature_major(bank, name, e, xs, kc=KC, lo_wait=None):
                for j, (wp, xp) in enumerate(PARTS):
                    if j == 2 and lo_wait is not None:
                        pe.wait_ge(*lo_wait)
                    for k in range(kc):
                        m = pe.matmul(bank[:, :], W(WC[wp], name, k, e * P, P), xs[xp][:, k, :],
                                      start=(j == 0 and k == 0), stop=(j == 2 and k == kc - 1))
                return m

            def token_major(o, name, s, xs, n):
                for j, (wp, xp) in enumerate(PARTS):
                    for k in range(KC):
                        m = pe.matmul(o, xs[xp][:, k, s * P:(s + 1) * P], W(WC[wp], name, k, 0, n),
                                      start=(j == 0 and k == 0), stop=(j == 2 and k == KC - 1))
                return m

            def transposes(src, banks, ready):
                for k in range(KC):
                    for s in range(SUB):
                        m = pe.transpose(banks[k][:, s * P:(s + 1) * P], src[:, s * D + k * P:s * D + (k + 1) * P],
                                         c.ident[:, :])
                    m.then_inc(ready.sem, 1)

            X = (xhi, xlo)

            def front(t):
                def f1():
                    pe.wait_ge(xn_ready.sem, xn_ready.at(t, 1))
                    pe.wait_ge(x_hi.sem, x_hi.at(t, 0))
                    transposes(xn, fb, xnT)

                def f2():
                    pe.wait_ge(x_hi.sem, x_hi.at(t, KC))
                    pe.wait_ge(h3_ready.sem, h3_ready.at(t, 0))
                    feature_major(fb[2], "Wk", 0, X, lo_wait=(x_lo.sem, x_lo.at(t, KC))).then_inc(k_ps.sem, 1)
                    feature_major(fb[3], "Wr", 0, X).then_inc(r_ps.sem, 1)
                    feature_major(fb[0], "Wk", 1, X).then_inc(k_ps.sem, 1)
                    feature_major(fb[1], "Wr", 1, X).then_inc(r_ps.sem, 1)

                def f5():
                    pe.wait_ge(z_hi.sem, z_hi.at(t))
                    pe.wait_ge(z_lo.sem, z_lo.at(t))
                    pe.wait_ge(tr_ready.sem, tr_ready.at(t))
                    for s in range(SUB):
                        m = token_major(fb[2 + s // 2][:, (s % 2) * D:(s % 2 + 1) * D], "Wo", s, X, D)
                        if s % 2:
                            m.then_inc(o_ps.sem, 1)

                def f6():
                    pe.wait_ge(xn_ready.sem, xn_ready.at(t, 2))
                    transposes(xn, fb, xnT)

                def prep(*subs):
                    def stacks(s):
                        for j, (src, ready) in enumerate(((qs, q_stack), (ks, k_stack))):
                            pe.wait_ge(ready.sem, ready.at(t, s + 1))
                            if s > 0:
                                pe.wait_ge(qkT_ready.sem, qkT_ready.at(t, 2 * s + j - 1))
                            bank = fb[j][:, :].bitcast(BF16)
                            for h in range(HEADS // 2):
                                m = pe.transpose(bank[:, h * P:(h + 1) * P],
                                                 src[:, 2 * h:2 * h + 2, :].rearrange("p a d -> p (a d)"),
                                                 c.identb[:, :])
                            m.then_inc(qkT_ps.sem, 1)

                    def g():
                        for s in subs:
                            if s == 0:
                                pe.wait_ge(x_hi.sem, x_hi.at(t, 2 * KC))
                                pe.wait_ge(x_lo.sem, x_lo.at(t, 2 * KC))
                                pe.wait_ge(h2_ready.sem, h2_ready.at(t))
                            else:
                                pe.wait_ge(v_hi.sem, v_hi.at(t, s))
                            if s == 2:
                                pe.wait_ge(ou_ready.sem, ou_ready.at(t, 2))
                            token_major(fb[2][:, :], "wqk", s, X, 2 * D).then_inc(qk_ps.sem, 1)
                            token_major(fb[3][:, 0:D], "wv", s, X, D).then_inc(v_ps.sem, 1)
                            stacks(s)
                    return g

                def rows(h):
                    return slice(64 * (h % 2), 64 * (h % 2) + 64)

                def maxima(b):
                    def f():
                        pe.wait_ge(qkT_ready.sem, qkT_ready.at(t, 4 * (b + 1)))
                        for n in range(12):
                            m = b * 12 + n
                            if n >= 2:
                                pe.wait_ge(mx_ready.sem, mx_ready.at(t, m - 1))
                            bank = fb[n % 2]
                            if n < 8:
                                for j, h in enumerate(group(n)):
                                    q = j * SEQ
                                    pe.matmul(bank[:, q:q + SEQ], qT[rows(h), h // 2, P:2 * P], kT[rows(h), h // 2, :],
                                              start=True, stop=False, skip_group_check=True)
                                    i = pe.matmul(bank[:, q + P:q + SEQ], c.identb[:, :], c.mask[:, 0:P],
                                                  start=False, stop=True, skip_group_check=True)
                            else:
                                for j, h in enumerate(group(n)):
                                    q = j * P
                                    pe.matmul(bank[:, q:q + P], qT[rows(h), h // 2, 0:P], kT[rows(h), h // 2, 0:P],
                                              start=True, stop=False, skip_group_check=True)
                                    i = pe.matmul(bank[:, q:q + P], c.identb[:, :], c.mask[:, 0:P],
                                                  start=False, stop=True, skip_group_check=True)
                            i.then_inc(S_ps.sem, 1)
                    return f

                def weights(b):
                    def scores(h):
                        n = b * HEADS + h
                        bank = fb[h % 2]
                        if h >= 2:
                            pe.wait_ge(p_f.sem, p_f.at(t, n - 1))
                        for lo, ks_, qs_ in ((0, 0, 0), (SEQ, P, P)):
                            w = SEQ - qs_
                            pe.matmul(bank[:, lo:lo + w], kT[rows(h), h // 2, ks_:ks_ + P], qT[rows(h), h // 2, qs_:SEQ],
                                      start=True, stop=False, skip_group_check=True)
                            pe.matmul(bank[:, lo:lo + P], c.identb[:, :], c.mask[:, P:2 * P],
                                      start=False, stop=False, skip_group_check=True)
                            i = pe.matmul(bank[:, lo:lo + w], c.sel[:, h, :], negT[:, qs_:SEQ],
                                          start=False, stop=True, skip_group_check=True)
                        i.then_inc(P_ps.sem, 1)

                    def values(h):
                        n = b * HEADS + h
                        pe.wait_ge(p_hi.sem, p_hi.at(t, n + 1))
                        pe.wait_ge(p_lo.sem, p_lo.at(t, n + 1))
                        for q, blocks in ((0, ((0, 0),)), (1, ((P, 0), (SEQ, 1)))):
                            o = fb[2 + q][:, h * VW:(h + 1) * VW]
                            for a, (lo, kt) in enumerate(blocks):
                                last = a == len(blocks) - 1
                                hi_, lo_ = ph[:, h % 2, lo:lo + P], pl[:, h % 2, lo:lo + P]
                                pe.matmul(o, hi_, vh[:, kt, h, :], start=(a == 0), stop=False, skip_group_check=True)
                                pe.matmul(o[:, 0:HD], hi_, vl[:, kt, h, :], start=False, stop=False,
                                          skip_group_check=True)
                                i = pe.matmul(o, lo_, vh[:, kt, h, :], start=False, stop=last, skip_group_check=True)
                        i.then_inc(pv_ps.sem, 1)

                    def f():
                        pe.wait_ge(np_ready.sem, np_ready.at(t, b + 1))
                        pe.wait_ge(v_hi.sem, v_hi.at(t, 2 * (b + 1)))
                        bank = fb[2][:, 0:P].bitcast(BF16)
                        for q in range(2):
                            m = pe.transpose(bank[:, q * P:(q + 1) * P], nstack[:, q, :],
                                             c.identb[:, :])
                        m.then_inc(negT_ps.sem, 1)
                        pe.wait_ge(negT_ready.sem, negT_ready.at(t, b + 1))
                        pe.wait_ge(v_lo.sem, v_lo.at(t, 2 * (b + 1)))
                        scores(0)
                        for h in range(1, HEADS):
                            scores(h)
                            values(h - 1)
                        values(HEADS - 1)
                    return f

                def f13():
                    pe.wait_ge(xn_ready.sem, xn_ready.at(t, 3))
                    transposes(xn, fb, xnT)
                    pe.wait_ge(x_hi.sem, x_hi.at(t, 3 * KC))
                    pe.wait_ge(x_lo.sem, x_lo.at(t, 3 * KC))
                    for s in range(SUB):
                        m = token_major(fb[2 + s // 2][:, (s % 2) * D:(s % 2) * D + DZ], "wo", s, X, DZ)
                        if s % 2:
                            m.then_inc(ao_ps.sem, 1)
                return {1: f1, 2: f2, 5: f5, 6: f6, 7: prep(0, 1), 8: maxima(0), 9: weights(0), 10: prep(2, 3),
                        11: maxima(1), 12: weights(1), 13: f13}

            def back(t):
                def b1():
                    pe.wait_ge(yn_ready.sem, yn_ready.at(t))
                    pe.wait_ge(gate_sl.sem, gate_sl.at(t, 0))
                    transposes(yn, bb[2:4], ynT)
                    pe.wait_ge(y_hi.sem, y_hi.at(t))
                    pe.wait_ge(down_used.sem, down_used.at(t, 0))
                    for s in range(SUB):
                        for k in range(KC):
                            m = pe.matmul(bb[0][:, s * E1:(s + 1) * E1], yf[:, k, s * P:(s + 1) * P],
                                          c.gate[:, k * E1:(k + 1) * E1], start=(k == 0), stop=(k == KC - 1))
                    m.then_inc(lg_ps.sem, 1)
                    pe.wait_ge(y_lo.sem, y_lo.at(t))

                def free(u):
                    v, g0 = u - 2, first_up["e1"]
                    if 0 <= v < g0:
                        pe.wait_ge(hi_ready.sem, hi_ready.at(t, v + 1))
                    elif v >= g0:
                        pe.wait_ge(gate_sl.sem, gate_sl.at(t, (v - g0) // 2 + 1))

                def ups(name):
                    src, kc, dst, cs = UPS[name]
                    xs = (yhi, ylo) if src is None else (hid_hi[src], hid_lo[src])
                    if src is not None:
                        h = first_hid[maker[name]] + kc
                        pe.wait_ge(hi_ready.sem, hi_ready.at(t, h))
                        pe.wait_ge(lo_ready.sem, lo_ready.at(t, h))
                    for k in range(cs):
                        u = first_up[name] + k
                        free(u)
                        feature_major(bb[2 + u % 2], name, k, xs, kc).then_inc(up_ps.sem, 1)

                def gated():
                    for k in range(HC):
                        for j, name in enumerate(("e1_w1", "e1_w2")):
                            u = first_up["e1"] + 2 * k + j
                            free(u)
                            feature_major(bb[2 + u % 2], name, k, (yhi, ylo)).then_inc(up_ps.sem, 1)

                def down(name, e, src):
                    d = first_down[name]
                    if d == 0:
                        pe.wait_ge(lg_ready.sem, lg_ready.at(t))
                    else:
                        pe.wait_ge(down_used.sem, down_used.at(t, d * SUB))
                    for k in range(HC):
                        h = first_hid[maker[name]] + k + 1
                        pe.wait_ge(hi_ready.sem, hi_ready.at(t, h))
                        pe.wait_ge(lo_ready.sem, lo_ready.at(t, h))
                        for s in range(SUB):
                            for j, (wp, xp) in enumerate(PARTS):
                                xs = (hid_hi[src], hid_lo[src])[xp]
                                m = pe.matmul(bb[s // 2][:, (s % 2) * D:(s % 2) * D + DZ], xs[:, k, s * P:(s + 1) * P],
                                              W(WC[wp], name, k, 0, DZ), start=(k == 0 and j == 0 and s % 2 == 0),
                                              stop=(k == HC - 1 and j == 2), skip_group_check=True)
                    m.then_inc(down_ps.sem, 1)

                def segment(n):
                    def f():
                        for w in SEGMENT[n]:
                            if w[0] == "up":
                                ups(w[1])
                            elif w[0] == "gated":
                                gated()
                            else:
                                down(*w[1:])
                    return f
                return {1: b1, **{n: segment(n) for n in SEGMENT}}
            run(pe, front, back)


def program(nc, ins, out, upto="c"):
    c = Chip()
    c.i = ins
    with ExitStack() as x:
        def sb(name, shape, dt=F32):
            return x.enter_context(nc.sbuf_tensor(name, shape, dt))
        c.h = sb("h", [P, TILES * SUB * D])
        c.w0 = sb("w0", [P, TILES * SUB * E0])
        c.vec, c.dec = sb("vec", [P, NVEC]), sb("dec", [P, 6])
        c.b1, c.b2 = sb("b1", [P, E0 * HC0]), sb("b2", [E0, D])
        c.Wrt, c.br, c.gate = sb("Wrt", [P, KC * E0]), sb("br", [1, E0]), sb("gate", [P, KC * E1])
        c.qkw, c.qkw2 = sb("qkw", [P, 2 * HD]), sb("qkw2", [P, 2 * HD])
        c.ident, c.identb = sb("ident", [P, P]), sb("identb", [P, P], BF16)
        c.mask, c.sel = sb("mask", [P, 2 * P], BF16), sb("sel", [P, HEADS, P], BF16)
        c.ones, c.eps, c.scr = sb("ones", [1, P]), sb("eps", [P, 13]), sb("scr", [P, 2])
        c.xT_hi, c.xT_lo = sb("xT_hi", [P, KC * N], BF16), sb("xT_lo", [P, KC * N], BF16)
        with ExitStack() as a:
            def sa(name, shape, dt=F32):
                return a.enter_context(nc.sbuf_tensor(name, shape, dt))
            c.tok, c.idx, c.zero_i = sa("tok_s", [P, TILES * SUB], I32), sa("idx", [P, SUB], I32), sa("zero_i", [P, SUB], I32)
            c.zero_j = sa("zero_j", [P, 1], I32)
            c.WA_hi, c.WA_lo = sa("WA_hi", [P, COLS_A], BF16), sa("WA_lo", [P, COLS_A], BF16)
            c.idx_ready = a.enter_context(nc.semaphore("idx_ready"))
            phase_load(nc, c)
            phase_a(nc, c)
        if upto == "a":
            s = x.enter_context(nc.semaphore("dump"))
            with nc.Block() as block:
                @block.sync
                def _(sp):
                    sp.dma_start(out[0], c.h[:, :]).then_inc(s, 16)
                    sp.dma_start(out[1], c.w0[:, :]).then_inc(s, 16)
                    sp.wait_ge(s, 32)
            return

        c.WC_hi, c.WC_lo = sb("WC_hi", [P, COLS_C], BF16), sb("WC_lo", [P, COLS_C], BF16)
        phase_b(nc, c)
        if upto == "b":
            s = x.enter_context(nc.semaphore("dump"))
            with nc.Block() as block:
                @block.sync
                def _(sp):
                    sp.dma_start(out[0], c.h[:, :]).then_inc(s, 16)
                    sp.wait_ge(s, 16)
            return

        phase_c(nc, c, out)


def pack(np, m):
    k, n = m.shape
    return np.ascontiguousarray(m.reshape(k // P, P, n).transpose(1, 0, 2).reshape(P, -1))


def layout(inputs):
    import numpy as np
    g = {k: np.asarray(v) for k, v in inputs.items()}
    a = {}
    a["tok"] = np.ascontiguousarray(g["x"].reshape(TILES * SUB, P).T)
    a["emb"] = g["L0_tok_W_E"]
    L = "L0_attn_"
    a["WA"] = np.concatenate([pack(np, g[L + n].T) for n in ("Ww", "Wk", "Wv", "Wr", "Wo", "Wrec", "Wkey", "Wval")], 1)
    names = (L + "ln1_g", L + "ln1_b", L + "ln2_g", L + "ln2_b", L + "time_decay", "L1_attn_time_decay",
             "L1_attn_time_first", "L1_ffn_n1_w", "L1_ffn_n2_w")
    a["vec"] = np.concatenate([g[n].reshape(KC, P).T for n in names], 1)
    a["b1"] = np.ascontiguousarray(g["L0_ffn_b1"].reshape(E0 * HC0, P).T)
    a["b2"] = g["L0_ffn_b2"]
    a["Wrt"] = pack(np, g["L0_ffn_Wr"])
    a["br"] = g["L0_ffn_br"].reshape(1, E0)
    a["gate"] = pack(np, g["L1_ffn_gate_w"].T)
    a["qn"], a["kn"] = g["L1_ffn_qn_w"], g["L1_ffn_kn_w"]
    w0 = np.stack([np.concatenate([pack(np, g["L0_ffn_W1"][e]), pack(np, g["L0_ffn_W2"][e])], 1)
                   for e in range(E0)])
    w0 = w0.reshape(E0, P, TILES, PIECE_E).transpose(0, 2, 1, 3).reshape(PIECES, P, PIECE_E)
    A, Fn = "L1_attn_", "L1_ffn_"
    m = {n: g[A + n].T for n in ("Wk", "Wr", "Wo")}
    m["wqk"] = np.concatenate([g[Fn + "wq"].T, g[Fn + "wk"].T], 1)
    m["wv"], m["wo"] = g[Fn + "wv"].T, g[Fn + "wo"].T[:, ZERO:]
    for n in OFF_C:
        if n[0] == "e":
            m[n] = g[Fn + n].T
            if OFF_C[n][1] == DZ:
                m[n] = m[n][:, ZERO:]
    wc = np.concatenate([pack(np, m[n]) for n in OFF_C], 1).reshape(P, PIECES, PIECE_C).transpose(1, 0, 2)
    a["WP"] = np.concatenate([w0, wc], 2)
    return {k: np.ascontiguousarray(v) for k, v in a.items()}


def kernel(**inputs):
    from concourse import bacc as _bacc
    from concourse.bass_utils import run_bass_kernel_spmd as _run

    arrays = layout(inputs)
    nc = _bacc.Bacc("TRN2", target_bir_lowering=False, num_devices=1)
    ins = {n: nc.dram_tensor(f"in_{n}", list(a.shape), mybir.dt.from_np(a.dtype), kind="ExternalInput").ap()
           for n, a in arrays.items()}
    out = nc.dram_tensor("out", [N, D], F32, kind="ExternalOutput").ap()
    program(nc, ins, out)
    r = _run(nc, [{f"in_{n}": a for n, a in arrays.items()}], core_ids=[0])
    return r.results[0]["out"].reshape(BATCH, SEQ, D)
```

```python
import concourse.bass as bass
from concourse import mybir
from contextlib import ExitStack

F32 = mybir.dt.float32
BF16 = mybir.dt.bfloat16
I32 = mybir.dt.int32
U32 = mybir.dt.uint32
ALU = mybir.AluOpType
ACT = mybir.ActivationFunctionType
AX = mybir.AxisListType

P = 128
BATCH, SEQ, D = 16, 256, 256
N = BATCH * SEQ
KC = D // P
TT = 512
EPS1 = 1.1920929e-07
TILES = N // TT
SUB = TT // P
SEQS = TT // SEQ
VOCAB = 50257
EMB_SCALE = float(D) ** 0.5
LN_EPS, WKV_EPS = 1e-5, 1e-8

F0 = 1024
OFF_A = {}
_at = 0
for _name, _k, _n in (("Ww", D, D), ("Wk", D, D), ("Wv", D, D), ("Wr", D, D), ("Wo", D, D),
                      ("Wrec", D, D), ("Wkey", D, F0), ("Wval", F0, D)):
    OFF_A[_name] = (_at, _n)
    _at += _k // P * _n
COLS_A = _at

E0, H0 = 8, 1024
HC0 = H0 // P
COLS_E = KC * H0 + HC0 * D

HEADS, HD = 16, 16
ZERO = 64
DZ = D - ZERO
E1, HID = 4, 512
OFF_C = {}
_at = 0
for _name, _k, _n in (("Wk", D, D), ("Wr", D, D), ("Wo", D, D),
                      ("wqk", D, 2 * D), ("wv", D, D), ("wo", D, DZ),
                      ("e0_up", D, HID), ("e0_down", HID, DZ),
                      ("e1_w1", D, HID), ("e1_w2", D, HID), ("e1_down", HID, DZ),
                      ("e2_l1", D, HID), ("e2_l2", HID, HID), ("e2_l3", HID, HID), ("e2_l4", HID, DZ),
                      ("e3_down", D, D), ("e3_up", D, HID), ("e3_out", HID, DZ)):
    OFF_C[_name] = (_at, _n)
    _at += _k // P * _n
COLS_C = _at


PIECES = E0 * TILES
PIECE_E, PIECE_C = COLS_E // TILES, COLS_C // PIECES
assert PIECE_C * PIECES == COLS_C

VEC = {n: 2 * i for i, n in enumerate(("ln1_g", "ln1_b", "ln2_g", "ln2_b", "decay0",
                                       "decay1", "first1", "n1_w", "n2_w"))}
NVEC = 2 * len(VEC)


class Count:

    def __init__(self, sem, per, base=0):
        self.sem, self.per, self.base = sem, per, base

    def at(self, t, n=None):
        return t * self.per + ((self.per if n is None else n) + self.base)


class Steps:

    def __init__(self, eng, count):
        self.eng, self.count = eng, count

    def begin(self, t):
        self.t, self.n = t, 0

    def done(self, ins):
        ins.then_inc(self.count.sem, 1)
        self.n += 1

    def settle(self):
        self.eng.wait_ge(self.count.sem, self.count.at(self.t, self.n))

    def end(self):
        assert self.n == self.count.per, (self.n, self.count.per)


class Chip:
    pass


def split_weights(nc, ctx, jobs, tag, engines, free=None):
    pass


def phase_load(nc, c):
    CH = 1024
    NCH = COLS_A // CH
    with ExitStack() as x:
        stage = x.enter_context(nc.sbuf_tensor("stage_a", [P, NCH, CH], F32))
        s_w = [x.enter_context(nc.semaphore(f"ld_weights{k}")) for k in range(NCH)]
        s_v = x.enter_context(nc.semaphore("ld_vectors"))
        s_hi = x.enter_context(nc.semaphore("ld_high"))
        s_lo = x.enter_context(nc.semaphore("ld_low"))
        s_c = x.enter_context(nc.semaphore("ld_constants"))
        s_d = x.enter_context(nc.semaphore("ld_decay"))
        block = x.enter_context(nc.Block())

        @block.sync
        def _(sp):
            for dst, src in ((c.tok, c.i["tok"]), (c.vec, c.i["vec"]), (c.b1, c.i["b1"]), (c.b2, c.i["b2"]),
                             (c.Wrt, c.i["Wrt"]), (c.br, c.i["br"]), (c.gate, c.i["gate"]),
                             (c.qkw[:, 0:HD], c.i["qn"].partition_broadcast(P)),
                             (c.qkw[:, HD:2 * HD], c.i["kn"].partition_broadcast(P))):
                sp.dma_start(dst[:, :] if dst is not c.qkw else dst, src).then_inc(s_v, 16)
            for k in range(NCH):
                sp.dma_start(stage[:, k, :], c.i["WA"][:, k * CH:(k + 1) * CH]).then_inc(s_w[k], 16)
            sp.wait_ge(s_v, 9 * 16)

        @block.scalar
        def _(act):
            act.wait_ge(s_v, 9 * 16)
            act.activation(c.dec[:, 0:4], c.vec[:, VEC["decay0"]:VEC["decay0"] + 4], ACT.Exp).then_inc(s_d, 1)
            for k in range(NCH):
                act.wait_ge(s_w[k], 16)
                act.activation(c.WA_hi[:, k * CH:(k + 1) * CH], stage[:, k, :], ACT.Copy).then_inc(s_hi, 1)

        @block.vector
        def _(dve):
            dve.memset(c.ones[:, :], 1.0).then_inc(s_c, 1)
            dve.memset(c.scr[:, :], 0.0).then_inc(s_c, 1)
            dve.memset(c.eps[:, 0:4], LN_EPS).then_inc(s_c, 1)
            dve.memset(c.eps[:, 4:8], -0.5).then_inc(s_c, 1)
            dve.memset(c.eps[:, 8:12], EPS1).then_inc(s_c, 1)
            dve.memset(c.eps[:, 12:13], 1.0 / HD).then_inc(s_c, 1)
            dve.wait_ge(s_d, 1)
            dve.tensor_scalar(c.dec[:, 4:6], c.dec[:, 2:4], -1.0, None, ALU.mult).then_inc(s_c, 1)
            dve.wait_ge(s_v, 9 * 16)
            dve.tensor_scalar(c.qkw2[:, 0:HD], c.qkw[:, 0:HD], float(HD) ** -0.5, None, ALU.mult).then_inc(s_c, 1)
            dve.tensor_copy(c.qkw2[:, HD:2 * HD], c.qkw[:, HD:2 * HD]).then_inc(s_c, 1)
            for k in range(NCH):
                dve.wait_ge(s_hi, k + 1)
                dve.tensor_tensor(c.WA_lo[:, k * CH:(k + 1) * CH], stage[:, k, :],
                                  c.WA_hi[:, k * CH:(k + 1) * CH], ALU.subtract).then_inc(s_lo, 1)

        @block.gpsimd
        def _(pool):
            pool.memset(c.ident[:, :], 0.0).then_inc(s_c, 1)
            pool.memset(c.identb[:, :], 0.0).then_inc(s_c, 1)
            pool.memset(c.mask[:, :], 0.0).then_inc(s_c, 1)
            pool.memset(c.sel[:, :, :], 0.0).then_inc(s_c, 1)
            pool.memset(c.zero_i[:, :], 0).then_inc(s_c, 1)
            pool.wait_ge(s_c, 14)
            for m in (c.ident, c.identb):
                pool.affine_select(out=m[:, :], in_=m[:, :], compare_op=ALU.not_equal, fill=1.0, base=0,
                                   pattern=[[-1, P]], channel_multiplier=1).then_inc(s_c, 1)
            pool.affine_select(out=c.mask[:, 0:P], in_=c.mask[:, 0:P], compare_op=ALU.is_ge, fill=-1e30, base=0,
                               pattern=[[-1, P]], channel_multiplier=1).then_inc(s_c, 1)
            pool.affine_select(out=c.mask[:, P:2 * P], in_=c.mask[:, P:2 * P], compare_op=ALU.is_ge, fill=-1e30,
                               base=0, pattern=[[1, P]], channel_multiplier=-1).then_inc(s_c, 1)
            for j in range(3):
                pool.wait_ge(s_c, 18 + j)
                pool.affine_select(out=c.sel[:, :, :], in_=c.sel[:, :, :], compare_op=ALU.not_equal, fill=1.0,
                                   base=-j, pattern=[[-3, HEADS], [0, P]], channel_multiplier=1).then_inc(s_c, 1)


def phase_a(nc, c):
    KF, KB = 32, 30
    with ExitStack() as x:
        def sb(name, shape, dt=F32):
            return x.enter_context(nc.sbuf_tensor("a_" + name, shape, dt))

        def count(name, per):
            return Count(x.enter_context(nc.semaphore("a_" + name)), per)

        fb = [x.enter_context(nc.psum_tensor(f"a_front{k}", [P, TT], F32)) for k in range(4)]
        bb = [x.enter_context(nc.psum_tensor(f"a_back{k}", [P, TT], F32)) for k in range(4)]

        emb, h0, x1, xn = (sb(n, [P, SUB * D]) for n in ("emb", "h0", "x1", "xn"))
        fst, bst = sb("fst", [P, SUB, 6]), sb("bst", [P, SUB, 6])
        fmv, bmv = sb("fmv", [P, SUB, 2]), sb("bmv", [P, SUB, 2])
        frs, brs = sb("frs", [P, 2, SUB]), sb("brs", [P, 2, SUB])
        xf, xhi, xlo = sb("xf", [P, KC, TT]), sb("xhi", [P, KC, TT], BF16), sb("xlo", [P, KC, TT], BF16)
        ew, kw, ek, ev, num, den, tr = (sb(n, [P, KC, TT]) for n in ("ew", "kw", "ek", "ev", "num", "den", "tr"))
        z = ew
        zhi, zlo = sb("zhi", [P, KC, TT], BF16), sb("zlo", [P, KC, TT], BF16)
        x2, xn2, tr2, mix = (sb(n, [P, SUB * D]) for n in ("x2", "xn2", "tr2", "mix"))
        hs = xn2
        yf, yhi, ylo = sb("yf", [P, KC, TT]), sb("yhi", [P, KC, TT], BF16), sb("ylo", [P, KC, TT], BF16)
        u, sq = sb("u", [P, 2, TT]), sb("sq", [P, 2, TT])
        khi, klo = sb("khi", [P, HC0, TT], BF16), sb("klo", [P, HC0, TT], BF16)
        lg, ex, sel, wsel = (sb(n, [P, SUB, E0]) for n in ("lg", "ex", "sel", "wsel"))
        m8, rsum = sb("m8", [P, SUB, 8]), sb("rsum", [P, 2, SUB])
        wT = u[:, 0, :]
        xmf = yf

        emb_in = count("emb_in", 16 * SUB)
        emb_used = count("emb_used", 1)
        f_var, f_rstd = count("f_var", 2), count("f_rstd", 2)
        b_var, b_rstd = count("b_var", 2), count("b_rstd", 2)
        f_pool, b_pool = count("f_pool", 2), count("b_pool", 2)
        xn_ready, xnT = count("xn_ready", 1), count("xnT", KC)
        x_hi, x_lo = count("x_hi", KC), count("x_lo", KC)
        w_ps, k_ps, v_ps, r_ps = (count(n, KC) for n in ("w_ps", "k_ps", "v_ps", "r_ps"))
        ew_ready, kw_ready, ek_ready, ev_ready = (count(n, KC) for n in ("ew_ready", "kw_ready", "ek_ready", "ev_ready"))
        tr_ready, z_ready, z_hi, z_lo = (count(n, KC) for n in ("tr_ready", "z_ready", "z_hi", "z_lo"))
        o_ps, xn2_ready, xn2T = count("o_ps", 2), count("xn2_ready", 1), count("xn2T", KC)
        x2_ready = count("x2_ready", 2)
        y_hi, y_lo = count("y_hi", KC), count("y_lo", KC)
        rec_ps, tr2_ready = count("rec_ps", 2), count("tr2_ready", 2)
        up_ps, u_ready, sq_ready, k_hi, k_lo = (count(n, HC0) for n in ("up_ps", "u_ready", "sq_ready", "k_hi", "k_lo"))
        val_ps, val_used = count("val_ps", 1), count("val_used", 2)
        xm_ready, xmT, xm_f = count("xm_ready", 1), count("xmT", KC), count("xm_f", KC)
        lg_ps, lg_used, lg_shift, lg_exp = (count(n, 1) for n in ("lg_ps", "lg_used", "lg_shift", "lg_exp"))
        w_ready, wT_ps, wT_ready = (count(n, 1) for n in ("w_ready", "wT_ps", "wT_ready"))
        b2_ps, h_ready = count("b2_ps", 2), count("h_ready", 2)
        f_steps, b_steps = count("f_steps", KF), count("b_steps", KB)

        W = {n: (o, w) for n, (o, w) in OFF_A.items()}

        def wslice(part, name, kc, lo, n):
            o, w = W[name]
            return part[:, o + kc * w + lo:o + kc * w + lo + n]

        def braid(front, back):
            order = "b0 f0 b1 f1 b2 f2 b3 f3 b4 f4 b5 f5 b6 b7".split()
            for o in order:
                part = (front if o[0] == "f" else back)
                if part and int(o[1]) in part:
                    part[int(o[1])]()

        def run(eng, front, back):
            braid(front(0), None)
            braid(front(1), back(0))
            with eng.Fori(1, TILES - 1) as t:
                braid(front(t + 1), back(t))
            braid(None, back(TILES - 1))

        block = x.enter_context(nc.Block())

        @block.gpsimd
        def _(pool):
            def rstd(mv, rs, var, ready, own, t, n):
                pool.wait_ge(var.sem, var.at(t, n + 1))
                pool.tensor_tensor(rs[:, 0, :], mv[:, :, 1], c.eps[:, 0:SUB], ALU.add).then_inc(own.sem, 1)
                pool.wait_ge(own.sem, own.at(t, n + 1))
                pool.tensor_tensor(rs[:, 1, :], rs[:, 0, :], c.eps[:, 4:4 + SUB], ALU.pow).then_inc(ready.sem, 1)

            def gather(t):
                for s in range(SUB):
                    pool.indirect_dma_start(emb[:, s * D:(s + 1) * D], None, c.i["emb"],
                                            bass.IndirectOffsetOnAxis(ap=c.idx[:, s:s + 1].bitcast(U32), axis=0)
                                            ).then_inc(emb_in.sem, 16)

            def front(t):
                def f0():
                    if isinstance(t, int):
                        if t > 0:
                            pool.wait_ge(emb_used.sem, emb_used.at(t, 0))
                        pool.tensor_copy(c.idx[:, :], c.tok[:, t * SUB:(t + 1) * SUB]).then_inc(c.idx_ready, 1)
                        pool.wait_ge(c.idx_ready, t + 1)
                    else:
                        pool.wait_ge(emb_used.sem, emb_used.at(t, 0))
                        pool.tensor_tensor(c.idx[:, :], c.tok[:, bass.ds(t * SUB, SUB)],
                                           c.zero_i[:, :], ALU.add).then_inc(c.idx_ready, 1)
                        pool.wait_ge(c.idx_ready, t + 1)
                        pool.tensor_tensor(c.zero_j[:, :], c.zero_i[:, 0:1], c.zero_i[:, 0:1], ALU.add)
                    gather(t)
                    rstd(fmv, frs, f_var, f_rstd, f_pool, t, 0)
                    rstd(fmv, frs, f_var, f_rstd, f_pool, t, 1)

                def f1():
                    for k in range(KC):
                        pool.wait_ge(x_hi.sem, x_hi.at(t, k + 1))
                        pool.tensor_tensor(xlo[:, k, :], xf[:, k, :], xhi[:, k, :], ALU.subtract).then_inc(x_lo.sem, 1)

                def fz(k):
                    def f():
                        pool.wait_ge(z_hi.sem, z_hi.at(t, k + 1))
                        pool.tensor_tensor(zlo[:, k, :], z[:, k, :], zhi[:, k, :], ALU.subtract).then_inc(z_lo.sem, 1)
                    return f
                return {0: f0, 1: f1, 4: fz(0), 5: fz(1)}

            def back(t):
                def b0():
                    rstd(bmv, brs, b_var, b_rstd, b_pool, t, 0)

                def b1():
                    for k in range(KC):
                        pool.wait_ge(y_hi.sem, y_hi.at(t, k + 1))
                        pool.tensor_tensor(ylo[:, k, :], yf[:, k, :], yhi[:, k, :], ALU.subtract).then_inc(y_lo.sem, 1)

                def low(*ks):
                    def f():
                        for k in ks:
                            pool.wait_ge(sq_ready.sem, sq_ready.at(t, k + 1))
                            pool.wait_ge(k_hi.sem, k_hi.at(t, k + 1))
                            pool.tensor_tensor(klo[:, k, :], sq[:, k % 2, :], khi[:, k, :],
                                               ALU.subtract).then_inc(k_lo.sem, 1)
                    return f

                def b6():
                    rstd(bmv, brs, b_var, b_rstd, b_pool, t, 1)
                return {0: b0, 1: b1, 2: low(0, 1), 3: low(2, 3), 4: low(4, 5), 5: low(6, 7), 6: b6}
            run(pool, front, back)

        @block.scalar
        def _(act):
            def affine(src, f, hi, g, b, psum_ready, ready, low_done, t):
                for k in range(KC):
                    act.wait_ge(psum_ready.sem, psum_ready.at(t, k + 1))
                    act.wait_ge(low_done.sem, low_done.at(t, 0))
                    act.activation(f[:, k, :], src[k][:, :], ACT.Identity, bias=c.vec[:, b + k:b + k + 1],
                                   scale=c.vec[:, g + k:g + k + 1])
                    act.activation(hi[:, k, :], src[k][:, :], ACT.Identity, bias=c.vec[:, b + k:b + k + 1],
                                   scale=c.vec[:, g + k:g + k + 1]).then_inc(ready.sem, 1)

            def front(t):
                def f1():
                    affine(fb, xf, xhi, VEC["ln1_g"], VEC["ln1_b"], xnT, x_hi, x_lo, t)

                def exps(k):
                    def f():
                        act.wait_ge(w_ps.sem, w_ps.at(t, k + 1))
                        act.activation(ew[:, k, :], (fb[2], fb[1])[k][:, :], ACT.Exp).then_inc(ew_ready.sem, 1)
                        act.wait_ge(kw_ready.sem, kw_ready.at(t, k + 1))
                        act.activation(ek[:, k, :], kw[:, k, :], ACT.Exp).then_inc(ek_ready.sem, 1)
                    return f

                def fz(k):
                    def f():
                        if k == 0:
                            for j in range(KC):
                                act.wait_ge(r_ps.sem, r_ps.at(t, j + 1))
                                act.activation(tr[:, j, :], fb[j][:, :], ACT.Tanh, scale=0.5).then_inc(tr_ready.sem, 1)
                        act.wait_ge(z_ready.sem, z_ready.at(t, k + 1))
                        act.activation(zhi[:, k, :], z[:, k, :], ACT.Copy).then_inc(z_hi.sem, 1)
                    return f
                return {1: f1, 2: exps(0), 3: exps(1), 4: fz(0), 5: fz(1)}

            def back(t):
                def b1():
                    affine(bb[2:4], yf, yhi, VEC["ln2_g"], VEC["ln2_b"], xn2T, y_hi, y_lo, t)

                def relus(*ks):
                    def f():
                        if ks[0] == 0:
                            for j in range(2):
                                act.wait_ge(rec_ps.sem, rec_ps.at(t, j + 1))
                                act.activation(tr2[:, j * TT:(j + 1) * TT], bb[j][:, :], ACT.Tanh,
                                               scale=0.5).then_inc(tr2_ready.sem, 1)
                        for k in ks:
                            act.wait_ge(up_ps.sem, up_ps.at(t, k + 1))
                            act.wait_ge(sq_ready.sem, sq_ready.at(t, max(k - 1, 0)))
                            act.activation(u[:, k % 2, :], bb[2 + k % 2][:, :], ACT.Relu).then_inc(u_ready.sem, 1)
                            act.wait_ge(u_ready.sem, u_ready.at(t, k + 1))
                            act.activation(khi[:, k, :], u[:, k % 2, :], ACT.Square).then_inc(k_hi.sem, 1)
                    return f

                def b7():
                    for k in range(KC):
                        act.wait_ge(xmT.sem, xmT.at(t, k + 1))
                        act.activation(xmf[:, k, :], bb[2 + k][:, :], ACT.Copy)
                        act.activation(c.xT_hi[:, bass.ds(t * TT + k * N, TT)], bb[2 + k][:, :],
                                       ACT.Copy).then_inc(xm_f.sem, 1)
                    act.wait_ge(lg_shift.sem, lg_shift.at(t))
                    act.activation(ex[:, :, :], lg[:, :, :], ACT.Exp).then_inc(lg_exp.sem, 1)
                    act.wait_ge(wT_ps.sem, wT_ps.at(t))
                    act.activation(wT[0:E0, :], bb[1][0:E0, :], ACT.Copy).then_inc(wT_ready.sem, 1)
                return {1: b1, 2: relus(0, 1), 3: relus(2, 3), 4: relus(4, 5), 5: relus(6, 7), 7: b7}
            run(act, front, back)

        @block.vector
        def _(dve):
            F, B = Steps(dve, f_steps), Steps(dve, b_steps)

            def norm(S, src, dst, st, mv, rs, var, rstd, t, n, ready=None):
                S.settle()
                for s in range(SUB):
                    S.done(dve.bn_stats(st[:, s, :], src[:, s * D:(s + 1) * D]))
                S.settle()
                S.done(dve.tensor_copy(c.scr[:, 0:1], c.scr[:, 1:2]))
                for s in range(SUB):
                    i = dve.bn_aggr(mv[:, s, :], st[:, s, :])
                i.then_inc(var.sem, 1)
                dve.wait_ge(rstd.sem, rstd.at(t, n + 1))
                for s in range(SUB):
                    i = dve.tensor_scalar(dst[:, s * D:(s + 1) * D], src[:, s * D:(s + 1) * D], mv[:, s, 0:1],
                                          rs[:, 1, s:s + 1], ALU.subtract, ALU.mult)
                    if ready is None or s < SUB - 1:
                        S.done(i)
                if ready is not None:
                    i.then_inc(ready.sem, 1)

            def front(t):
                def f0():
                    F.begin(t)
                    dve.wait_ge(emb_in.sem, emb_in.at(t))
                    F.done(dve.tensor_scalar(h0[:, :], emb[:, :], EMB_SCALE, None, ALU.mult))
                    dve.tensor_scalar(c.h[:, bass.ds(t * SUB * D, SUB * D)], emb[:, :], EMB_SCALE, None,
                                      ALU.mult).then_inc(emb_used.sem, 1)
                    norm(F, h0, x1, fst, fmv, frs, f_var, f_rstd, t, 0)
                    norm(F, x1, xn, fst, fmv, frs, f_var, f_rstd, t, 1, xn_ready)

                def recur(k):
                    def f():
                        dve.wait_ge(ew_ready.sem, ew_ready.at(t, k + 1))
                        dve.wait_ge(k_ps.sem, k_ps.at(t, k + 1))
                        dve.tensor_tensor(kw[:, k, :], (fb[3], fb[2])[k][:, :], ew[:, k, :],
                                          ALU.subtract).then_inc(kw_ready.sem, 1)
                        dve.wait_ge(ek_ready.sem, ek_ready.at(t, k + 1))
                        dve.wait_ge(v_ps.sem, v_ps.at(t, k + 1))
                        dve.tensor_tensor(ev[:, k, :], (fb[0], fb[3])[k][:, :], ek[:, k, :],
                                          ALU.mult).then_inc(ev_ready.sem, 1)
                        decay = c.dec[:, k:k + 1].to_broadcast([P, SEQ])
                        for b in range(SEQS):
                            q = slice(b * SEQ, (b + 1) * SEQ)
                            F.done(dve.tensor_tensor_scan(den[:, k, q], decay, ek[:, k, q], 0.0, ALU.mult, ALU.add))
                        dve.wait_ge(ev_ready.sem, ev_ready.at(t, k + 1))
                        for b in range(SEQS):
                            q = slice(b * SEQ, (b + 1) * SEQ)
                            F.done(dve.tensor_tensor_scan(num[:, k, q], decay, ev[:, k, q], 0.0, ALU.mult, ALU.add))
                        F.settle()
                        F.done(dve.tensor_scalar(ew[:, k, :], den[:, k, :], 2.0, 2 * WKV_EPS, ALU.mult, ALU.add))
                    return f

                def fz(k):
                    def f():
                        F.settle()
                        F.done(dve.reciprocal(den[:, k, :], ew[:, k, :]))
                        F.settle()
                        F.done(dve.tensor_tensor(kw[:, k, :], num[:, k, :], den[:, k, :], ALU.mult))
                        F.settle()
                        dve.wait_ge(tr_ready.sem, tr_ready.at(t, k + 1))
                        dve.scalar_tensor_tensor(z[:, k, :], tr[:, k, :], 1.0, kw[:, k, :], ALU.add,
                                                 ALU.mult).then_inc(z_ready.sem, 1)
                        if k == KC - 1:
                            F.end()
                    return f
                return {0: f0, 2: recur(0), 3: recur(1), 4: fz(0), 5: fz(1)}

            def back(t):
                def b0():
                    B.begin(t)
                    for j in range(2):
                        q = slice(j * TT, (j + 1) * TT)
                        dve.wait_ge(o_ps.sem, o_ps.at(t, j + 1))
                        dve.tensor_tensor(x2[:, q], x1[:, q], bb[j][:, :], ALU.add).then_inc(x2_ready.sem, 1)
                    dve.wait_ge(x2_ready.sem, x2_ready.at(t))
                    norm(B, x2, xn2, bst, bmv, brs, b_var, b_rstd, t, 0, xn2_ready)

                def squares(*ks):
                    def f():
                        for k in ks:
                            dve.wait_ge(u_ready.sem, u_ready.at(t, k + 1))
                            dve.wait_ge(k_lo.sem, k_lo.at(t, max(k - 1, 0)))
                            dve.tensor_tensor(sq[:, k % 2, :], u[:, k % 2, :], u[:, k % 2, :],
                                              ALU.mult).then_inc(sq_ready.sem, 1)
                    return f

                def b6():
                    dve.wait_ge(tr2_ready.sem, tr2_ready.at(t))
                    dve.wait_ge(val_ps.sem, val_ps.at(t))
                    for j in range(2):
                        q = slice(j * TT, (j + 1) * TT)
                        dve.scalar_tensor_tensor(mix[:, q], tr2[:, q], 1.0, bb[j][:, :], ALU.add,
                                                 ALU.mult).then_inc(val_used.sem, 1)
                    dve.wait_ge(val_used.sem, val_used.at(t))
                    B.done(dve.scalar_tensor_tensor(hs[:, :], mix[:, :], 0.5, x2[:, :], ALU.mult, ALU.add))
                    B.settle()
                    B.done(dve.tensor_tensor(hs[:, :], hs[:, :], c.h[:, bass.ds(t * SUB * D, SUB * D)], ALU.add))
                    norm(B, hs, mix, bst, bmv, brs, b_var, b_rstd, t, 1, xm_ready)

                def b7():
                    for k in range(KC):
                        at = bass.ds(t * TT + k * N, TT)
                        dve.wait_ge(xm_f.sem, xm_f.at(t, k + 1))
                        B.done(dve.tensor_tensor(c.xT_lo[:, at], xmf[:, k, :], c.xT_hi[:, at], ALU.subtract))
                    dve.wait_ge(lg_ps.sem, lg_ps.at(t))
                    dve.tensor_copy(lg[:, :, :], bb[0][:, 0:SUB * E0].rearrange("p (s e) -> p s e", s=SUB)
                                    ).then_inc(lg_used.sem, 1)
                    dve.wait_ge(lg_used.sem, lg_used.at(t))
                    B.done(dve.tensor_copy(c.scr[:, 0:1], c.scr[:, 1:2]))
                    for s in range(SUB):
                        B.done(dve.max(m8[:, s, :], lg[:, s, :]))
                    B.settle()
                    B.done(dve.tensor_tensor(sel[:, :, :], lg[:, :, :], m8[:, :, 1:2].to_broadcast([P, SUB, E0]),
                                             ALU.is_ge))
                    B.settle()
                    dve.tensor_tensor(lg[:, :, :], lg[:, :, :], m8[:, :, 0:1].to_broadcast([P, SUB, E0]),
                                      ALU.subtract).then_inc(lg_shift.sem, 1)
                    dve.wait_ge(lg_exp.sem, lg_exp.at(t))
                    B.done(dve.tensor_tensor(sel[:, :, :], ex[:, :, :], sel[:, :, :], ALU.mult))
                    B.settle()
                    B.done(dve.tensor_reduce(rsum[:, 0, :], sel[:, :, :], AX.X, ALU.add))
                    B.settle()
                    B.done(dve.reciprocal(rsum[:, 1, :], rsum[:, 0, :]))
                    B.settle()
                    weights = rsum[:, 1, :].unsqueeze(2).to_broadcast([P, SUB, E0])
                    dve.tensor_tensor(wsel[:, :, :], sel[:, :, :], weights, ALU.mult).then_inc(w_ready.sem, 1)
                    dve.wait_ge(w_ready.sem, w_ready.at(t))
                    B.done(dve.tensor_copy(c.w0[:, bass.ds(t * SUB * E0, SUB * E0)],
                                           wsel[:, :, :].rearrange("p s e -> p (s e)")))
                    for j in range(2):
                        dve.wait_ge(b2_ps.sem, b2_ps.at(t, j + 1))
                        dve.tensor_tensor(c.h[:, bass.ds(t * SUB * D + j * TT, TT)], hs[:, j * TT:(j + 1) * TT],
                                          bb[2 + j][:, :], ALU.add).then_inc(h_ready.sem, 1)
                    B.end()
                return {0: b0, 2: squares(0, 1), 3: squares(2, 3), 4: squares(4, 5), 5: squares(6, 7), 6: b6, 7: b7}
            run(dve, front, back)

        @block.tensor
        def _(pe):
            def feature_major(out, name, e, hi, lo, ready, lo_sem, lo_at):
                cols = e * P
                for j, (wp, xp) in enumerate(((c.WA_hi, hi), (c.WA_lo, hi), (c.WA_hi, lo))):
                    if j == 2 and lo_sem is not None:
                        pe.wait_ge(lo_sem, lo_at)
                    for k in range(KC):
                        m = pe.matmul(out[:, :], wslice(wp, name, k, cols, P), xp[:, k, :],
                                      start=(j == 0 and k == 0), stop=(j == 2 and k == KC - 1))
                m.then_inc(ready.sem, 1)

            def token_major(out, name, s, hi, lo):
                for j, (wp, xp) in enumerate(((c.WA_hi, hi), (c.WA_lo, hi), (c.WA_hi, lo))):
                    for k in range(KC):
                        m = pe.matmul(out, xp[:, k, s * P:(s + 1) * P], wslice(wp, name, k, 0, D),
                                      start=(j == 0 and k == 0), stop=(j == 2 and k == KC - 1))
                return m

            def transposes(src, banks, ready):
                for k in range(KC):
                    for s in range(SUB):
                        m = pe.transpose(banks[k][:, s * P:(s + 1) * P], src[:, s * D + k * P:s * D + (k + 1) * P],
                                         c.ident[:, :])
                    m.then_inc(ready.sem, 1)

            def front(t):
                def f1():
                    pe.wait_ge(xn_ready.sem, xn_ready.at(t))
                    pe.wait_ge(tr_ready.sem, tr_ready.at(t, 0))
                    transposes(xn, fb, xnT)

                def f2():
                    pe.wait_ge(x_hi.sem, x_hi.at(t))
                    pe.wait_ge(kw_ready.sem, kw_ready.at(t, 0))
                    feature_major(fb[2], "Ww", 0, xhi, xlo, w_ps, x_lo.sem, x_lo.at(t))
                    pe.wait_ge(ev_ready.sem, ev_ready.at(t, 0))
                    feature_major(fb[3], "Wk", 0, xhi, xlo, k_ps, None, None)
                    feature_major(fb[0], "Wv", 0, xhi, xlo, v_ps, None, None)

                def f3():
                    feature_major(fb[1], "Ww", 1, xhi, xlo, w_ps, None, None)
                    pe.wait_ge(ew_ready.sem, ew_ready.at(t, 1))
                    feature_major(fb[2], "Wk", 1, xhi, xlo, k_ps, None, None)
                    pe.wait_ge(kw_ready.sem, kw_ready.at(t, 1))
                    feature_major(fb[3], "Wv", 1, xhi, xlo, v_ps, None, None)

                def f4():
                    pe.wait_ge(ev_ready.sem, ev_ready.at(t, 1))
                    feature_major(fb[0], "Wr", 0, xhi, xlo, r_ps, None, None)
                    pe.wait_ge(ew_ready.sem, ew_ready.at(t, 2))
                    feature_major(fb[1], "Wr", 1, xhi, xlo, r_ps, None, None)
                return {1: f1, 2: f2, 3: f3, 4: f4}

            def back(t):
                def b0():
                    pe.wait_ge(z_lo.sem, z_lo.at(t))
                    pe.wait_ge(z_hi.sem, z_hi.at(t))
                    pe.wait_ge(lg_used.sem, lg_used.at(t, 0))
                    pe.wait_ge(wT_ready.sem, wT_ready.at(t, 0))
                    for s in range(SUB):
                        m = token_major(bb[s // 2][:, (s % 2) * D:(s % 2 + 1) * D], "Wo", s, zhi, zlo)
                        if s % 2:
                            m.then_inc(o_ps.sem, 1)

                def b1():
                    pe.wait_ge(xn2_ready.sem, xn2_ready.at(t))
                    pe.wait_ge(h_ready.sem, h_ready.at(t, 0))
                    transposes(xn2, bb[2:4], xn2T)

                def up(k):
                    if k >= 2:
                        pe.wait_ge(u_ready.sem, u_ready.at(t, k - 1))
                    feature_major(bb[2 + k % 2], "Wkey", k, yhi, ylo, up_ps, None, None)

                def down(k):
                    if k == 0:
                        pe.wait_ge(tr2_ready.sem, tr2_ready.at(t))
                    pe.wait_ge(k_hi.sem, k_hi.at(t, k + 1))
                    pe.wait_ge(k_lo.sem, k_lo.at(t, k + 1))
                    o, w = W["Wval"]
                    for s in range(SUB):
                        for j, (wp, xp) in enumerate(((c.WA_hi, khi), (c.WA_lo, khi), (c.WA_hi, klo))):
                            m = pe.matmul(bb[s // 2][:, (s % 2) * D:(s % 2 + 1) * D], xp[:, k, s * P:(s + 1) * P],
                                          wp[:, o + k * w:o + (k + 1) * w],
                                          start=(k == 0 and j == 0 and s % 2 == 0), stop=(k == HC0 - 1 and j == 2),
                                          skip_group_check=True)
                    if k == HC0 - 1:
                        m.then_inc(val_ps.sem, 1)

                def b2():
                    pe.wait_ge(y_hi.sem, y_hi.at(t))
                    pe.wait_ge(y_lo.sem, y_lo.at(t))
                    pe.wait_ge(x2_ready.sem, x2_ready.at(t))
                    for s in range(SUB):
                        m = token_major(bb[s // 2][:, (s % 2) * D:(s % 2 + 1) * D], "Wrec", s, yhi, ylo)
                        if s % 2:
                            m.then_inc(rec_ps.sem, 1)
                    up(0)
                    up(1)

                def pairs(k):
                    def f():
                        down(k)
                        up(k + 2)
                        down(k + 1)
                        up(k + 3)
                    return f

                def b6():
                    down(6)
                    down(7)

                def b7():
                    pe.wait_ge(xm_ready.sem, xm_ready.at(t))
                    pe.wait_ge(u_ready.sem, u_ready.at(t))
                    transposes(mix, bb[2:4], xmT)
                    pe.wait_ge(xm_f.sem, xm_f.at(t))
                    for s in range(SUB):
                        out = bb[0][:, s * E0:(s + 1) * E0]
                        for k in range(KC):
                            pe.matmul(out, xmf[:, k, s * P:(s + 1) * P], c.Wrt[:, k * E0:(k + 1) * E0],
                                      start=(k == 0), stop=False)
                        m = pe.matmul(out, c.ones[0:1, :], c.br[0:1, :], start=False, stop=True)
                    m.then_inc(lg_ps.sem, 1)
                    pe.wait_ge(w_ready.sem, w_ready.at(t))
                    for s in range(SUB):
                        m = pe.transpose(bb[1][0:E0, s * P:(s + 1) * P], wsel[:, s, :], c.ident[:, :])
                    m.then_inc(wT_ps.sem, 1)
                    pe.wait_ge(wT_ready.sem, wT_ready.at(t))
                    for s in range(SUB):
                        m = pe.matmul(bb[2 + s // 2][:, (s % 2) * D:(s % 2 + 1) * D], wT[0:E0, s * P:(s + 1) * P],
                                      c.b2[0:E0, :], start=True, stop=True)
                        if s % 2:
                            m.then_inc(b2_ps.sem, 1)
                return {0: b0, 1: b1, 2: b2, 3: pairs(0), 4: pairs(2), 5: pairs(4), 6: b6, 7: b7}
            run(pe, front, back)


def phase_b(nc, c):
    with ExitStack() as x:
        def sb(name, shape, dt=F32):
            return x.enter_context(nc.sbuf_tensor("b_" + name, shape, dt))

        def count(name, per, base=0):
            return Count(x.enter_context(nc.semaphore("b_" + name)), per, base)

        ub = [x.enter_context(nc.psum_tensor(f"b_up{k}", [P, TT], F32)) for k in range(4)]
        ob = [x.enter_context(nc.psum_tensor(f"b_down{k}", [P, TT], F32)) for k in range(2)]
        W_hi, W_lo = ([sb(f"{n}{p}", [P, COLS_E], BF16) for p in range(2)] for n in ("W_hi", "W_lo"))
        stage = [sb(f"stage{j}", [P, PIECE_E + PIECE_C]) for j in range(2)]
        b1 = [sb(f"b1_{p}", [P, HC0]) for p in range(2)]
        f = sb("f", [P, 4, TT])
        ghi, glo = sb("ghi", [P, HC0, TT], BF16), sb("glo", [P, HC0, TT], BF16)

        up_ps, g_hi, g_lo = count("up_ps", HC0), count("g_hi", HC0), count("g_lo", HC0, 1)
        out_ps, out_used = count("out_ps", 1), count("out_used", SUB, 1)
        landed = [count(f"landed{j}", 16) for j in range(2)]
        w_hi, w_lo = count("w_hi", 1), count("w_lo", 1)
        b1_ready = count("b1_ready", 1)

        def run(eng, step, begin=None, last_begin=None):
            def expert(e, par, more):
                if begin:
                    begin(e, par)
                with eng.Fori(0, TILES // 2) as tp:
                    for j in range(2):
                        step(e, par, tp, j, more)
            with eng.Fori(0, E0 // 2 - 1) as pair:
                expert(pair * 2, 0, True)
                expert(pair * 2 + 1, 1, True)
            expert(E0 - 2, 0, True)
            expert(E0 - 1, 1, False)

        def split_at(piece):
            return piece * PIECE_E, piece * PIECE_C

        block = x.enter_context(nc.Block())

        @block.sync
        def _(sp):
            for p in range(TILES):
                if p >= 2:
                    sp.wait_ge(w_lo.sem, p - 1)
                sp.dma_start(stage[p % 2][:, :], c.i["WP"][p, :, :]).then_inc(landed[p % 2].sem, 16)

            def step(e, par, tp, j, more):
                if more:
                    g = e * TILES + tp * 2 + (TILES + j)
                    sp.wait_ge(w_lo.sem, g - 1)
                    sp.dma_start(stage[j][:, :], c.i["WP"][bass.ds(g, 1), :, :].rearrange("g p n -> (g p) n")
                                 ).then_inc(landed[j].sem, 16)
            run(sp, step)

        @block.scalar
        def _(act):
            def high(buf, j, piece, piece_c):
                act.activation(c.WC_hi[:, bass.ds(piece_c * PIECE_C, PIECE_C)], stage[j][:, PIECE_E:], ACT.Copy)
                act.activation(buf[:, bass.ds(piece * PIECE_E, PIECE_E)], stage[j][:, 0:PIECE_E],
                               ACT.Copy).then_inc(w_hi.sem, 1)
            for p in range(TILES):
                act.wait_ge(landed[p % 2].sem, 16 * (p // 2 + 1))
                high(W_hi[0], p % 2, p, p)

            def step(e, par, tp, j, more):
                g = e * TILES + tp * 2 + j
                for k in range(HC0):
                    act.wait_ge(up_ps.sem, up_ps.at(g, k + 1))
                    if k == 0 and j == 0:
                        act.wait_ge(b1_ready.sem, e + 1)
                    act.wait_ge(g_lo.sem, g_lo.at(g, max(k - 3, 0)))
                    if k == HC0 - 1 and more:
                        act.wait_ge(landed[j].sem, (e * (TILES // 2) + tp + (TILES // 2 + 1)) * 16)
                    act.activation(f[:, k % 4, :], ub[k % 4][:, :], ACT.Gelu, bias=b1[par][:, k:k + 1])
                    act.activation(ghi[:, k, :], ub[k % 4][:, :], ACT.Gelu,
                                   bias=b1[par][:, k:k + 1]).then_inc(g_hi.sem, 1)
                if more:
                    high(W_hi[1 - par], j, tp * 2 + j, g + TILES)
            run(act, step)

        @block.vector
        def _(dve):
            def low(hi, lo, j, piece, piece_c):
                q = bass.ds(piece_c * PIECE_C, PIECE_C)
                dve.tensor_tensor(c.WC_lo[:, q], stage[j][:, PIECE_E:], c.WC_hi[:, q], ALU.subtract)
                q = bass.ds(piece * PIECE_E, PIECE_E)
                dve.tensor_tensor(lo[:, q], stage[j][:, 0:PIECE_E], hi[:, q], ALU.subtract).then_inc(w_lo.sem, 1)
            dve.memset(c.scr[:, 0:1], 0.0).then_inc(g_lo.sem, 1)
            dve.memset(c.scr[:, 1:2], 0.0).then_inc(out_used.sem, 1)
            for p in range(TILES):
                dve.wait_ge(w_hi.sem, p + 1)
                low(W_hi[0], W_lo[0], p % 2, p, p)

            def begin(e, par):
                dve.tensor_copy(b1[par][:, :], c.b1[:, bass.ds(e * HC0, HC0)]).then_inc(b1_ready.sem, 1)

            def step(e, par, tp, j, more):
                g = e * TILES + tp * 2 + j
                t = tp * 2 + j
                for k in range(HC0):
                    dve.wait_ge(g_hi.sem, g_hi.at(g, k + 1))
                    dve.tensor_tensor(glo[:, k, :], f[:, k % 4, :], ghi[:, k, :], ALU.subtract).then_inc(g_lo.sem, 1)
                if more:
                    dve.wait_ge(w_hi.sem, g + (TILES + 1))
                    low(W_hi[1 - par], W_lo[1 - par], j, tp * 2 + j, g + TILES)
                dve.wait_ge(out_ps.sem, out_ps.at(g))
                dve.wait_ge(out_used.sem, out_used.at(g, 0))
                for s in range(SUB):
                    at = bass.ds((t * SUB + s) * D, D)
                    dve.scalar_tensor_tensor(c.h[:, at], ob[s // 2][:, (s % 2) * D:(s % 2 + 1) * D],
                                             c.w0[:, bass.ds((t * SUB + s) * E0 + e, 1)], c.h[:, at],
                                             ALU.mult, ALU.add).then_inc(out_used.sem, 1)
            run(dve, step, begin)

        @block.tensor
        def _(pe):
            def step(e, par, tp, j, more):
                g = e * TILES + tp * 2 + j
                t = tp * 2 + j

                def up(k):
                    for n, (wp, xp) in enumerate(((W_hi, c.xT_hi), (W_lo, c.xT_hi), (W_hi, c.xT_lo))):
                        for q in range(KC):
                            m = pe.matmul(ub[k % 4][:, :], wp[par][:, q * H0 + k * P:q * H0 + (k + 1) * P],
                                          xp[:, bass.ds(t * TT + q * N, TT)], start=(n == 0 and q == 0),
                                          stop=(n == 2 and q == KC - 1))
                    m.then_inc(up_ps.sem, 1)

                def down(k):
                    pe.wait_ge(g_hi.sem, g_hi.at(g, k + 1))
                    pe.wait_ge(g_lo.sem, g_lo.at(g, k + 1))
                    if k == 0:
                        pe.wait_ge(out_used.sem, out_used.at(g, 0))
                    w = slice(KC * H0 + k * D, KC * H0 + (k + 1) * D)
                    for s in range(SUB):
                        for n, (wp, xp) in enumerate(((W_hi, ghi), (W_lo, ghi), (W_hi, glo))):
                            m = pe.matmul(ob[s // 2][:, (s % 2) * D:(s % 2 + 1) * D], xp[:, k, s * P:(s + 1) * P],
                                          wp[par][:, w], start=(k == 0 and n == 0 and s % 2 == 0),
                                          stop=(k == HC0 - 1 and n == 2), skip_group_check=True)
                    if k == HC0 - 1:
                        m.then_inc(out_ps.sem, 1)
                pe.wait_ge(w_lo.sem, (e + 1) * TILES)
                up(0)
                up(1)
                for k in range(2, HC0):
                    up(k)
                    down(k - 2)
                down(HC0 - 2)
                down(HC0 - 1)
            run(pe, step)


def heads_order(b, fill):
    steps = []
    for h in range(HEADS):
        steps.append("S%d" % (b * HEADS + h))
        if h >= 2:
            steps.append("V%d" % (b * HEADS + h - 2))
        if h in fill:
            steps.append(str(fill[h]))
    return " ".join(steps + ["V%d" % (b * HEADS + h) for h in (HEADS - 2, HEADS - 1)])


ORDER_C = " ".join((
    "b0 f0 b1 f1 1 f2 A0 3 R0 A1 4 Z0 R1 4 Z1 f5 6 f6 1 Q0 Q1 4 K0 T0 2 K1 T1 1 M0 N0",
    heads_order(0, {3: 1, 7: 1, 11: 1, 15: 1}), "O0",
    "Q2 Q3 2 K2 T2 2 K3 T3 M1 N1",
    heads_order(1, {1: 1, 3: 1, 5: 1, 7: 1, 9: 1, 11: 1, 13: 1, 15: 1}), "O1 f13"))


def phase_c(nc, c, out):
    KF, KB = 94, 28
    PB = 4
    VW = HD + 1
    with ExitStack() as x:
        def sb(name, shape, dt=F32):
            return x.enter_context(nc.sbuf_tensor("c_" + name, shape, dt))

        def count(name, per):
            return Count(x.enter_context(nc.semaphore("c_" + name)), per)

        fb = [x.enter_context(nc.psum_tensor(f"c_front{k}", [P, TT], F32)) for k in range(4)]
        bb = [x.enter_context(nc.psum_tensor(f"c_back{k}", [P, TT], F32)) for k in range(4)]

        room = [c.xT_hi[:, :].bitcast(F32), c.xT_lo[:, :].bitcast(F32)]
        at = [0, 0]

        def reuse(n, which):
            at[which] += n
            assert at[which] <= KC * N // 2
            return room[which][:, at[which] - n:at[which]]

        h2 = sb("h2", [P, SUB * D])
        xn = sb("xn", [P, SUB * D])
        fst, fmv, frs = sb("fst", [P, SUB, 6]), sb("fmv", [P, SUB, 2]), sb("frs", [P, 5, SUB])
        bst, bmv, brs = sb("bst", [P, SUB, 6]), sb("bmv", [P, SUB, 2]), sb("brs", [P, 2, SUB])
        xf = reuse(KC * TT, 0).rearrange("p (k n) -> p k n", k=KC)
        xhi, xlo = sb("xhi", [P, KC, TT], BF16), sb("xlo", [P, KC, TT], BF16)
        kk, vv, tr = (reuse(KC * TT, 0).rearrange("p (k n) -> p k n", k=KC) for _ in range(3))
        T = reuse(5 * TT, 1).rearrange("p (k n) -> p k n", k=5)
        z = reuse(TT, 1)
        pp, av, bv = (sb(n, [P, SEQS, SEQ + 1]) for n in ("pp", "av", "bv"))
        qkr, qsq = (z, reuse(TT, 1)), reuse(TT, 1)
        T_ = T.rearrange("p k n -> p (k n)")
        used = [0]

        def in_T(n):
            used[0] += n
            assert used[0] <= 5 * TT
            return T_[:, used[0] - n:used[0]]
        vf = in_T(D)
        ss, ms, qrs = (sb(n, [P, 2, 2 * HEADS]) for n in ("ss", "ms", "qrs"))
        qs, ks = sb("qs", [P, HEADS, 64], BF16), sb("ks", [P, HEADS, 64], BF16)
        qT, kT = (a.rearrange("p k n -> p (k n)").bitcast(BF16).rearrange("p (h n) -> p h n", h=HEADS // 2)
                  for a in (kk, vv))
        vh, vl = sb("vh", [P, 2, HEADS, VW], BF16), sb("vl", [P, 2, HEADS, HD], BF16)
        mx, mr = sb("mx", [P, 2, HEADS]), sb("mr", [P, 2, 2, HEADS])
        nstack, negT = sb("nstack", [P, 2, P], BF16), sb("negT", [P, SEQ], BF16)
        npart = nstack[:, :, 0:3 * HEADS].rearrange("p q (h a) -> p q h a", h=HEADS)
        pf = in_T(PB * 3 * P).rearrange("p (b n) -> p b n", b=PB)
        ph, pl = (a.rearrange("p k n -> p (k n)").bitcast(BF16)[:, 0:PB * 3 * P].rearrange("p (b n) -> p b n", b=PB)
                  for a in (tr, xf))
        ou = in_T(2 * HEADS * VW).rearrange("p (q h d) -> p q h d", q=2, h=HEADS)
        den = sb("den", [P, 2, HEADS])
        yn, yf = sb("yn", [P, SUB * D]), sb("yf", [P, KC, TT])
        yhi, ylo = sb("yhi", [P, KC, TT], BF16), sb("ylo", [P, KC, TT], BF16)
        hid_hi = [sb(f"hid_hi{n}", [P, HID // P, TT], BF16) for n in range(3)]
        hid_lo = [sb(f"hid_lo{n}", [P, HID // P, TT], BF16) for n in range(3)]
        g = sb("g", [P, 2, TT])
        sl, sl2 = sb("sl", [P, TT]), sb("sl2", [P, TT])
        lg, pr, wt = (sb(n, [P, SUB, E1]) for n in ("lg", "pr", "wt"))
        gt, eq = sb("gt", [P, SUB, E1, E1]), sb("eq", [P, SUB, E1, E1])
        r1 = sb("r1", [P, 4, SUB])
        below = sb("below", [P, E1, E1])

        f_var, f_rstd, f_pool = count("f_var", 2), count("f_rstd", 2), count("f_pool", 6)
        b_var, b_rstd, b_pool = count("b_var", 1), count("b_rstd", 1), count("b_pool", 3)
        xn_ready, xnT, x_hi, x_lo = count("xn_ready", 3), count("xnT", 3 * KC), count("x_hi", 3 * KC), count("x_lo", 3 * KC)
        k_ps, r_ps, kv_ready, tr_ready = (count(n, KC) for n in ("k_ps", "r_ps", "kv_ready", "tr_ready"))
        arg_ready, exp_ready, z_ready, z_hi, z_lo = (count(n, KC) for n in ("arg_ready", "exp_ready", "z_ready", "z_hi", "z_lo"))
        o_ps, h2_ready = count("o_ps", 2), count("h2_ready", 2)
        qk_ps, v_ps, qk_sq, v_hi, v_lo, ss_ready, q_rstd, _, q_stack, k_stack = (
            count(n, SUB * m) for n, m in (("qk_ps", 1), ("v_ps", 1), ("qk_sq", 1), ("v_hi", 1), ("v_lo", 1),
                                           ("ss_ready", 1), ("q_rstd", 1), ("q_pool", 0), ("q_stack", 1), ("k_stack", 1)))
        qkT_ps, qkT_ready = count("qkT_ps", 2 * SUB), count("qkT_ready", 2 * SUB)
        S_ps, mx_ready = count("S_ps", 12 * SEQS), count("mx_ready", 12 * SEQS)
        np_ready, negT_ps, negT_ready = (count(n, SEQS) for n in ("np_ready", "negT_ps", "negT_ready"))
        P_ps, p_f, p_hi, p_lo, pv_ps = (count(n, HEADS * SEQS) for n in ("P_ps", "p_f", "p_hi", "p_lo", "pv_ps"))
        ou_ready = count("ou_ready", 2 * SEQS)
        ao_ps, h3_ready = count("ao_ps", 2), count("h3_ready", 1)
        yn_ready, ynT, y_hi, y_lo = count("yn_ready", 1), count("ynT", KC), count("y_hi", KC), count("y_lo", KC)
        lg_ps, lg_ready, lg_shift, lg_exp = (count(n, 1) for n in ("lg_ps", "lg_ready", "lg_shift", "lg_exp"))
        f_steps, b_steps = count("f_steps", KF), count("b_steps", KB)
        stored, set_up = count("stored", 16), count("set_up", 1)

        HC = HID // P
        UPS = {}
        for n, (name, src, ks_, dst, cs) in enumerate((
                ("e2_l1", None, KC, 0, HC), ("e0_up", None, KC, 2, HC), ("e2_l2", 0, HC, 1, HC),
                ("e2_l3", 1, HC, 0, HC), ("e3_down", None, KC, 2, KC), ("e3_up", 2, KC, 1, HC))):
            UPS[name] = (src, ks_, dst, cs)
        WORK = [("up", "e2_l1"), ("up", "e0_up"), ("up", "e2_l2"), ("down", "e0_down", 0, 2),
                ("up", "e2_l3"), ("up", "e3_down"), ("up", "e3_up"), ("down", "e2_l4", 2, 0),
                ("gated", None), ("down", "e3_out", 3, 1), ("down", "e1_down", 1, 0)]
        first_up, first_hid, first_down, nu, nh, nd = {}, {}, {}, 0, 0, 0
        hid_of = {}
        for w in WORK:
            if w[0] == "up":
                first_up[w[1]], first_hid[w[1]] = nu, nh
                nu, nh = nu + UPS[w[1]][3], nh + UPS[w[1]][3]
            elif w[0] == "gated":
                first_up["e1"], first_hid["e1"] = nu, nh
                nu, nh = nu + 2 * HC, nh + HC
            else:
                first_down[w[1]] = nd
                nd += 1
        NU, NH, ND = nu, nh, nd
        assert NU % 2 == 0
        maker = {"e0_down": "e0_up", "e2_l4": "e2_l3", "e3_out": "e3_up", "e1_down": "e1",
                 "e2_l2": "e2_l1", "e2_l3": "e2_l2", "e3_up": "e3_down"}
        up_ps = count("up_ps", NU)
        gate_th, gate_sl = count("gate_th", HC), count("gate_sl", HC)
        hi_ready, lo_ready = count("hi_ready", NH), count("lo_ready", NH)
        down_ps, down_used = count("down_ps", ND), count("down_used", ND * SUB)

        CHUNKS = [(w, k) for w in WORK for k in range(UPS[w[1]][3] if w[0] == "up" else HC)]

        def chunks(up=None, gated=None, down=None):
            steps = {}
            for n, (w, k) in enumerate(CHUNKS):
                if w[0] == "up" and up:
                    steps["w%d" % n] = lambda w=w, k=k: up(w[1], k)
                elif w[0] == "gated" and gated:
                    steps["w%d" % n] = lambda k=k: gated(k)
                elif w[0] == "down" and down:
                    steps["w%d" % n] = lambda w=w, k=k: down(*w[1:], k)
            return steps

        order = ORDER_C.split()
        assert sum(int(o) for o in order if o.isdigit()) == len(CHUNKS), len(CHUNKS)
        ORDER, n = [], 0
        for o in order:
            if o.isdigit():
                ORDER += ["w%d" % (n + j) for j in range(int(o))]
                n += int(o)
            else:
                ORDER.append(o)

        def braid(front, back):
            for o in ORDER:
                for part in (front, back):
                    if o in part:
                        part[o]()

        def run(eng, front, back):
            braid(front(0), {})
            braid(front(1), back(0))
            with eng.Fori(1, TILES - 1) as t:
                braid(front(t + 1), back(t))
            braid({}, back(TILES - 1))

        def group(n):
            if n < 8:
                return [4 * (n // 2) + n % 2 + 2 * j for j in range(2)]
            return [8 * ((n - 8) // 2) + n % 2 + 2 * j for j in range(4)]

        def W(part, name, k, lo, n):
            o, w = OFF_C[name]
            return part[:, o + k * w + lo:o + k * w + lo + n]

        block = x.enter_context(nc.Block())

        @block.sync
        def _(sp):
            with sp.Fori(0, TILES) as t:
                sp.wait_ge(down_used.sem, down_used.at(t))
                sp.dma_start(out[bass.ds(t * TT, TT), :].rearrange("(s p) d -> p s d", p=P),
                             c.h[:, bass.ds(t * SUB * D, SUB * D)].rearrange("p (s d) -> p s d", s=SUB)
                             ).then_inc(stored.sem, 16)
            sp.wait_ge(stored.sem, 16 * TILES)

        @block.gpsimd
        def _(pool):
            def rstd(mv, rs, var, ready, own, t, n, m, centred):
                pool.wait_ge(var.sem, var.at(t, n + 1))
                v = mv[:, :, 1]
                if not centred:
                    pool.tensor_tensor(rs[:, 0, :], mv[:, :, 0], mv[:, :, 0], ALU.mult).then_inc(own.sem, 1)
                    pool.wait_ge(own.sem, own.at(t, m + 1))
                    pool.tensor_tensor(rs[:, 1, :], rs[:, 0, :], v, ALU.add).then_inc(own.sem, 1)
                    pool.wait_ge(own.sem, own.at(t, m + 2))
                    v, m = rs[:, 1, :], m + 2
                pool.tensor_tensor(rs[:, 0, :], v, c.eps[:, 0:SUB] if centred else c.eps[:, 8:8 + SUB],
                                   ALU.add).then_inc(own.sem, 1)
                pool.wait_ge(own.sem, own.at(t, m + 1))
                pool.tensor_tensor(rs[:, 1, :], rs[:, 0, :], c.eps[:, 4:4 + SUB], ALU.pow).then_inc(ready.sem, 1)

            def front(t):
                def both_norms():
                    v, a, r1, b_, d_, r2 = (fmv[:, :, 1],) + tuple(frs[:, k, :] for k in range(5))
                    steps = ((a, v, c.eps[:, 0:SUB], ALU.add), (r1, a, c.eps[:, 4:4 + SUB], ALU.pow),
                             (b_, r1, r1, ALU.mult), (d_, b_, v, ALU.mult), (a, d_, c.eps[:, 8:8 + SUB], ALU.add))
                    pool.wait_ge(f_var.sem, f_var.at(t, 2))
                    for k, (o, p_, q, op) in enumerate(steps):
                        pool.tensor_tensor(o, p_, q, op).then_inc(f_pool.sem, 1)
                        pool.wait_ge(f_pool.sem, f_pool.at(t, k + 2))
                    pool.tensor_tensor(r2, a, c.eps[:, 4:4 + SUB], ALU.pow).then_inc(f_rstd.sem, 1)

                def low(n):
                    def f():
                        for k in range(KC):
                            pool.wait_ge(x_hi.sem, x_hi.at(t, n * KC + k + 1))
                            pool.tensor_tensor(xlo[:, k, :], xf[:, k, :], xhi[:, k, :],
                                               ALU.subtract).then_inc(x_lo.sem, 1)
                    return f

                def qnorm(s):
                    def f():
                        pool.wait_ge(ss_ready.sem, ss_ready.at(t, s + 1))
                        if s >= 2 or not isinstance(t, int) or t > 0:
                            pool.wait_ge(k_stack.sem, k_stack.at(t, s - 1))
                        pool.tensor_tensor(qrs[:, s % 2, :], ms[:, s % 2, :],
                                           c.eps[:, 4:5].to_broadcast([P, 2 * HEADS]), ALU.pow).then_inc(q_rstd.sem, 1)
                    return f

                def low_weights(n):
                    def f():
                        pool.wait_ge(p_hi.sem, p_hi.at(t, n + 1))
                        pool.tensor_tensor(pl[:, n % PB, :], pf[:, n % PB, :], ph[:, n % PB, :],
                                           ALU.subtract).then_inc(p_lo.sem, 1)
                    return f
                return {"f0": lambda: rstd(fmv, frs, f_var, f_rstd, f_pool, t, 0, 0, True), "f1": low(0),
                        "f5": both_norms, "f6": low(1), "f13": low(2), **{"Q%d" % s: qnorm(s) for s in range(SUB)},
                        **{"S%d" % n: low_weights(n) for n in range(SEQS * HEADS)}}

            def back(t):
                def low(h, dst, k):
                    pool.wait_ge(hi_ready.sem, hi_ready.at(t, h + 1))
                    pool.tensor_tensor(hid_lo[dst][:, k, :], g[:, h % 2, :], hid_hi[dst][:, k, :],
                                       ALU.subtract).then_inc(lo_ready.sem, 1)

                def b1():
                    for k in range(KC):
                        pool.wait_ge(y_hi.sem, y_hi.at(t, k + 1))
                        pool.tensor_tensor(ylo[:, k, :], yf[:, k, :], yhi[:, k, :], ALU.subtract).then_inc(y_lo.sem, 1)
                return {"b0": lambda: rstd(bmv, brs, b_var, b_rstd, b_pool, t, 0, 0, False), "b1": b1,
                        **chunks(up=lambda name, k: low(first_hid[name] + k, UPS[name][2], k),
                                 gated=lambda k: low(first_hid["e1"] + k, 0, k))}
            run(pool, front, back)

        @block.scalar
        def _(act):
            def halves(src, f, hi, gain, psum_ready, ready, low_done, t, n, at_low):
                for k in range(KC):
                    act.wait_ge(psum_ready.sem, psum_ready.at(t, n * KC + k + 1))
                    act.wait_ge(low_done.sem, low_done.at(t, at_low))
                    scale = 1.0 if gain is None else c.vec[:, gain + k:gain + k + 1]
                    act.activation(f[:, k, :], src[k][:, :], ACT.Identity, scale=scale)
                    act.activation(hi[:, k, :], src[k][:, :], ACT.Identity, scale=scale).then_inc(ready.sem, 1)

            def front(t):
                def split(n, gain):
                    return lambda: halves(fb, xf, xhi, gain, xnT, x_hi, x_lo, t, n, n * KC)

                def evacuate(k):
                    def f():
                        b = (fb[2], fb[3]) if k == 0 else (fb[0], fb[1])
                        act.wait_ge(k_ps.sem, k_ps.at(t, k + 1))
                        act.activation(kk[:, k, :], b[0][:, :], ACT.Copy)
                        act.wait_ge(r_ps.sem, r_ps.at(t, k + 1))
                        act.activation(vv[:, k, :], b[1][:, :], ACT.Copy).then_inc(kv_ready.sem, 1)
                        act.activation(tr[:, k, :], b[1][:, :], ACT.Tanh, scale=0.5).then_inc(tr_ready.sem, 1)
                    return f

                def exps(k):
                    def f():
                        act.wait_ge(arg_ready.sem, arg_ready.at(t, k + 1))
                        act.activation(T[:, 0:4, :], T[:, 0:4, :], ACT.Exp).then_inc(exp_ready.sem, 1)
                    return f

                def f2():
                    evacuate(0)()
                    evacuate(1)()

                def zsplit(k):
                    def f():
                        act.wait_ge(z_ready.sem, z_ready.at(t, k + 1))
                        act.activation(xhi[:, k, :], z, ACT.Copy).then_inc(z_hi.sem, 1)
                    return f

                def qkv(s):
                    def f():
                        act.wait_ge(qk_ps.sem, qk_ps.at(t, s + 1))
                        if s > 0:
                            act.wait_ge(ss_ready.sem, ss_ready.at(t, s))
                        if s >= 2:
                            act.wait_ge(k_stack.sem, k_stack.at(t, s - 1))
                        act.activation(qkr[s % 2], fb[2][:, :], ACT.Copy)
                        act.activation(qsq, fb[2][:, :], ACT.Square).then_inc(qk_sq.sem, 1)
                        act.wait_ge(v_ps.sem, v_ps.at(t, s + 1))
                        act.wait_ge(v_lo.sem, v_lo.at(t, s))
                        act.activation(vf, fb[3][:, 0:D], ACT.Copy)
                        act.activation(vh[:, s % 2, :, 0:HD], fb[3][:, 0:D].rearrange("p (h d) -> p h d", h=HEADS),
                                       ACT.Copy).then_inc(v_hi.sem, 1)
                    return f

                def stacks(s):
                    def f():
                        for j, dst in enumerate((qT, kT)):
                            act.wait_ge(qkT_ps.sem, qkT_ps.at(t, 2 * s + j + 1))
                            act.activation(dst[:, :, (s % 2) * P:(s % 2 + 1) * P],
                                           fb[j][:, :].bitcast(BF16).rearrange("p (h n) -> p h n", h=HEADS // 2),
                                           ACT.Copy).then_inc(qkT_ready.sem, 1)
                    return f

                def negated(b):
                    def f():
                        act.wait_ge(negT_ps.sem, negT_ps.at(t, b + 1))
                        act.activation(negT[:, :], fb[2][:, 0:P].bitcast(BF16), ACT.Copy).then_inc(negT_ready.sem, 1)
                    return f

                def weights(n):
                    def f():
                        act.wait_ge(P_ps.sem, P_ps.at(t, n + 1))
                        act.wait_ge(p_lo.sem, p_lo.at(t, max(n - PB + 1, 0)))
                        act.activation(pf[:, n % PB, :], fb[n % 2][:, 0:3 * P], ACT.Exp).then_inc(p_f.sem, 1)
                    return f

                def output(b):
                    def f():
                        for q in range(2):
                            act.wait_ge(pv_ps.sem, pv_ps.at(t, (b + 1) * HEADS))
                            act.activation(ou[:, q, :, :], fb[2 + q][:, 0:HEADS * VW].rearrange("p (h d) -> p h d", h=HEADS),
                                           ACT.Copy).then_inc(ou_ready.sem, 1)
                    return f
                return {"f1": split(0, None), "f2": f2, "R0": exps(0), "Z0": zsplit(0), "R1": exps(1), "Z1": zsplit(1),
                        "f6": split(1, VEC["n1_w"]), "f13": split(2, None),
                        **{"Q%d" % s: qkv(s) for s in range(SUB)}, **{"T%d" % s: stacks(s) for s in range(SUB)},
                        **{"N%d" % b: negated(b) for b in range(SEQS)}, **{"O%d" % b: output(b) for b in range(SEQS)},
                        **{"S%d" % n: weights(n) for n in range(SEQS * HEADS)}}

            def back(t):
                def b1():
                    halves(bb[2:4], yf, yhi, VEC["n2_w"], ynT, y_hi, y_lo, t, 0, 0)
                    act.wait_ge(lg_shift.sem, lg_shift.at(t))
                    act.activation(pr[:, :, :], lg[:, :, :], ACT.Exp).then_inc(lg_exp.sem, 1)

                def gelu(name, k):
                    u, h, dst = first_up[name] + k, first_hid[name] + k, UPS[name][2]
                    act.wait_ge(up_ps.sem, up_ps.at(t, u + 1))
                    act.wait_ge(lo_ready.sem, lo_ready.at(t, max(h - 1, 0)))
                    act.activation(g[:, h % 2, :], bb[2 + u % 2][:, :], ACT.Gelu)
                    act.activation(hid_hi[dst][:, k, :], bb[2 + u % 2][:, :], ACT.Gelu).then_inc(hi_ready.sem, 1)

                def gated(k):
                    u, h = first_up["e1"] + 2 * k, first_hid["e1"] + k
                    act.wait_ge(up_ps.sem, up_ps.at(t, u + 1))
                    act.activation(sl[:, :], bb[2][:, :], ACT.Tanh, scale=0.5).then_inc(gate_th.sem, 1)
                    act.wait_ge(gate_sl.sem, gate_sl.at(t, k + 1))
                    act.activation(hid_hi[0][:, k, :], g[:, h % 2, :], ACT.Copy).then_inc(hi_ready.sem, 1)
                return {"b1": b1, **chunks(up=gelu, gated=gated)}
            run(act, front, back)

        @block.vector
        def _(dve):
            F, B = Steps(dve, f_steps), Steps(dve, b_steps)

            def norm(S, src, dst, st, mv, rs, var, rstd, t, n, centred, ready, own=None):
                S.settle()
                for s in range(SUB):
                    S.done(dve.bn_stats(st[:, s, :], src[:, s * D:(s + 1) * D]))
                S.settle()
                S.done(dve.tensor_copy(c.scr[:, 0:1], c.scr[:, 1:2]))
                for s in range(SUB):
                    i = dve.bn_aggr(mv[:, s, :], st[:, s, :])
                i.then_inc(var.sem, 1)
                dve.wait_ge(rstd.sem, rstd.at(t, n + 1))
                if own is not None:
                    for s in range(SUB):
                        q = slice(s * D, (s + 1) * D)
                        i = dve.tensor_scalar(src[:, q], src[:, q], mv[:, s, 0:1], rs[:, 1, s:s + 1],
                                              ALU.subtract, ALU.mult)
                    S.done(i)
                    S.settle()
                    rs = own
                for s in range(SUB):
                    a = (mv[:, s, 0:1], rs[:, 1, s:s + 1], ALU.subtract, ALU.mult) if centred else \
                        (rs[:, 1, s:s + 1], None, ALU.mult)
                    i = dve.tensor_scalar(dst[:, s * D:(s + 1) * D], src[:, s * D:(s + 1) * D], *a)
                i.then_inc(ready.sem, 1)

            dve.memset(pp[:, :, 0:1], -1e38).then_inc(set_up.sem, 1)
            dve.memset(av[:, :, 0:1], 0.0).then_inc(set_up.sem, 1)
            dve.memset(bv[:, :, 0:1], 0.0).then_inc(set_up.sem, 1)
            dve.memset(vh[:, :, :, HD:VW], 1.0).then_inc(set_up.sem, 1)
            dve.memset(qs[:, :, 3 * HD:], 0.0).then_inc(set_up.sem, 1)
            dve.memset(ks[:, :, 3 * HD:], 0.0).then_inc(set_up.sem, 1)
            dve.memset(below[:, :, :], 0.0).then_inc(set_up.sem, 1)
            dve.memset(nstack[:, :, :], 0.0).then_inc(set_up.sem, 1)
            dve.wait_ge(set_up.sem, 8)
            for e in range(1, E1):
                dve.memset(below[:, e, 0:e], 1.0).then_inc(set_up.sem, 1)
            dve.wait_ge(set_up.sem, 8 + E1 - 1)

            def front(t):
                here = bass.ds(t * SUB * D, SUB * D)

                def f0():
                    F.begin(t)
                    dve.wait_ge(yn_ready.sem, yn_ready.at(t, 0))
                    dve.tensor_copy(c.scr[:, 0:1], c.scr[:, 1:2])
                    F.done(dve.tensor_copy(h2[:, :], c.h[:, here]))
                    norm(F, h2, xn, fst, fmv, frs, f_var, f_rstd, t, 0, True, xn_ready)

                def seqs(a, n=SEQ):
                    return a.rearrange("p (b n) -> p b n", b=SEQS)

                def recur_args(k):
                    def f():
                        w, u = c.dec[:, 4 + k:5 + k], c.vec[:, VEC["first1"] + k:VEC["first1"] + k + 1]
                        dve.wait_ge(kv_ready.sem, kv_ready.at(t, k + 1))
                        for b in range(SEQS):
                            F.done(dve.tensor_tensor_scan(pp[:, b, 1:], w.to_broadcast([P, SEQ]),
                                                          kk[:, k, b * SEQ:(b + 1) * SEQ], -1e38, ALU.add, ALU.max))
                        F.settle()
                        before, now, K = pp[:, :, 0:SEQ], pp[:, :, 1:], seqs(kk[:, k, :])
                        F.done(dve.scalar_tensor_tensor(seqs(T[:, 0, :]), before, w, now, ALU.add, ALU.subtract))
                        F.done(dve.tensor_tensor(seqs(T[:, 1, :]), K, now, ALU.subtract))
                        F.done(dve.scalar_tensor_tensor(seqs(T[:, 4, :]), K, u, before, ALU.add, ALU.max))
                        F.settle()
                        F.done(dve.tensor_tensor(seqs(T[:, 2, :]), before, seqs(T[:, 4, :]), ALU.subtract))
                        dve.scalar_tensor_tensor(T[:, 3, :], kk[:, k, :], u, T[:, 4, :], ALU.add,
                                                 ALU.subtract).then_inc(arg_ready.sem, 1)
                    return f

                def recur(k):
                    def f():
                        V = vv[:, k, :]
                        dve.wait_ge(exp_ready.sem, exp_ready.at(t, k + 1))
                        F.done(dve.tensor_tensor(T[:, 4, :], T[:, 1, :], V, ALU.mult))
                        for b in range(SEQS):
                            q = slice(b * SEQ, (b + 1) * SEQ)
                            F.done(dve.tensor_tensor_scan(bv[:, b, 1:], T[:, 0, q], T[:, 1, q], 0.0, ALU.mult, ALU.add))
                        F.settle()
                        for b in range(SEQS):
                            q = slice(b * SEQ, (b + 1) * SEQ)
                            F.done(dve.tensor_tensor_scan(av[:, b, 1:], T[:, 0, q], T[:, 4, q], 0.0, ALU.mult, ALU.add))
                        F.settle()
                        F.done(dve.tensor_tensor(seqs(T[:, 0, :]), seqs(T[:, 2, :]), av[:, :, 0:SEQ], ALU.mult))
                        F.done(dve.tensor_tensor(T[:, 4, :], T[:, 3, :], V, ALU.mult))
                        F.done(dve.tensor_tensor(seqs(T[:, 1, :]), seqs(T[:, 2, :]), bv[:, :, 0:SEQ], ALU.mult))
                        F.settle()
                        F.done(dve.tensor_tensor(T[:, 0, :], T[:, 0, :], T[:, 4, :], ALU.add))
                        F.done(dve.tensor_tensor(T[:, 3, :], T[:, 1, :], T[:, 3, :], ALU.add))
                        F.settle()
                        F.done(dve.reciprocal(T[:, 2, :], T[:, 3, :]))
                        F.settle()
                        F.done(dve.scalar_tensor_tensor(T[:, 1, :], T[:, 0, :], 0.5, T[:, 2, :], ALU.mult, ALU.mult))
                        F.settle()
                        dve.wait_ge(tr_ready.sem, tr_ready.at(t, k + 1))
                        dve.scalar_tensor_tensor(z, tr[:, k, :], 1.0, T[:, 1, :], ALU.add,
                                                 ALU.mult).then_inc(z_ready.sem, 1)
                    return f

                def z_low(k):
                    def f():
                        dve.wait_ge(z_hi.sem, z_hi.at(t, k + 1))
                        dve.tensor_tensor(xlo[:, k, :], z, xhi[:, k, :], ALU.subtract).then_inc(z_lo.sem, 1)
                    return f

                def f5():
                    for j in range(2):
                        q = slice(j * TT, (j + 1) * TT)
                        dve.wait_ge(o_ps.sem, o_ps.at(t, j + 1))
                        dve.tensor_tensor(h2[:, q], h2[:, q], fb[2 + j][:, :], ALU.add).then_inc(h2_ready.sem, 1)
                    dve.wait_ge(h2_ready.sem, h2_ready.at(t))
                    dve.tensor_copy(c.scr[:, 0:1], c.scr[:, 1:2])
                    F.done(dve.tensor_copy(c.h[:, here], h2[:, :]))
                    norm(F, h2, xn, fst, fmv, frs, f_var, f_rstd, t, 1, False, xn_ready, frs[:, 3:5, :])

                def heads_of(s):
                    return qkr[s % 2].rearrange("p (h d) -> p h d", h=2 * HEADS)

                def squares(s):
                    def f():
                        dve.wait_ge(qk_sq.sem, qk_sq.at(t, s + 1))
                        F.done(dve.tensor_reduce(ss[:, s % 2, :], qsq.rearrange("p (h d) -> p h d", h=2 * HEADS), AX.X,
                                                 ALU.add))
                        F.settle()
                        dve.tensor_scalar(ms[:, s % 2, :], ss[:, s % 2, :], 1.0 / HD, EPS1, ALU.mult,
                                          ALU.add).then_inc(ss_ready.sem, 1)
                        dve.wait_ge(v_hi.sem, v_hi.at(t, s + 1))
                        dve.tensor_tensor(vl[:, s % 2, :, :], vf.rearrange("p (h d) -> p h d", h=HEADS),
                                          vh[:, s % 2, :, 0:HD], ALU.subtract).then_inc(v_lo.sem, 1)
                    return f

                def stack(s):
                    def f():
                        heads = heads_of(s)
                        dve.wait_ge(q_rstd.sem, q_rstd.at(t, s + 1))
                        F.done(dve.tensor_tensor(heads, heads, qrs[:, s % 2, :].unsqueeze(2).to_broadcast(
                            [P, 2 * HEADS, HD]), ALU.mult))
                        F.settle()
                        for j in range(2):
                            part = heads[:, j * HEADS:(j + 1) * HEADS, :]
                            F.done(dve.tensor_tensor(part, part, c.qkw2[:, j * HD:(j + 1) * HD].unsqueeze(1)
                                                     .to_broadcast([P, HEADS, HD]), ALU.mult))
                        F.settle()
                        if s > 0:
                            dve.wait_ge(qkT_ps.sem, qkT_ps.at(t, 2 * s))
                        qh, kh = heads[:, 0:HEADS, :], heads[:, HEADS:, :]
                        F.done(dve.tensor_copy(qs[:, :, 0:HD], qh))
                        F.done(dve.tensor_copy(qs[:, :, HD:2 * HD], qh))
                        F.done(dve.tensor_copy(ks[:, :, 0:HD], kh))
                        F.done(dve.tensor_copy(ks[:, :, 2 * HD:3 * HD], kh))
                        F.settle()
                        dve.tensor_tensor(qs[:, :, 2 * HD:3 * HD], qh, qs[:, :, 0:HD],
                                          ALU.subtract).then_inc(q_stack.sem, 1)
                        dve.tensor_tensor(ks[:, :, HD:2 * HD], kh, ks[:, :, 0:HD],
                                          ALU.subtract).then_inc(k_stack.sem, 1)
                    return f

                def maxima(b):
                    def f():
                        for n in range(12):
                            m = b * 12 + n
                            dve.wait_ge(S_ps.sem, S_ps.at(t, m + 1))
                            if n < 8:
                                o, w = mx[:, 1, group(n)[0]:group(n)[-1] + 1:2], SEQ
                            else:
                                o, w = mx[:, 0, group(n)[0]:group(n)[-1] + 1:2], P
                            dve.tensor_reduce(o, fb[n % 2][:, :].rearrange("p (h k) -> p h k", k=w), AX.X,
                                              ALU.max).then_inc(mx_ready.sem, 1)
                        dve.wait_ge(mx_ready.sem, mx_ready.at(t, (b + 1) * 12))
                        F.done(dve.tensor_scalar(npart[:, :, :, 0], mx[:, :, :], -1.0, None, ALU.mult))
                        F.settle()
                        F.done(dve.scalar_tensor_tensor(mr[:, 0, :, :], mx[:, :, :], -1.0, npart[:, :, :, 0], ALU.mult,
                                                        ALU.subtract))
                        F.settle()
                        F.done(dve.tensor_copy(npart[:, :, :, 1], mr[:, 0, :, :]))
                        F.settle()
                        dve.tensor_tensor(npart[:, :, :, 2], mr[:, 0, :, :], npart[:, :, :, 1],
                                          ALU.subtract).then_inc(np_ready.sem, 1)
                    return f

                def high_weights(n):
                    def f():
                        dve.wait_ge(p_f.sem, p_f.at(t, n + 1))
                        if n >= PB:
                            dve.wait_ge(pv_ps.sem, pv_ps.at(t, n - PB + 1))
                        dve.tensor_copy(ph[:, n % PB, :], pf[:, n % PB, :]).then_inc(p_hi.sem, 1)
                    return f

                def output(b):
                    def f():
                        dve.wait_ge(ou_ready.sem, ou_ready.at(t, 2 * (b + 1)))
                        F.done(dve.reciprocal(den[:, :, :], ou[:, :, :, HD]))
                        F.settle()
                        for q in range(2):
                            o = xn[:, (2 * b + q) * D:(2 * b + q + 1) * D].rearrange("p (h d) -> p h d", h=HEADS)
                            i = dve.tensor_tensor(o, ou[:, q, :, 0:HD], den[:, q, :].unsqueeze(2).to_broadcast(
                                [P, HEADS, HD]), ALU.mult)
                            if q == 0 or b == 0:
                                F.done(i)
                        if b == SEQS - 1:
                            i.then_inc(xn_ready.sem, 1)
                    return f

                def f13():
                    for j in range(2):
                        dve.wait_ge(ao_ps.sem, ao_ps.at(t, j + 1))
                        q = h2[:, j * TT:(j + 1) * TT].rearrange("p (s d) -> p s d", s=2)[:, :, ZERO:]
                        F.done(dve.tensor_tensor(q, q, fb[2 + j][:, :].rearrange("p (s d) -> p s d", s=2)[:, :, 0:DZ],
                                                 ALU.add))
                    F.settle()
                    dve.tensor_tensor(c.h[:, here], c.h[:, here], h2[:, :], ALU.add).then_inc(h3_ready.sem, 1)
                    F.end()
                return {"f0": f0, "A0": recur_args(0), "R0": recur(0), "Z0": z_low(0), "A1": recur_args(1),
                        "R1": recur(1), "Z1": z_low(1), "f5": f5, "f13": f13,
                        **{"Q%d" % s: squares(s) for s in range(SUB)}, **{"K%d" % s: stack(s) for s in range(SUB)},
                        **{"M%d" % b: maxima(b) for b in range(SEQS)}, **{"O%d" % b: output(b) for b in range(SEQS)},
                        **{"S%d" % n: high_weights(n) for n in range(SEQS * HEADS)}}

            def back(t):
                def b0():
                    B.begin(t)
                    dve.wait_ge(h3_ready.sem, h3_ready.at(t))
                    norm(B, h2, yn, bst, bmv, brs, b_var, b_rstd, t, 0, False, yn_ready)

                def b1():
                    dve.wait_ge(lg_ps.sem, lg_ps.at(t))
                    dve.tensor_copy(pr[:, :, :], bb[0][:, 0:SUB * E1].rearrange("p (s e) -> p s e", s=SUB)
                                    ).then_inc(lg_ready.sem, 1)
                    dve.wait_ge(lg_ready.sem, lg_ready.at(t))
                    dve.wait_ge(down_used.sem, down_used.at(t, 0))
                    B.done(dve.memset(lg[:, :, :], 0.0))
                    B.settle()
                    B.done(dve.tensor_tensor(wt[:, :, :], pr[:, :, :], pr[:, :, :], ALU.is_equal))
                    B.settle()
                    B.done(dve.tensor_copy(c.scr[:, 0:1], c.scr[:, 1:2]))
                    B.done(dve.copy_predicated(lg[:, :, :], wt[:, :, :].bitcast(U32), pr[:, :, :]))
                    B.settle()
                    B.done(dve.tensor_scalar(lg[:, :, :], lg[:, :, :], -3.4028234e38, 3.4028234e38, ALU.max, ALU.min))
                    B.settle()
                    B.done(dve.tensor_reduce(r1[:, 0, :], lg[:, :, :], AX.X, ALU.max))
                    B.settle()

                    def over(n):
                        return r1[:, n, :].unsqueeze(2).to_broadcast([P, SUB, E1])
                    dve.tensor_tensor(lg[:, :, :], lg[:, :, :], over(0), ALU.subtract).then_inc(lg_shift.sem, 1)
                    dve.wait_ge(lg_exp.sem, lg_exp.at(t))
                    B.done(dve.tensor_reduce(r1[:, 1, :], pr[:, :, :], AX.X, ALU.add))
                    B.settle()
                    B.done(dve.reciprocal(r1[:, 2, :], r1[:, 1, :]))
                    B.settle()
                    B.done(dve.tensor_tensor(pr[:, :, :], pr[:, :, :], over(2), ALU.mult))
                    B.settle()
                    pj = pr[:, :, :].unsqueeze(2).to_broadcast([P, SUB, E1, E1])
                    pe_ = pr[:, :, :].unsqueeze(3).to_broadcast([P, SUB, E1, E1])
                    B.done(dve.tensor_tensor(gt[:, :, :, :], pj, pe_, ALU.is_gt))
                    B.done(dve.tensor_tensor(eq[:, :, :, :], pj, pe_, ALU.is_equal))
                    B.settle()
                    B.done(dve.tensor_tensor(eq[:, :, :, :], eq[:, :, :, :],
                                             below[:, :, :].unsqueeze(1).to_broadcast([P, SUB, E1, E1]), ALU.mult))
                    B.settle()
                    B.done(dve.tensor_tensor(gt[:, :, :, :], gt[:, :, :, :], eq[:, :, :, :], ALU.add))
                    B.settle()
                    B.done(dve.tensor_reduce(lg[:, :, :], gt[:, :, :, :], AX.X, ALU.add))
                    B.settle()
                    B.done(dve.scalar_tensor_tensor(wt[:, :, :], lg[:, :, :], 2.0, pr[:, :, :], ALU.is_lt, ALU.mult))
                    B.settle()
                    B.done(dve.tensor_reduce(r1[:, 0, :], wt[:, :, :], AX.X, ALU.add))
                    B.settle()
                    B.done(dve.tensor_scalar(r1[:, 1, :], r1[:, 0, :], 1e-8, None, ALU.add))
                    B.settle()
                    B.done(dve.reciprocal(r1[:, 3, :], r1[:, 1, :]))
                    B.settle()
                    B.done(dve.tensor_tensor(wt[:, :, :], wt[:, :, :], over(3), ALU.mult))
                    B.settle()

                def gated(k):
                    h, u = first_hid["e1"] + k, first_up["e1"] + 2 * k
                    dve.wait_ge(gate_th.sem, gate_th.at(t, k + 1))
                    B.done(dve.scalar_tensor_tensor(sl2[:, :], sl[:, :], 1.0, bb[2][:, :], ALU.add, ALU.mult))
                    B.settle()
                    dve.wait_ge(up_ps.sem, up_ps.at(t, u + 2))
                    dve.wait_ge(lo_ready.sem, lo_ready.at(t, h - 1))
                    dve.scalar_tensor_tensor(g[:, h % 2, :], sl2[:, :], 0.5, bb[3][:, :], ALU.mult,
                                             ALU.mult).then_inc(gate_sl.sem, 1)

                def down(name, e, src, k):
                    if k < HC - 1:
                        return
                    d = first_down[name]
                    dve.wait_ge(down_ps.sem, down_ps.at(t, d + 1))
                    dve.wait_ge(down_used.sem, down_used.at(t, d * SUB))
                    for s in range(SUB):
                        q = bass.ds((t * SUB + s) * D + ZERO, DZ)
                        dve.scalar_tensor_tensor(c.h[:, q], bb[s // 2][:, (s % 2) * D:(s % 2) * D + DZ],
                                                 wt[:, s, e:e + 1], c.h[:, q], ALU.mult,
                                                 ALU.add).then_inc(down_used.sem, 1)
                    if d == ND - 1:
                        B.end()
                return {"b0": b0, "b1": b1, **chunks(gated=gated, down=down)}
            run(dve, front, back)

        @block.tensor
        def _(pe):
            PARTS = ((0, 0), (1, 0), (0, 1))
            WC = (c.WC_hi, c.WC_lo)

            def feature_major(bank, name, e, xs, kc=KC, lo_wait=None):
                for j, (wp, xp) in enumerate(PARTS):
                    if j == 2 and lo_wait is not None:
                        pe.wait_ge(*lo_wait)
                    for k in range(kc):
                        m = pe.matmul(bank[:, :], W(WC[wp], name, k, e * P, P), xs[xp][:, k, :],
                                      start=(j == 0 and k == 0), stop=(j == 2 and k == kc - 1))
                return m

            def token_major(o, name, s, xs, n):
                for j, (wp, xp) in enumerate(PARTS):
                    for k in range(KC):
                        m = pe.matmul(o, xs[xp][:, k, s * P:(s + 1) * P], W(WC[wp], name, k, 0, n),
                                      start=(j == 0 and k == 0), stop=(j == 2 and k == KC - 1))
                return m

            def transposes(src, banks, ready):
                for k in range(KC):
                    for s in range(SUB):
                        m = pe.transpose(banks[k][:, s * P:(s + 1) * P], src[:, s * D + k * P:s * D + (k + 1) * P],
                                         c.ident[:, :])
                    m.then_inc(ready.sem, 1)

            X = (xhi, xlo)

            def front(t):
                def f1():
                    pe.wait_ge(xn_ready.sem, xn_ready.at(t, 1))
                    pe.wait_ge(x_hi.sem, x_hi.at(t, 0))
                    transposes(xn, fb, xnT)

                def f2():
                    pe.wait_ge(x_hi.sem, x_hi.at(t, KC))
                    pe.wait_ge(h3_ready.sem, h3_ready.at(t, 0))
                    feature_major(fb[2], "Wk", 0, X, lo_wait=(x_lo.sem, x_lo.at(t, KC))).then_inc(k_ps.sem, 1)
                    feature_major(fb[3], "Wr", 0, X).then_inc(r_ps.sem, 1)
                    feature_major(fb[0], "Wk", 1, X).then_inc(k_ps.sem, 1)
                    feature_major(fb[1], "Wr", 1, X).then_inc(r_ps.sem, 1)

                def f5():
                    pe.wait_ge(z_hi.sem, z_hi.at(t))
                    pe.wait_ge(z_lo.sem, z_lo.at(t))
                    pe.wait_ge(tr_ready.sem, tr_ready.at(t))
                    for s in range(SUB):
                        m = token_major(fb[2 + s // 2][:, (s % 2) * D:(s % 2 + 1) * D], "Wo", s, X, D)
                        if s % 2:
                            m.then_inc(o_ps.sem, 1)

                def f6():
                    pe.wait_ge(xn_ready.sem, xn_ready.at(t, 2))
                    transposes(xn, fb, xnT)

                def qkv(s):
                    def f():
                        if s == 0:
                            pe.wait_ge(x_hi.sem, x_hi.at(t, 2 * KC))
                            pe.wait_ge(x_lo.sem, x_lo.at(t, 2 * KC))
                            pe.wait_ge(h2_ready.sem, h2_ready.at(t))
                        else:
                            pe.wait_ge(v_hi.sem, v_hi.at(t, s))
                        if s == 2:
                            pe.wait_ge(ou_ready.sem, ou_ready.at(t, 2))
                        token_major(fb[2][:, :], "wqk", s, X, 2 * D).then_inc(qk_ps.sem, 1)
                        token_major(fb[3][:, 0:D], "wv", s, X, D).then_inc(v_ps.sem, 1)
                    return f

                def stacks(s):
                    def f():
                        for j, (src, ready) in enumerate(((qs, q_stack), (ks, k_stack))):
                            pe.wait_ge(ready.sem, ready.at(t, s + 1))
                            if s > 0:
                                pe.wait_ge(qkT_ready.sem, qkT_ready.at(t, 2 * s + j - 1))
                            bank = fb[j][:, :].bitcast(BF16)
                            for h in range(HEADS // 2):
                                m = pe.transpose(bank[:, h * P:(h + 1) * P],
                                                 src[:, 2 * h:2 * h + 2, :].rearrange("p a d -> p (a d)"),
                                                 c.identb[:, :])
                            m.then_inc(qkT_ps.sem, 1)
                    return f

                def rows(h):
                    return slice(64 * (h % 2), 64 * (h % 2) + 64)

                def maxima(b):
                    def f():
                        pe.wait_ge(qkT_ready.sem, qkT_ready.at(t, 4 * (b + 1)))
                        for n in range(12):
                            m = b * 12 + n
                            if n >= 2:
                                pe.wait_ge(mx_ready.sem, mx_ready.at(t, m - 1))
                            bank = fb[n % 2]
                            if n < 8:
                                for j, h in enumerate(group(n)):
                                    q = j * SEQ
                                    pe.matmul(bank[:, q:q + SEQ], qT[rows(h), h // 2, P:2 * P], kT[rows(h), h // 2, :],
                                              start=True, stop=False, skip_group_check=True)
                                    i = pe.matmul(bank[:, q + P:q + SEQ], c.identb[:, :], c.mask[:, 0:P],
                                                  start=False, stop=True, skip_group_check=True)
                            else:
                                for j, h in enumerate(group(n)):
                                    q = j * P
                                    pe.matmul(bank[:, q:q + P], qT[rows(h), h // 2, 0:P], kT[rows(h), h // 2, 0:P],
                                              start=True, stop=False, skip_group_check=True)
                                    i = pe.matmul(bank[:, q:q + P], c.identb[:, :], c.mask[:, 0:P],
                                                  start=False, stop=True, skip_group_check=True)
                            i.then_inc(S_ps.sem, 1)
                    return f

                def scores(n):
                    def f():
                        h = n % HEADS
                        bank = fb[n % 2]
                        if h == 0:
                            pe.wait_ge(negT_ready.sem, negT_ready.at(t, n // HEADS + 1))
                        if h >= 2:
                            pe.wait_ge(p_f.sem, p_f.at(t, n - 1))
                        for lo, ks_, qs_ in ((0, 0, 0), (SEQ, P, P)):
                            w = SEQ - qs_
                            pe.matmul(bank[:, lo:lo + w], kT[rows(h), h // 2, ks_:ks_ + P], qT[rows(h), h // 2, qs_:SEQ],
                                      start=True, stop=False, skip_group_check=True)
                            pe.matmul(bank[:, lo:lo + P], c.identb[:, :], c.mask[:, P:2 * P],
                                      start=False, stop=False, skip_group_check=True)
                            i = pe.matmul(bank[:, lo:lo + w], c.sel[:, h, :], negT[:, qs_:SEQ],
                                          start=False, stop=True, skip_group_check=True)
                        i.then_inc(P_ps.sem, 1)
                    return f

                def values(n):
                    def f():
                        h = n % HEADS
                        if h == 0:
                            pe.wait_ge(v_lo.sem, v_lo.at(t, 2 * (n // HEADS + 1)))
                        pe.wait_ge(p_hi.sem, p_hi.at(t, n + 1))
                        pe.wait_ge(p_lo.sem, p_lo.at(t, n + 1))
                        for q, blocks in ((0, ((0, 0),)), (1, ((P, 0), (SEQ, 1)))):
                            o = fb[2 + q][:, h * VW:(h + 1) * VW]
                            for a, (lo, kt) in enumerate(blocks):
                                last = a == len(blocks) - 1
                                hi_, lo_ = ph[:, n % PB, lo:lo + P], pl[:, n % PB, lo:lo + P]
                                pe.matmul(o, hi_, vh[:, kt, h, :], start=(a == 0), stop=False, skip_group_check=True)
                                pe.matmul(o[:, 0:HD], hi_, vl[:, kt, h, :], start=False, stop=False,
                                          skip_group_check=True)
                                i = pe.matmul(o, lo_, vh[:, kt, h, :], start=False, stop=last, skip_group_check=True)
                        i.then_inc(pv_ps.sem, 1)
                    return f

                def negated(b):
                    def f():
                        pe.wait_ge(np_ready.sem, np_ready.at(t, b + 1))
                        pe.wait_ge(v_hi.sem, v_hi.at(t, 2 * (b + 1)))
                        bank = fb[2][:, 0:P].bitcast(BF16)
                        for q in range(2):
                            m = pe.transpose(bank[:, q * P:(q + 1) * P], nstack[:, q, :],
                                             c.identb[:, :])
                        m.then_inc(negT_ps.sem, 1)
                    return f

                def f13():
                    pe.wait_ge(xn_ready.sem, xn_ready.at(t, 3))
                    transposes(xn, fb, xnT)
                    pe.wait_ge(x_hi.sem, x_hi.at(t, 3 * KC))
                    pe.wait_ge(x_lo.sem, x_lo.at(t, 3 * KC))
                    for s in range(SUB):
                        m = token_major(fb[2 + s // 2][:, (s % 2) * D:(s % 2) * D + DZ], "wo", s, X, DZ)
                        if s % 2:
                            m.then_inc(ao_ps.sem, 1)
                return {"f1": f1, "f2": f2, "f5": f5, "f6": f6, "f13": f13,
                        **{"Q%d" % s: qkv(s) for s in range(SUB)}, **{"T%d" % s: stacks(s) for s in range(SUB)},
                        **{"M%d" % b: maxima(b) for b in range(SEQS)}, **{"N%d" % b: negated(b) for b in range(SEQS)},
                        **{"S%d" % n: scores(n) for n in range(SEQS * HEADS)},
                        **{"V%d" % n: values(n) for n in range(SEQS * HEADS)}}

            def back(t):
                def b1():
                    pe.wait_ge(yn_ready.sem, yn_ready.at(t))
                    pe.wait_ge(gate_sl.sem, gate_sl.at(t, 0))
                    transposes(yn, bb[2:4], ynT)
                    pe.wait_ge(y_hi.sem, y_hi.at(t))
                    pe.wait_ge(down_used.sem, down_used.at(t, 0))
                    for s in range(SUB):
                        for k in range(KC):
                            m = pe.matmul(bb[0][:, s * E1:(s + 1) * E1], yf[:, k, s * P:(s + 1) * P],
                                          c.gate[:, k * E1:(k + 1) * E1], start=(k == 0), stop=(k == KC - 1))
                    m.then_inc(lg_ps.sem, 1)
                    pe.wait_ge(y_lo.sem, y_lo.at(t))

                def free(u):
                    v, g0 = u - 2, first_up["e1"]
                    if 0 <= v < g0:
                        pe.wait_ge(hi_ready.sem, hi_ready.at(t, v + 1))
                    elif v >= g0:
                        pe.wait_ge(gate_sl.sem, gate_sl.at(t, (v - g0) // 2 + 1))

                def up(name, k):
                    src, kc, dst, cs = UPS[name]
                    xs = (yhi, ylo) if src is None else (hid_hi[src], hid_lo[src])
                    if src is not None and k == 0:
                        h = first_hid[maker[name]] + kc
                        pe.wait_ge(hi_ready.sem, hi_ready.at(t, h))
                        pe.wait_ge(lo_ready.sem, lo_ready.at(t, h))
                    u = first_up[name] + k
                    free(u)
                    feature_major(bb[2 + u % 2], name, k, xs, kc).then_inc(up_ps.sem, 1)

                def gated(k):
                    for j, name in enumerate(("e1_w1", "e1_w2")):
                        u = first_up["e1"] + 2 * k + j
                        free(u)
                        feature_major(bb[2 + u % 2], name, k, (yhi, ylo)).then_inc(up_ps.sem, 1)

                def down(name, e, src, k):
                    d = first_down[name]
                    if k == 0 and d == 0:
                        pe.wait_ge(lg_ready.sem, lg_ready.at(t))
                    elif k == 0:
                        pe.wait_ge(down_used.sem, down_used.at(t, d * SUB))
                    h = first_hid[maker[name]] + k + 1
                    pe.wait_ge(hi_ready.sem, hi_ready.at(t, h))
                    pe.wait_ge(lo_ready.sem, lo_ready.at(t, h))
                    for s in range(SUB):
                        for j, (wp, xp) in enumerate(PARTS):
                            xs = (hid_hi[src], hid_lo[src])[xp]
                            m = pe.matmul(bb[s // 2][:, (s % 2) * D:(s % 2) * D + DZ], xs[:, k, s * P:(s + 1) * P],
                                          W(WC[wp], name, k, 0, DZ), start=(k == 0 and j == 0 and s % 2 == 0),
                                          stop=(k == HC - 1 and j == 2), skip_group_check=True)
                    if k == HC - 1:
                        m.then_inc(down_ps.sem, 1)
                return {"b1": b1, **chunks(up=up, gated=gated, down=down)}
            run(pe, front, back)


def program(nc, ins, out, upto="c"):
    c = Chip()
    c.i = ins
    with ExitStack() as x:
        def sb(name, shape, dt=F32):
            return x.enter_context(nc.sbuf_tensor(name, shape, dt))
        c.h = sb("h", [P, TILES * SUB * D])
        c.w0 = sb("w0", [P, TILES * SUB * E0])
        c.vec, c.dec = sb("vec", [P, NVEC]), sb("dec", [P, 6])
        c.b1, c.b2 = sb("b1", [P, E0 * HC0]), sb("b2", [E0, D])
        c.Wrt, c.br, c.gate = sb("Wrt", [P, KC * E0]), sb("br", [1, E0]), sb("gate", [P, KC * E1])
        c.qkw, c.qkw2 = sb("qkw", [P, 2 * HD]), sb("qkw2", [P, 2 * HD])
        c.ident, c.identb = sb("ident", [P, P]), sb("identb", [P, P], BF16)
        c.mask, c.sel = sb("mask", [P, 2 * P], BF16), sb("sel", [P, HEADS, P], BF16)
        c.ones, c.eps, c.scr = sb("ones", [1, P]), sb("eps", [P, 13]), sb("scr", [P, 2])
        c.xT_hi, c.xT_lo = sb("xT_hi", [P, KC * N], BF16), sb("xT_lo", [P, KC * N], BF16)
        with ExitStack() as a:
            def sa(name, shape, dt=F32):
                return a.enter_context(nc.sbuf_tensor(name, shape, dt))
            c.tok, c.idx, c.zero_i = sa("tok_s", [P, TILES * SUB], I32), sa("idx", [P, SUB], I32), sa("zero_i", [P, SUB], I32)
            c.zero_j = sa("zero_j", [P, 1], I32)
            c.WA_hi, c.WA_lo = sa("WA_hi", [P, COLS_A], BF16), sa("WA_lo", [P, COLS_A], BF16)
            c.idx_ready = a.enter_context(nc.semaphore("idx_ready"))
            phase_load(nc, c)
            phase_a(nc, c)
        if upto == "a":
            s = x.enter_context(nc.semaphore("dump"))
            with nc.Block() as block:
                @block.sync
                def _(sp):
                    sp.dma_start(out[0], c.h[:, :]).then_inc(s, 16)
                    sp.dma_start(out[1], c.w0[:, :]).then_inc(s, 16)
                    sp.wait_ge(s, 32)
            return

        c.WC_hi, c.WC_lo = sb("WC_hi", [P, COLS_C], BF16), sb("WC_lo", [P, COLS_C], BF16)
        phase_b(nc, c)
        if upto == "b":
            s = x.enter_context(nc.semaphore("dump"))
            with nc.Block() as block:
                @block.sync
                def _(sp):
                    sp.dma_start(out[0], c.h[:, :]).then_inc(s, 16)
                    sp.wait_ge(s, 16)
            return

        phase_c(nc, c, out)


def pack(np, m):
    k, n = m.shape
    return np.ascontiguousarray(m.reshape(k // P, P, n).transpose(1, 0, 2).reshape(P, -1))


def layout(inputs):
    import numpy as np
    g = {k: np.asarray(v) for k, v in inputs.items()}
    a = {}
    a["tok"] = np.ascontiguousarray(g["x"].reshape(TILES * SUB, P).T)
    a["emb"] = g["L0_tok_W_E"]
    L = "L0_attn_"
    a["WA"] = np.concatenate([pack(np, g[L + n].T) for n in ("Ww", "Wk", "Wv", "Wr", "Wo", "Wrec", "Wkey", "Wval")], 1)
    names = (L + "ln1_g", L + "ln1_b", L + "ln2_g", L + "ln2_b", L + "time_decay", "L1_attn_time_decay",
             "L1_attn_time_first", "L1_ffn_n1_w", "L1_ffn_n2_w")
    a["vec"] = np.concatenate([g[n].reshape(KC, P).T for n in names], 1)
    a["b1"] = np.ascontiguousarray(g["L0_ffn_b1"].reshape(E0 * HC0, P).T)
    a["b2"] = g["L0_ffn_b2"]
    a["Wrt"] = pack(np, g["L0_ffn_Wr"])
    a["br"] = g["L0_ffn_br"].reshape(1, E0)
    a["gate"] = pack(np, g["L1_ffn_gate_w"].T)
    a["qn"], a["kn"] = g["L1_ffn_qn_w"], g["L1_ffn_kn_w"]
    w0 = np.stack([np.concatenate([pack(np, g["L0_ffn_W1"][e]), pack(np, g["L0_ffn_W2"][e])], 1)
                   for e in range(E0)])
    w0 = w0.reshape(E0, P, TILES, PIECE_E).transpose(0, 2, 1, 3).reshape(PIECES, P, PIECE_E)
    A, Fn = "L1_attn_", "L1_ffn_"
    m = {n: g[A + n].T for n in ("Wk", "Wr", "Wo")}
    m["wqk"] = np.concatenate([g[Fn + "wq"].T, g[Fn + "wk"].T], 1)
    m["wv"], m["wo"] = g[Fn + "wv"].T, g[Fn + "wo"].T[:, ZERO:]
    for n in OFF_C:
        if n[0] == "e":
            m[n] = g[Fn + n].T
            if OFF_C[n][1] == DZ:
                m[n] = m[n][:, ZERO:]
    wc = np.concatenate([pack(np, m[n]) for n in OFF_C], 1).reshape(P, PIECES, PIECE_C).transpose(1, 0, 2)
    a["WP"] = np.concatenate([w0, wc], 2)
    return {k: np.ascontiguousarray(v) for k, v in a.items()}


def kernel(**inputs):
    from concourse import bacc as _bacc
    from concourse.bass_utils import run_bass_kernel_spmd as _run

    arrays = layout(inputs)
    nc = _bacc.Bacc("TRN2", target_bir_lowering=False, num_devices=1)
    ins = {n: nc.dram_tensor(f"in_{n}", list(a.shape), mybir.dt.from_np(a.dtype), kind="ExternalInput").ap()
           for n, a in arrays.items()}
    out = nc.dram_tensor("out", [N, D], F32, kind="ExternalOutput").ap()
    program(nc, ins, out)
    r = _run(nc, [{f"in_{n}": a for n, a in arrays.items()}], core_ids=[0])
    return r.results[0]["out"].reshape(BATCH, SEQ, D)
```

```python
import concourse.bass as bass
from concourse import mybir
from contextlib import ExitStack

F32 = mybir.dt.float32
BF16 = mybir.dt.bfloat16
I32 = mybir.dt.int32
U32 = mybir.dt.uint32
ALU = mybir.AluOpType
ACT = mybir.ActivationFunctionType
AX = mybir.AxisListType

P = 128
BATCH, SEQ, D = 16, 256, 256
N = BATCH * SEQ
KC = D // P
TT = 512
EPS1 = 1.1920929e-07
TILES = N // TT
SUB = TT // P
SEQS = TT // SEQ
VOCAB = 50257
EMB_SCALE = float(D) ** 0.5
LN_EPS, WKV_EPS = 1e-5, 1e-8

F0 = 1024
OFF_A = {}
_at = 0
for _name, _k, _n in (("Ww", D, D), ("Wk", D, D), ("Wv", D, D), ("Wr", D, D), ("Wo", D, D),
                      ("Wrec", D, D), ("Wkey", D, F0), ("Wval", F0, D)):
    OFF_A[_name] = (_at, _n)
    _at += _k // P * _n
COLS_A = _at

E0, H0 = 8, 1024
HC0 = H0 // P
COLS_E = KC * H0 + HC0 * D

HEADS, HD = 16, 16
ZERO = 64
DZ = D - ZERO
E1, HID = 4, 512
OFF_C = {}
_at = 0
for _name, _k, _n in (("Wk", D, D), ("Wr", D, D), ("Wo", D, D),
                      ("wqk", D, 2 * D), ("wv", D, D), ("wo", D, DZ),
                      ("e0_up", D, HID), ("e0_down", HID, DZ),
                      ("e1_w1", D, HID), ("e1_w2", D, HID), ("e1_down", HID, DZ),
                      ("e2_l1", D, HID), ("e2_l2", HID, HID), ("e2_l3", HID, HID), ("e2_l4", HID, DZ),
                      ("e3_down", D, D), ("e3_up", D, HID), ("e3_out", HID, DZ)):
    OFF_C[_name] = (_at, _n)
    _at += _k // P * _n
COLS_C = _at


PIECES = E0 * TILES
PIECE_E, PIECE_C = COLS_E // TILES, COLS_C // PIECES
assert PIECE_C * PIECES == COLS_C

VEC = {n: 2 * i for i, n in enumerate(("ln1_g", "ln1_b", "ln2_g", "ln2_b", "decay0",
                                       "decay1", "first1", "n1_w", "n2_w"))}
NVEC = 2 * len(VEC)


class Count:

    def __init__(self, sem, per, base=0):
        self.sem, self.per, self.base = sem, per, base

    def at(self, t, n=None):
        return t * self.per + ((self.per if n is None else n) + self.base)


class Steps:

    def __init__(self, eng, count):
        self.eng, self.count = eng, count

    def begin(self, t):
        self.t, self.n = t, 0

    def done(self, ins):
        ins.then_inc(self.count.sem, 1)
        self.n += 1

    def settle(self):
        self.eng.wait_ge(self.count.sem, self.count.at(self.t, self.n))

    def end(self):
        assert self.n == self.count.per, (self.n, self.count.per)


class Chip:
    pass


def phase_load(nc, c):
    CH = 1024
    NCH = COLS_A // CH
    with ExitStack() as x:
        stage = x.enter_context(nc.sbuf_tensor("stage_a", [P, NCH, CH], F32))
        s_w = [x.enter_context(nc.semaphore(f"ld_weights{k}")) for k in range(NCH)]
        s_v = x.enter_context(nc.semaphore("ld_vectors"))
        s_hi = x.enter_context(nc.semaphore("ld_high"))
        s_lo = x.enter_context(nc.semaphore("ld_low"))
        s_c = x.enter_context(nc.semaphore("ld_constants"))
        s_d = x.enter_context(nc.semaphore("ld_decay"))
        s_p = x.enter_context(nc.semaphore("ld_router_parts"))
        block = x.enter_context(nc.Block())

        @block.sync
        def _(sp):
            for dst, src in ((c.tok, c.i["tok"]), (c.vec, c.i["vec"]), (c.b1, c.i["b1"]),
                             (c.rw[0], c.i["Wrt"]), (c.br, c.i["br"].partition_broadcast(P)), (c.rw[1], c.i["gate"]),
                             (c.qkw[:, 0:HD], c.i["qn"].partition_broadcast(P)),
                             (c.qkw[:, HD:2 * HD], c.i["kn"].partition_broadcast(P))):
                sp.dma_start(dst[:, :] if dst is not c.qkw else dst, src).then_inc(s_v, 16)
            for k in range(NCH):
                sp.dma_start(stage[:, k, :], c.i["WA"][:, k * CH:(k + 1) * CH]).then_inc(s_w[k], 16)
            sp.wait_ge(s_v, 8 * 16)

        @block.scalar
        def _(act):
            act.wait_ge(s_v, 8 * 16)
            act.activation(c.dec[:, 0:4], c.vec[:, VEC["decay0"]:VEC["decay0"] + 4], ACT.Exp).then_inc(s_d, 1)
            for k in range(NCH):
                act.wait_ge(s_w[k], 16)
                act.activation(c.WA_hi[:, k * CH:(k + 1) * CH], stage[:, k, :], ACT.Copy).then_inc(s_hi, 1)

        @block.vector
        def _(dve):
            dve.memset(c.ones[:, :], 1.0).then_inc(s_c, 1)
            dve.memset(c.scr[:, :], 0.0).then_inc(s_c, 1)
            dve.memset(c.eps[:, 0:4], LN_EPS).then_inc(s_c, 1)
            dve.memset(c.eps[:, 4:8], -0.5).then_inc(s_c, 1)
            dve.memset(c.eps[:, 8:12], EPS1).then_inc(s_c, 1)
            dve.memset(c.eps[:, 12:13], 1.0 / HD).then_inc(s_c, 1)
            dve.wait_ge(s_d, 1)
            dve.tensor_scalar(c.dec[:, 4:6], c.dec[:, 2:4], -1.0, None, ALU.mult).then_inc(s_c, 1)
            dve.wait_ge(s_v, 8 * 16)
            dve.tensor_scalar(c.qkw2[:, 0:HD], c.qkw[:, 0:HD], float(HD) ** -0.5, None, ALU.mult).then_inc(s_c, 1)
            dve.tensor_copy(c.qkw2[:, HD:2 * HD], c.qkw[:, HD:2 * HD]).then_inc(s_c, 1)
            for w, rest, parts in zip(c.rw, c.rw_rest, c.rw3):
                dve.tensor_copy(parts[:, 0, :], w[:, :]).then_inc(s_p, 1)
            for n, (w, rest, parts) in enumerate(zip(c.rw, c.rw_rest, c.rw3)):
                dve.wait_ge(s_p, 2)
                dve.tensor_tensor(rest[:, :], w[:, :], parts[:, 0, :], ALU.subtract).then_inc(s_p, 1)
            for n, (w, rest, parts) in enumerate(zip(c.rw, c.rw_rest, c.rw3)):
                dve.wait_ge(s_p, 4)
                dve.tensor_copy(parts[:, 1, :], rest[:, :]).then_inc(s_p, 1)
            for n, (w, rest, parts) in enumerate(zip(c.rw, c.rw_rest, c.rw3)):
                dve.wait_ge(s_p, 6)
                dve.tensor_tensor(parts[:, 2, :], rest[:, :], parts[:, 1, :], ALU.subtract).then_inc(s_p, 1)
            for k in range(NCH):
                dve.wait_ge(s_hi, k + 1)
                dve.tensor_tensor(c.WA_lo[:, k * CH:(k + 1) * CH], stage[:, k, :],
                                  c.WA_hi[:, k * CH:(k + 1) * CH], ALU.subtract).then_inc(s_lo, 1)

        @block.gpsimd
        def _(pool):
            pool.memset(c.ident[:, :], 0.0).then_inc(s_c, 1)
            pool.memset(c.identb[:, :], 0.0).then_inc(s_c, 1)
            pool.memset(c.mask[:, :], 0.0).then_inc(s_c, 1)
            pool.memset(c.sel[:, :, :], 0.0).then_inc(s_c, 1)
            pool.memset(c.zero_i[:, :], 0).then_inc(s_c, 1)
            pool.wait_ge(s_c, 14)
            for m in (c.ident, c.identb):
                pool.affine_select(out=m[:, :], in_=m[:, :], compare_op=ALU.not_equal, fill=1.0, base=0,
                                   pattern=[[-1, P]], channel_multiplier=1).then_inc(s_c, 1)
            pool.affine_select(out=c.mask[:, 0:P], in_=c.mask[:, 0:P], compare_op=ALU.is_ge, fill=-1e30, base=0,
                               pattern=[[-1, P]], channel_multiplier=1).then_inc(s_c, 1)
            pool.affine_select(out=c.mask[:, P:2 * P], in_=c.mask[:, P:2 * P], compare_op=ALU.is_ge, fill=-1e30,
                               base=0, pattern=[[1, P]], channel_multiplier=-1).then_inc(s_c, 1)
            for j in range(3):
                pool.wait_ge(s_c, 18 + j)
                pool.affine_select(out=c.sel[:, :, :], in_=c.sel[:, :, :], compare_op=ALU.not_equal, fill=1.0,
                                   base=-j, pattern=[[-3, HEADS], [0, P]], channel_multiplier=1).then_inc(s_c, 1)


ORDER_A = "ag c0 bx b0 d0 b1 c1 b2 c2 z0 c3 z1 a0 c4 an c5 c6 a1".split()


def phase_a(nc, c):
    KA, KF, KB = 5, 14, 20
    with ExitStack() as x:
        def sb(name, shape, dt=F32):
            return x.enter_context(nc.sbuf_tensor("a_" + name, shape, dt))

        def count(name, per):
            return Count(x.enter_context(nc.semaphore("a_" + name)), per)

        fb = [x.enter_context(nc.psum_tensor(f"a_front{k}", [P, TT], F32)) for k in range(4)]
        bb = [x.enter_context(nc.psum_tensor(f"a_back{k}", [P, TT], F32)) for k in range(4)]

        emb, h0, x1, xn = (sb(n, [P, SUB * D]) for n in ("emb", "h0", "x1", "xn"))
        fst, bst = sb("fst", [P, SUB, 6]), sb("bst", [P, SUB, 6])
        fmv, bmv = sb("fmv", [P, SUB, 2]), sb("bmv", [P, SUB, 2])
        frs, brs = sb("frs", [P, 6, SUB]), sb("brs", [P, 2, SUB])
        xf, xhi, xlo = sb("xf", [P, KC, TT]), sb("xhi", [P, KC, TT], BF16), sb("xlo", [P, KC, TT], BF16)
        ew, kw, ek, ev, num, den, tr = (sb(n, [P, KC, TT]) for n in ("ew", "kw", "ek", "ev", "num", "den", "tr"))
        z = ew
        zhi, zlo = sb("zhi", [P, KC, TT], BF16), sb("zlo", [P, KC, TT], BF16)
        x2, xn2, tr2, mix = (sb(n, [P, SUB * D]) for n in ("x2", "xn2", "tr2", "mix"))
        hs = xn2
        yf, yhi, ylo = sb("yf", [P, KC, TT]), sb("yhi", [P, KC, TT], BF16), sb("ylo", [P, KC, TT], BF16)
        u, sq = sb("u", [P, 2, TT]), sb("sq", [P, 2, TT])
        khi, klo = sb("khi", [P, HC0, TT], BF16), sb("klo", [P, HC0, TT], BF16)

        emb_in = count("emb_in", 16 * SUB)
        emb_used, h_kept = count("emb_used", 1), count("h_kept", 1)
        x1_ready = count("x1_ready", SUB)
        f_var, f_rstd = count("f_var", 1), count("f_rstd", 1)
        b_var, b_rstd = count("b_var", 2), count("b_rstd", 2)
        f_pool, b_pool = count("f_pool", 6), count("b_pool", 2)
        xn_ready, xnT = count("xn_ready", 1), count("xnT", KC)
        x_hi, x_lo = count("x_hi", KC), count("x_lo", KC)
        w_ps, k_ps, v_ps, r_ps = (count(n, KC) for n in ("w_ps", "k_ps", "v_ps", "r_ps"))
        ew_ready, kw_ready, ek_ready, ev_ready = (count(n, KC) for n in ("ew_ready", "kw_ready", "ek_ready", "ev_ready"))
        tr_ready, z_ready, z_hi, z_lo = (count(n, KC) for n in ("tr_ready", "z_ready", "z_hi", "z_lo"))
        o_ps, xn2_ready, xn2T = count("o_ps", 2), count("xn2_ready", 1), count("xn2T", KC)
        x2_ready = count("x2_ready", 2)
        y_hi, y_lo = count("y_hi", KC), count("y_lo", KC)
        rec_ps, tr2_ready = count("rec_ps", 2), count("tr2_ready", 2)
        up_ps, u_ready, sq_ready, k_hi, k_lo = (count(n, HC0) for n in ("up_ps", "u_ready", "sq_ready", "k_hi", "k_lo"))
        val_ps, val_used = count("val_ps", 1), count("val_used", 2)
        xm_ready, xmT, xm_hi, xm_lo = count("xm_ready", 1), count("xmT", KC), count("xm_hi", KC), count("xm_lo", KC)
        a_steps, f_steps, b_steps = count("a_steps", KA), count("f_steps", KF), count("b_steps", KB)

        W = {n: (o, w) for n, (o, w) in OFF_A.items()}

        def wslice(part, name, kc, lo, n):
            o, w = W[name]
            return part[:, o + kc * w + lo:o + kc * w + lo + n]

        def braid(*stages):
            for o in ORDER_A:
                for stage in stages:
                    if o in stage:
                        stage[o]()

        def run(eng, A, B, C, D):
            braid(A(0))
            braid(A(1), B(0))
            braid(A(2), B(1), C(0))
            with eng.Fori(1, TILES - 2) as t:
                braid(A(t + 2), B(t + 1), C(t), D(t - 1))
            braid(B(TILES - 1), C(TILES - 2), D(TILES - 3))
            braid(C(TILES - 1), D(TILES - 2))
            braid(D(TILES - 1))

        block = x.enter_context(nc.Block())

        @block.gpsimd
        def _(pool):
            def rstd(mv, rs, var, ready, own, t, n):
                pool.wait_ge(var.sem, var.at(t, n + 1))
                pool.tensor_tensor(rs[:, 0, :], mv[:, :, 1], c.eps[:, 0:SUB], ALU.add).then_inc(own.sem, 1)
                pool.wait_ge(own.sem, own.at(t, n + 1))
                pool.tensor_tensor(rs[:, 1, :], rs[:, 0, :], c.eps[:, 4:4 + SUB], ALU.pow).then_inc(ready.sem, 1)

            def gather(t):
                for s in range(SUB):
                    pool.indirect_dma_start(emb[:, s * D:(s + 1) * D], None, c.i["emb"],
                                            bass.IndirectOffsetOnAxis(ap=c.idx[:, s:s + 1].bitcast(U32), axis=0)
                                            ).then_inc(emb_in.sem, 16)

            def stage_a(t):
                def ag():
                    if isinstance(t, int):
                        if t > 0:
                            pool.wait_ge(h_kept.sem, h_kept.at(t, 0))
                            pool.wait_ge(emb_used.sem, emb_used.at(t, 0))
                        pool.tensor_copy(c.idx[:, :], c.tok[:, t * SUB:(t + 1) * SUB]).then_inc(c.idx_ready, 1)
                        pool.wait_ge(c.idx_ready, t + 1)
                    else:
                        pool.wait_ge(h_kept.sem, h_kept.at(t, 0))
                        pool.wait_ge(emb_used.sem, emb_used.at(t, 0))
                        pool.tensor_tensor(c.idx[:, :], c.tok[:, bass.ds(t * SUB, SUB)],
                                           c.zero_i[:, :], ALU.add).then_inc(c.idx_ready, 1)
                        pool.wait_ge(c.idx_ready, t + 1)
                        pool.tensor_tensor(c.zero_j[:, :], c.zero_i[:, 0:1], c.zero_i[:, 0:1], ALU.add)
                    gather(t)

                def a0():
                    v, a, r1, b_, d_, r2 = (fmv[:, :, 1],) + tuple(frs[:, k, :] for k in range(5))
                    steps = ((a, v, c.eps[:, 0:SUB], ALU.add), (r1, a, c.eps[:, 4:4 + SUB], ALU.pow),
                             (b_, r1, r1, ALU.mult), (d_, b_, v, ALU.mult), (a, d_, c.eps[:, 0:SUB], ALU.add))
                    pool.wait_ge(f_var.sem, f_var.at(t))
                    for k, (o, p_, q, op) in enumerate(steps):
                        pool.tensor_tensor(o, p_, q, op).then_inc(f_pool.sem, 1)
                        pool.wait_ge(f_pool.sem, f_pool.at(t, k + 1))
                    pool.tensor_tensor(r2, a, c.eps[:, 4:4 + SUB], ALU.pow).then_inc(f_pool.sem, 1)
                    pool.wait_ge(f_pool.sem, f_pool.at(t))
                    pool.tensor_tensor(frs[:, 5, :], r1, r2, ALU.mult).then_inc(f_rstd.sem, 1)

                def a1():
                    for k in range(KC):
                        pool.wait_ge(x_hi.sem, x_hi.at(t, k + 1))
                        pool.tensor_tensor(xlo[:, k, :], xf[:, k, :], xhi[:, k, :], ALU.subtract).then_inc(x_lo.sem, 1)
                return {"ag": ag, "a0": a0, "a1": a1}

            def stage_b(t):
                def fz(k):
                    def f():
                        pool.wait_ge(z_hi.sem, z_hi.at(t, k + 1))
                        pool.tensor_tensor(zlo[:, k, :], z[:, k, :], zhi[:, k, :], ALU.subtract).then_inc(z_lo.sem, 1)
                    return f
                return {"z0": fz(0), "z1": fz(1)}

            def stage_c(t):
                def b0():
                    rstd(bmv, brs, b_var, b_rstd, b_pool, t, 0)

                def b1():
                    for k in range(KC):
                        pool.wait_ge(y_hi.sem, y_hi.at(t, k + 1))
                        pool.tensor_tensor(ylo[:, k, :], yf[:, k, :], yhi[:, k, :], ALU.subtract).then_inc(y_lo.sem, 1)

                def low(*ks):
                    def f():
                        for k in ks:
                            pool.wait_ge(sq_ready.sem, sq_ready.at(t, k + 1))
                            pool.wait_ge(k_hi.sem, k_hi.at(t, k + 1))
                            pool.tensor_tensor(klo[:, k, :], sq[:, k % 2, :], khi[:, k, :],
                                               ALU.subtract).then_inc(k_lo.sem, 1)
                    return f

                def b6():
                    rstd(bmv, brs, b_var, b_rstd, b_pool, t, 1)
                return {"c0": b0, "c1": b1, "c2": low(0, 1), "c3": low(2, 3), "c4": low(4, 5), "c5": low(6, 7), "c6": b6}
            run(pool, stage_a, stage_b, stage_c, lambda t: {})

        @block.scalar
        def _(act):
            def affine(src, f, hi, g, b, psum_ready, ready, low_done, t):
                for k in range(KC):
                    act.wait_ge(psum_ready.sem, psum_ready.at(t, k + 1))
                    act.wait_ge(low_done.sem, low_done.at(t, 0))
                    act.activation(f[:, k, :], src[k][:, :], ACT.Identity, bias=c.vec[:, b + k:b + k + 1],
                                   scale=c.vec[:, g + k:g + k + 1])
                    act.activation(hi[:, k, :], src[k][:, :], ACT.Identity, bias=c.vec[:, b + k:b + k + 1],
                                   scale=c.vec[:, g + k:g + k + 1]).then_inc(ready.sem, 1)

            def stage_a(t):
                def a0():
                    act.wait_ge(emb_in.sem, emb_in.at(t))
                    act.activation(c.h[:, bass.ds(t * SUB * D, SUB * D)], emb[:, :], ACT.Copy,
                                   scale=EMB_SCALE).then_inc(h_kept.sem, 1)

                def a1():
                    affine(fb, xf, xhi, VEC["ln1_g"], VEC["ln1_b"], xnT, x_hi, x_lo, t)

                return {"a0": a0, "a1": a1}

            def stage_b(t):
                def exps(k):
                    def f():
                        act.wait_ge(w_ps.sem, w_ps.at(t, k + 1))
                        act.activation(ew[:, k, :], (fb[2], fb[1])[k][:, :], ACT.Exp).then_inc(ew_ready.sem, 1)
                        act.wait_ge(kw_ready.sem, kw_ready.at(t, k + 1))
                        act.activation(ek[:, k, :], kw[:, k, :], ACT.Exp).then_inc(ek_ready.sem, 1)
                    return f

                def fz(k):
                    def f():
                        if k == 0:
                            for j in range(KC):
                                act.wait_ge(r_ps.sem, r_ps.at(t, j + 1))
                                act.activation(tr[:, j, :], fb[j][:, :], ACT.Tanh, scale=0.5).then_inc(tr_ready.sem, 1)
                        act.wait_ge(z_ready.sem, z_ready.at(t, k + 1))
                        act.activation(zhi[:, k, :], z[:, k, :], ACT.Copy).then_inc(z_hi.sem, 1)
                    return f
                return {"b0": exps(0), "b1": exps(1), "z0": fz(0), "z1": fz(1)}

            def stage_c(t):
                def b1():
                    affine(bb[2:4], yf, yhi, VEC["ln2_g"], VEC["ln2_b"], xn2T, y_hi, y_lo, t)

                def relus(*ks):
                    def f():
                        if ks[0] == 0:
                            for j in range(2):
                                act.wait_ge(rec_ps.sem, rec_ps.at(t, j + 1))
                                act.activation(tr2[:, j * TT:(j + 1) * TT], bb[j][:, :], ACT.Tanh,
                                               scale=0.5).then_inc(tr2_ready.sem, 1)
                        for k in ks:
                            act.wait_ge(up_ps.sem, up_ps.at(t, k + 1))
                            act.wait_ge(sq_ready.sem, sq_ready.at(t, max(k - 1, 0)))
                            act.activation(u[:, k % 2, :], bb[2 + k % 2][:, :], ACT.Relu).then_inc(u_ready.sem, 1)
                            act.wait_ge(u_ready.sem, u_ready.at(t, k + 1))
                            act.activation(khi[:, k, :], u[:, k % 2, :], ACT.Square).then_inc(k_hi.sem, 1)
                            act.wait_ge(k_lo.sem, k_lo.at(t, max(k - 1, 0)))
                            act.activation(sq[:, k % 2, :], u[:, k % 2, :], ACT.Square).then_inc(sq_ready.sem, 1)
                    return f

                return {"c1": b1, "c2": relus(0, 1), "c3": relus(2, 3), "c4": relus(4, 5), "c5": relus(6, 7)}

            def stage_d(t):
                def b7():
                    for k in range(KC):
                        act.wait_ge(xmT.sem, xmT.at(t, k + 1))
                        act.activation(c.xT_hi[:, bass.ds(t * TT + k * N, TT)], bb[2 + k][:, :],
                                       ACT.Copy).then_inc(xm_hi.sem, 1)
                return {"d0": b7}
            run(act, stage_a, stage_b, stage_c, stage_d)

        @block.vector
        def _(dve):
            SA, F, S = Steps(dve, a_steps), Steps(dve, f_steps), Steps(dve, b_steps)

            def norm(S, src, dst, st, mv, rs, var, rstd, t, n, ready=None):
                S.settle()
                for s in range(SUB):
                    S.done(dve.bn_stats(st[:, s, :], src[:, s * D:(s + 1) * D]))
                S.settle()
                S.done(dve.tensor_copy(c.scr[:, 0:1], c.scr[:, 1:2]))
                for s in range(SUB):
                    i = dve.bn_aggr(mv[:, s, :], st[:, s, :])
                i.then_inc(var.sem, 1)
                dve.wait_ge(rstd.sem, rstd.at(t, n + 1))
                for s in range(SUB):
                    i = dve.tensor_scalar(dst[:, s * D:(s + 1) * D], src[:, s * D:(s + 1) * D], mv[:, s, 0:1],
                                          rs[:, 1, s:s + 1], ALU.subtract, ALU.mult)
                    if ready is None or s < SUB - 1:
                        S.done(i)
                if ready is not None:
                    i.then_inc(ready.sem, 1)

            def stage_a(t):
                def a0():
                    SA.begin(t)
                    dve.wait_ge(x1_ready.sem, x1_ready.at(t, 0))
                    dve.wait_ge(emb_in.sem, emb_in.at(t))
                    dve.tensor_scalar(h0[:, :], emb[:, :], EMB_SCALE, None, ALU.mult).then_inc(emb_used.sem, 1)
                    dve.wait_ge(emb_used.sem, emb_used.at(t))
                    for s in range(SUB):
                        SA.done(dve.bn_stats(fst[:, s, :], h0[:, s * D:(s + 1) * D]))
                    SA.settle()
                    SA.done(dve.tensor_copy(c.scr[:, 0:1], c.scr[:, 1:2]))
                    for s in range(SUB):
                        i = dve.bn_aggr(fmv[:, s, :], fst[:, s, :])
                    i.then_inc(f_var.sem, 1)
                    SA.end()

                def an():
                    dve.wait_ge(f_rstd.sem, f_rstd.at(t))
                    for s in range(SUB):
                        i = dve.tensor_scalar(xn[:, s * D:(s + 1) * D], h0[:, s * D:(s + 1) * D], fmv[:, s, 0:1],
                                              frs[:, 5, s:s + 1], ALU.subtract, ALU.mult)
                    i.then_inc(xn_ready.sem, 1)
                return {"a0": a0, "an": an}

            def stage_b(t):
                def bx():
                    F.begin(t)
                    dve.wait_ge(x2_ready.sem, x2_ready.at(t, 0))
                    for s in range(SUB):
                        dve.tensor_scalar(x1[:, s * D:(s + 1) * D], h0[:, s * D:(s + 1) * D], fmv[:, s, 0:1],
                                          frs[:, 1, s:s + 1], ALU.subtract, ALU.mult).then_inc(x1_ready.sem, 1)

                def recur(k):
                    def f():
                        dve.wait_ge(ew_ready.sem, ew_ready.at(t, k + 1))
                        dve.wait_ge(k_ps.sem, k_ps.at(t, k + 1))
                        dve.tensor_tensor(kw[:, k, :], (fb[3], fb[2])[k][:, :], ew[:, k, :],
                                          ALU.subtract).then_inc(kw_ready.sem, 1)
                        dve.wait_ge(ek_ready.sem, ek_ready.at(t, k + 1))
                        dve.wait_ge(v_ps.sem, v_ps.at(t, k + 1))
                        dve.tensor_tensor(ev[:, k, :], (fb[0], fb[3])[k][:, :], ek[:, k, :],
                                          ALU.mult).then_inc(ev_ready.sem, 1)
                        decay = c.dec[:, k:k + 1].to_broadcast([P, SEQ])
                        for b in range(SEQS):
                            q = slice(b * SEQ, (b + 1) * SEQ)
                            F.done(dve.tensor_tensor_scan(den[:, k, q], decay, ek[:, k, q], 0.0, ALU.mult, ALU.add))
                        dve.wait_ge(ev_ready.sem, ev_ready.at(t, k + 1))
                        for b in range(SEQS):
                            q = slice(b * SEQ, (b + 1) * SEQ)
                            F.done(dve.tensor_tensor_scan(num[:, k, q], decay, ev[:, k, q], 0.0, ALU.mult, ALU.add))
                        F.settle()
                        F.done(dve.tensor_scalar(ew[:, k, :], den[:, k, :], 2.0, 2 * WKV_EPS, ALU.mult, ALU.add))
                    return f

                def fz(k):
                    def f():
                        F.settle()
                        F.done(dve.reciprocal(den[:, k, :], ew[:, k, :]))
                        F.settle()
                        F.done(dve.tensor_tensor(kw[:, k, :], num[:, k, :], den[:, k, :], ALU.mult))
                        F.settle()
                        dve.wait_ge(tr_ready.sem, tr_ready.at(t, k + 1))
                        dve.scalar_tensor_tensor(z[:, k, :], tr[:, k, :], 1.0, kw[:, k, :], ALU.add,
                                                 ALU.mult).then_inc(z_ready.sem, 1)
                        if k == KC - 1:
                            F.end()
                    return f
                return {"bx": bx, "b0": recur(0), "b1": recur(1), "z0": fz(0), "z1": fz(1)}

            def stage_c(t):
                def b0():
                    S.begin(t)
                    dve.wait_ge(x1_ready.sem, x1_ready.at(t))
                    for j in range(2):
                        q = slice(j * TT, (j + 1) * TT)
                        dve.wait_ge(o_ps.sem, o_ps.at(t, j + 1))
                        dve.tensor_tensor(x2[:, q], x1[:, q], bb[j][:, :], ALU.add).then_inc(x2_ready.sem, 1)
                    dve.wait_ge(x2_ready.sem, x2_ready.at(t))
                    norm(S, x2, xn2, bst, bmv, brs, b_var, b_rstd, t, 0, xn2_ready)

                def b6():
                    dve.wait_ge(tr2_ready.sem, tr2_ready.at(t))
                    dve.wait_ge(val_ps.sem, val_ps.at(t))
                    for j in range(2):
                        q = slice(j * TT, (j + 1) * TT)
                        dve.scalar_tensor_tensor(mix[:, q], tr2[:, q], 1.0, bb[j][:, :], ALU.add,
                                                 ALU.mult).then_inc(val_used.sem, 1)
                    dve.wait_ge(val_used.sem, val_used.at(t))
                    S.done(dve.scalar_tensor_tensor(hs[:, :], mix[:, :], 0.5, x2[:, :], ALU.mult, ALU.add))
                    S.settle()
                    dve.wait_ge(h_kept.sem, h_kept.at(t))
                    S.done(dve.tensor_copy(c.scr[:, 0:1], c.scr[:, 1:2]))
                    S.done(dve.tensor_tensor(hs[:, :], hs[:, :], c.h[:, bass.ds(t * SUB * D, SUB * D)], ALU.add))
                    norm(S, hs, mix, bst, bmv, brs, b_var, b_rstd, t, 1, xm_ready)
                    S.done(dve.tensor_copy(c.h[:, bass.ds(t * SUB * D, SUB * D)], hs[:, :]))
                    S.end()
                return {"c0": b0, "c6": b6}

            def stage_d(t):
                def b7():
                    for k in range(KC):
                        at = bass.ds(t * TT + k * N, TT)
                        dve.wait_ge(xm_hi.sem, xm_hi.at(t, k + 1))
                        dve.tensor_tensor(c.xT_lo[:, at], bb[2 + k][:, :], c.xT_hi[:, at],
                                          ALU.subtract).then_inc(xm_lo.sem, 1)
                return {"d0": b7}
            run(dve, stage_a, stage_b, stage_c, stage_d)

        @block.tensor
        def _(pe):
            def feature_major(out, name, e, hi, lo, ready, lo_sem, lo_at):
                cols = e * P
                for j, (wp, xp) in enumerate(((c.WA_hi, hi), (c.WA_lo, hi), (c.WA_hi, lo))):
                    if j == 2 and lo_sem is not None:
                        pe.wait_ge(lo_sem, lo_at)
                    for k in range(KC):
                        m = pe.matmul(out[:, :], wslice(wp, name, k, cols, P), xp[:, k, :],
                                      start=(j == 0 and k == 0), stop=(j == 2 and k == KC - 1))
                m.then_inc(ready.sem, 1)

            def token_major(out, name, s, hi, lo):
                for j, (wp, xp) in enumerate(((c.WA_hi, hi), (c.WA_lo, hi), (c.WA_hi, lo))):
                    for k in range(KC):
                        m = pe.matmul(out, xp[:, k, s * P:(s + 1) * P], wslice(wp, name, k, 0, D),
                                      start=(j == 0 and k == 0), stop=(j == 2 and k == KC - 1))
                return m

            def transposes(src, banks, ready):
                for k in range(KC):
                    for s in range(SUB):
                        m = pe.transpose(banks[k][:, s * P:(s + 1) * P], src[:, s * D + k * P:s * D + (k + 1) * P],
                                         c.ident[:, :])
                    m.then_inc(ready.sem, 1)

            def stage_a(t):
                def a1():
                    pe.wait_ge(xn_ready.sem, xn_ready.at(t))
                    pe.wait_ge(tr_ready.sem, tr_ready.at(t, 0))
                    transposes(xn, fb, xnT)
                return {"a1": a1}

            def stage_b(t):
                def f2():
                    pe.wait_ge(x_hi.sem, x_hi.at(t))
                    pe.wait_ge(kw_ready.sem, kw_ready.at(t, 0))
                    feature_major(fb[2], "Ww", 0, xhi, xlo, w_ps, x_lo.sem, x_lo.at(t))
                    pe.wait_ge(ev_ready.sem, ev_ready.at(t, 0))
                    feature_major(fb[3], "Wk", 0, xhi, xlo, k_ps, None, None)
                    feature_major(fb[0], "Wv", 0, xhi, xlo, v_ps, None, None)

                def f3():
                    feature_major(fb[1], "Ww", 1, xhi, xlo, w_ps, None, None)
                    pe.wait_ge(ew_ready.sem, ew_ready.at(t, 1))
                    feature_major(fb[2], "Wk", 1, xhi, xlo, k_ps, None, None)
                    pe.wait_ge(kw_ready.sem, kw_ready.at(t, 1))
                    feature_major(fb[3], "Wv", 1, xhi, xlo, v_ps, None, None)

                def f4():
                    pe.wait_ge(ev_ready.sem, ev_ready.at(t, 1))
                    feature_major(fb[0], "Wr", 0, xhi, xlo, r_ps, None, None)
                    pe.wait_ge(ew_ready.sem, ew_ready.at(t, 2))
                    feature_major(fb[1], "Wr", 1, xhi, xlo, r_ps, None, None)
                return {"b0": f2, "b1": f3, "b2": f4}

            def stage_c(t):
                def b0():
                    pe.wait_ge(z_lo.sem, z_lo.at(t))
                    pe.wait_ge(z_hi.sem, z_hi.at(t))
                    pe.wait_ge(val_used.sem, val_used.at(t, 0))
                    for s in range(SUB):
                        m = token_major(bb[s // 2][:, (s % 2) * D:(s % 2 + 1) * D], "Wo", s, zhi, zlo)
                        if s % 2:
                            m.then_inc(o_ps.sem, 1)

                def b1():
                    pe.wait_ge(xn2_ready.sem, xn2_ready.at(t))
                    pe.wait_ge(xm_lo.sem, xm_lo.at(t, 0))
                    transposes(xn2, bb[2:4], xn2T)

                def up(k):
                    if k >= 2:
                        pe.wait_ge(u_ready.sem, u_ready.at(t, k - 1))
                    feature_major(bb[2 + k % 2], "Wkey", k, yhi, ylo, up_ps, None, None)

                def down(k):
                    if k == 0:
                        pe.wait_ge(tr2_ready.sem, tr2_ready.at(t))
                    pe.wait_ge(k_hi.sem, k_hi.at(t, k + 1))
                    pe.wait_ge(k_lo.sem, k_lo.at(t, k + 1))
                    o, w = W["Wval"]
                    for s in range(SUB):
                        for j, (wp, xp) in enumerate(((c.WA_hi, khi), (c.WA_lo, khi), (c.WA_hi, klo))):
                            m = pe.matmul(bb[s // 2][:, (s % 2) * D:(s % 2 + 1) * D], xp[:, k, s * P:(s + 1) * P],
                                          wp[:, o + k * w:o + (k + 1) * w],
                                          start=(k == 0 and j == 0 and s % 2 == 0), stop=(k == HC0 - 1 and j == 2),
                                          skip_group_check=True)
                    if k == HC0 - 1:
                        m.then_inc(val_ps.sem, 1)

                def b2():
                    pe.wait_ge(y_hi.sem, y_hi.at(t))
                    pe.wait_ge(y_lo.sem, y_lo.at(t))
                    pe.wait_ge(x2_ready.sem, x2_ready.at(t))
                    for s in range(SUB):
                        m = token_major(bb[s // 2][:, (s % 2) * D:(s % 2 + 1) * D], "Wrec", s, yhi, ylo)
                        if s % 2:
                            m.then_inc(rec_ps.sem, 1)
                    up(0)
                    up(1)

                def pairs(k):
                    def f():
                        up(k + 2)
                        down(k)
                        up(k + 3)
                        down(k + 1)
                    return f

                def b6():
                    down(6)
                    down(7)

                return {"c0": b0, "c1": b1, "c2": b2, "c3": pairs(0), "c4": pairs(2), "c5": pairs(4), "c6": b6}

            def stage_d(t):
                def b7():
                    pe.wait_ge(xm_ready.sem, xm_ready.at(t))
                    pe.wait_ge(u_ready.sem, u_ready.at(t))
                    transposes(mix, bb[2:4], xmT)
                return {"d0": b7}
            run(pe, stage_a, stage_b, stage_c, stage_d)


def phase_b(nc, c):
    with ExitStack() as x:
        def sb(name, shape, dt=F32):
            return x.enter_context(nc.sbuf_tensor("b_" + name, shape, dt))

        def count(name, per, base=0):
            return Count(x.enter_context(nc.semaphore("b_" + name)), per, base)

        ub = [x.enter_context(nc.psum_tensor(f"b_up{k}", [P, TT], F32)) for k in range(4)]
        ob = [x.enter_context(nc.psum_tensor(f"b_down{k}", [P, TT], F32)) for k in range(2)]
        W_hi, W_lo = ([sb(f"{n}{p}", [P, COLS_E], BF16) for p in range(2)] for n in ("W_hi", "W_lo"))
        stage = [sb(f"stage{j}", [P, PIECE_E + PIECE_C]) for j in range(2)]
        b1 = [sb(f"b1_{p}", [P, HC0]) for p in range(2)]
        f = sb("f", [P, 4, TT])
        b2 = sb("b2", [P, E0 * D])
        rb = x.enter_context(nc.psum_tensor("b_logits", [P, TILES * SUB * E0], F32))
        lg, ex, sel, m8 = (f[:, j, 0:TILES * SUB * 8].rearrange("p (s e) -> p s e", e=8) for j in range(4))
        rsum = sb("rsum", [P, 2, TILES * SUB])
        lg_ps, lg_shift, lg_exp, w_ready, b2_in = (count(n, 1) for n in ("lg_ps", "lg_shift", "lg_exp", "w_ready", "b2_in"))
        r_steps = count("r_steps", TILES * SUB + 6)
        biased = count("biased", SUB)
        ghi, glo = sb("ghi", [P, HC0, TT], BF16), sb("glo", [P, HC0, TT], BF16)

        up_ps, g_hi, g_lo = count("up_ps", HC0), count("g_hi", HC0), count("g_lo", HC0, 1)
        out_ps, out_used = count("out_ps", 1), count("out_used", SUB, 1)
        landed = [count(f"landed{j}", 16) for j in range(2)]
        w_hi, w_lo = count("w_hi", 1), count("w_lo", 1)
        b1_ready = count("b1_ready", 1)

        def run(eng, step, begin=None):
            def expert(e, par, more):
                if begin:
                    begin(e, par)
                with eng.Fori(0, TILES // 2) as tp:
                    for j in range(2):
                        step(e, par, tp, j, more)
            with eng.Fori(0, E0 // 2 - 1) as pair:
                expert(pair * 2, 0, True)
                expert(pair * 2 + 1, 1, True)
            expert(E0 - 2, 0, True)
            expert(E0 - 1, 1, False)

        block = x.enter_context(nc.Block())

        @block.sync
        def _(sp):
            sp.dma_start(b2[:, :], c.i["b2"].partition_broadcast(P)).then_inc(b2_in.sem, 16)
            for p in range(TILES):
                if p >= 2:
                    sp.wait_ge(w_lo.sem, p - 1)
                sp.dma_start(stage[p % 2][:, :], c.i["WP"][p, :, :]).then_inc(landed[p % 2].sem, 16)

            def step(e, par, tp, j, more):
                if more:
                    g = e * TILES + tp * 2 + (TILES + j)
                    sp.wait_ge(w_lo.sem, g - 1)
                    sp.dma_start(stage[j][:, :], c.i["WP"][bass.ds(g, 1), :, :].rearrange("g p n -> (g p) n")
                                 ).then_inc(landed[j].sem, 16)
            run(sp, step)

        @block.scalar
        def _(act):
            def high(buf, j, piece, piece_c):
                act.activation(c.WC_hi[:, bass.ds(piece_c * PIECE_C, PIECE_C)], stage[j][:, PIECE_E:], ACT.Copy)
                act.activation(buf[:, bass.ds(piece * PIECE_E, PIECE_E)], stage[j][:, 0:PIECE_E],
                               ACT.Copy).then_inc(w_hi.sem, 1)
            for p in range(TILES):
                act.wait_ge(landed[p % 2].sem, 16 * (p // 2 + 1))
                high(W_hi[0], p % 2, p, p)
                if p == 0:
                    act.wait_ge(lg_shift.sem, 1)
                    act.activation(ex[:, :, :], lg[:, :, :], ACT.Exp).then_inc(lg_exp.sem, 1)

            def step(e, par, tp, j, more):
                g = e * TILES + tp * 2 + j
                for k in range(HC0):
                    act.wait_ge(up_ps.sem, up_ps.at(g, k + 1))
                    if k == 0 and j == 0:
                        act.wait_ge(b1_ready.sem, e + 1)
                    act.wait_ge(g_lo.sem, g_lo.at(g, max(k - 3, 0)))
                    if k == HC0 - 1 and more:
                        act.wait_ge(landed[j].sem, (e * (TILES // 2) + tp + (TILES // 2 + 1)) * 16)
                    act.activation(f[:, k % 4, :], ub[k % 4][:, :], ACT.Gelu, bias=b1[par][:, k:k + 1])
                    act.activation(ghi[:, k, :], ub[k % 4][:, :], ACT.Gelu,
                                   bias=b1[par][:, k:k + 1]).then_inc(g_hi.sem, 1)
                if more:
                    high(W_hi[1 - par], j, tp * 2 + j, g + TILES)
            run(act, step)

        @block.vector
        def _(dve):
            def low(hi, lo, j, piece, piece_c):
                q = bass.ds(piece_c * PIECE_C, PIECE_C)
                dve.tensor_tensor(c.WC_lo[:, q], stage[j][:, PIECE_E:], c.WC_hi[:, q], ALU.subtract)
                q = bass.ds(piece * PIECE_E, PIECE_E)
                dve.tensor_tensor(lo[:, q], stage[j][:, 0:PIECE_E], hi[:, q], ALU.subtract).then_inc(w_lo.sem, 1)
            dve.memset(c.scr[:, 0:1], 0.0).then_inc(g_lo.sem, 1)
            dve.memset(c.scr[:, 1:2], 0.0).then_inc(out_used.sem, 1)
            R = Steps(dve, r_steps)
            R.begin(0)
            dve.wait_ge(lg_ps.sem, 1)
            R.done(dve.tensor_tensor(lg[:, :, :], rb[:, :].rearrange("p (s e) -> p s e", e=E0),
                                     c.br[:, :].unsqueeze(1).to_broadcast([P, TILES * SUB, E0]), ALU.add))
            R.settle()
            for s in range(TILES * SUB):
                R.done(dve.max(m8[:, s, :], lg[:, s, :]))
            R.settle()
            R.done(dve.tensor_tensor(sel[:, :, :], lg[:, :, :], m8[:, :, 1:2].to_broadcast([P, TILES * SUB, E0]),
                                     ALU.is_ge))
            R.settle()
            dve.tensor_tensor(lg[:, :, :], lg[:, :, :], m8[:, :, 0:1].to_broadcast([P, TILES * SUB, E0]),
                              ALU.subtract).then_inc(lg_shift.sem, 1)
            dve.wait_ge(w_hi.sem, 1)
            low(W_hi[0], W_lo[0], 0, 0, 0)
            dve.wait_ge(lg_exp.sem, 1)
            R.done(dve.tensor_tensor(sel[:, :, :], ex[:, :, :], sel[:, :, :], ALU.mult))
            R.settle()
            R.done(dve.tensor_reduce(rsum[:, 0, :], sel[:, :, :], AX.X, ALU.add))
            R.settle()
            R.done(dve.reciprocal(rsum[:, 1, :], rsum[:, 0, :]))
            R.settle()
            R.done(dve.tensor_tensor(c.w0[:, :].rearrange("p (s e) -> p s e", e=E0), sel[:, :, :],
                                     rsum[:, 1, :].unsqueeze(2).to_broadcast([P, TILES * SUB, E0]), ALU.mult))
            R.settle()
            R.end()
            for p in range(1, TILES):
                dve.wait_ge(w_hi.sem, p + 1)
                low(W_hi[0], W_lo[0], p % 2, p, p)
            dve.wait_ge(b2_in.sem, 16)

            def begin(e, par):
                dve.tensor_copy(b1[par][:, :], c.b1[:, bass.ds(e * HC0, HC0)]).then_inc(b1_ready.sem, 1)

            def step(e, par, tp, j, more):
                g = e * TILES + tp * 2 + j
                t = tp * 2 + j
                for k in range(HC0):
                    dve.wait_ge(g_hi.sem, g_hi.at(g, k + 1))
                    dve.tensor_tensor(glo[:, k, :], f[:, k % 4, :], ghi[:, k, :], ALU.subtract).then_inc(g_lo.sem, 1)
                if more:
                    dve.wait_ge(w_hi.sem, g + (TILES + 1))
                    low(W_hi[1 - par], W_lo[1 - par], j, tp * 2 + j, g + TILES)
                dve.wait_ge(out_used.sem, out_used.at(g, 0))
                for s in range(SUB):
                    at = bass.ds((t * SUB + s) * D, D)
                    dve.scalar_tensor_tensor(c.h[:, at], b2[:, bass.ds(e * D, D)],
                                             c.w0[:, bass.ds((t * SUB + s) * E0 + e, 1)], c.h[:, at],
                                             ALU.mult, ALU.add).then_inc(biased.sem, 1)
                dve.wait_ge(biased.sem, biased.at(g))
                dve.wait_ge(out_ps.sem, out_ps.at(g))
                for s in range(SUB):
                    at = bass.ds((t * SUB + s) * D, D)
                    dve.scalar_tensor_tensor(c.h[:, at], ob[s // 2][:, (s % 2) * D:(s % 2 + 1) * D],
                                             c.w0[:, bass.ds((t * SUB + s) * E0 + e, 1)], c.h[:, at],
                                             ALU.mult, ALU.add).then_inc(out_used.sem, 1)
            run(dve, step, begin)

        @block.tensor
        def _(pe):
            for s in range(TILES * SUB):
                for n, (xp, p, k) in enumerate((xp, p, k) for xp, ps in ((c.xT_hi, 3), (c.xT_lo, 2))
                                               for p in range(ps) for k in range(KC)):
                    m = pe.matmul(rb[:, s * E0:(s + 1) * E0], xp[:, k * N + s * P:k * N + (s + 1) * P],
                                  c.rw3[0][:, p, k * E0:(k + 1) * E0], start=(n == 0), stop=(n == 5 * KC - 1))
            m.then_inc(lg_ps.sem, 1)

            def step(e, par, tp, j, more):
                g = e * TILES + tp * 2 + j
                t = tp * 2 + j

                def up(k):
                    for n, (wp, xp) in enumerate(((W_hi, c.xT_hi), (W_lo, c.xT_hi), (W_hi, c.xT_lo))):
                        for q in range(KC):
                            m = pe.matmul(ub[k % 4][:, :], wp[par][:, q * H0 + k * P:q * H0 + (k + 1) * P],
                                          xp[:, bass.ds(t * TT + q * N, TT)], start=(n == 0 and q == 0),
                                          stop=(n == 2 and q == KC - 1))
                    m.then_inc(up_ps.sem, 1)

                def down(k):
                    pe.wait_ge(g_hi.sem, g_hi.at(g, k + 1))
                    pe.wait_ge(g_lo.sem, g_lo.at(g, k + 1))
                    if k == 0:
                        pe.wait_ge(out_used.sem, out_used.at(g, 0))
                    w = slice(KC * H0 + k * D, KC * H0 + (k + 1) * D)
                    for s in range(SUB):
                        for n, (wp, xp) in enumerate(((W_hi, ghi), (W_lo, ghi), (W_hi, glo))):
                            m = pe.matmul(ob[s // 2][:, (s % 2) * D:(s % 2 + 1) * D], xp[:, k, s * P:(s + 1) * P],
                                          wp[par][:, w], start=(k == 0 and n == 0 and s % 2 == 0),
                                          stop=(k == HC0 - 1 and n == 2), skip_group_check=True)
                    if k == HC0 - 1:
                        m.then_inc(out_ps.sem, 1)
                pe.wait_ge(w_lo.sem, (e + 1) * TILES)
                up(0)
                up(1)
                for k in range(2, HC0):
                    up(k)
                    down(k - 2)
                down(HC0 - 2)
                down(HC0 - 1)
            run(pe, step)


def heads_order(b, fill, lag=3):
    steps = []
    for h in range(HEADS + lag):
        if h < HEADS:
            steps.append("S%d" % (b * HEADS + h))
        if h >= lag:
            steps.append("V%d" % (b * HEADS + h - lag))
        if h in fill:
            steps.append(str(fill[h]))
    return " ".join(steps)


ORDER_C = " ".join((
    "f2 A0 r2 R0 A1 8 Z0 1 R1 6 Z1 f5 3 g5 2 f6 1 Q0 Q1 2 K0 T0 1 K1 T1 1 M0 1 N0",
    heads_order(0, {8: 1}), "O0",
    "Q2 3 Q3 1 K2 T2 2 K3 T3 1 M1 1 N1",
    heads_order(1, {9: 1}), "O1 1 f13 1 g13 b0 1 f0 1 y0 g0 2 b1 f1 r1"))




def phase_c(nc, c, out):
    KF, KB, KB2 = 90, 13, 13
    PB = 4
    VW = HD + 1
    with ExitStack() as x:
        def sb(name, shape, dt=F32):
            return x.enter_context(nc.sbuf_tensor("c_" + name, shape, dt))

        def count(name, per):
            return Count(x.enter_context(nc.semaphore("c_" + name)), per)

        fb = [x.enter_context(nc.psum_tensor(f"c_front{k}", [P, TT], F32)) for k in range(4)]
        bb = [x.enter_context(nc.psum_tensor(f"c_back{k}", [P, TT], F32)) for k in range(4)]

        room = [c.xT_hi[:, :].bitcast(F32), c.xT_lo[:, :].bitcast(F32)]
        at = [0, 0]

        def reuse(n, which):
            at[which] += n
            assert at[which] <= KC * N // 2
            return room[which][:, at[which] - n:at[which]]

        h2 = sb("h2", [P, SUB * D])
        xn = sb("xn", [P, SUB * D])
        fst, fmv, frs = sb("fst", [P, SUB, 6]), sb("fmv", [P, SUB, 2]), sb("frs", [P, 6, SUB])
        bst, bmv, brs = sb("bst", [P, SUB, 6]), sb("bmv", [P, SUB, 2]), sb("brs", [P, 2, SUB])
        xf = reuse(KC * TT, 0).rearrange("p (k n) -> p k n", k=KC)
        xhi, xlo = sb("xhi", [P, KC, TT], BF16), sb("xlo", [P, KC, TT], BF16)
        kk, vv, tr = (reuse(KC * TT, 0).rearrange("p (k n) -> p k n", k=KC) for _ in range(3))
        T = reuse(5 * TT, 1).rearrange("p (k n) -> p k n", k=5)
        z = reuse(TT, 1)
        pp, av, bv = (sb(n, [P, SEQS, SEQ + 1]) for n in ("pp", "av", "bv"))
        qkr, qsq = (z, reuse(TT, 1)), reuse(TT, 1)
        T_ = T.rearrange("p k n -> p (k n)")
        used = [0]

        def in_T(n):
            used[0] += n
            assert used[0] <= 5 * TT
            return T_[:, used[0] - n:used[0]]
        vf = in_T(D)
        ss, ms, inv, qrs = (sb(n, [P, 2, 2 * HEADS]) for n in ("ss", "ms", "inv", "qrs"))
        qs, ks = sb("qs", [P, HEADS, 64], BF16), sb("ks", [P, HEADS, 64], BF16)
        qT, kT = (a.rearrange("p k n -> p (k n)").bitcast(BF16).rearrange("p (h n) -> p h n", h=HEADS // 2)
                  for a in (kk, vv))
        vh, vl = sb("vh", [P, 2, HEADS, VW], BF16), sb("vl", [P, 2, HEADS, HD], BF16)
        mx, mr = sb("mx", [P, 2, HEADS]), sb("mr", [P, 2, 2, HEADS])
        nstack, negT = sb("nstack", [P, 2, P], BF16), sb("negT", [P, SEQ], BF16)
        npart = nstack[:, :, 0:3 * HEADS].rearrange("p q (h a) -> p q h a", h=HEADS)
        pf = in_T(PB * 3 * P).rearrange("p (b n) -> p b n", b=PB)
        ph, pl = (a.rearrange("p k n -> p (k n)").bitcast(BF16)[:, 0:PB * 3 * P].rearrange("p (b n) -> p b n", b=PB)
                  for a in (tr, xf))
        ou = in_T(2 * HEADS * VW).rearrange("p (q h d) -> p q h d", q=2, h=HEADS)
        den = sb("den", [P, 2, HEADS])
        yn, yf = sb("yn", [P, SUB * D]), sb("yf", [P, KC, TT])
        yhi, ylo = sb("yhi", [P, KC, TT], BF16), sb("ylo", [P, KC, TT], BF16)
        hid_hi = [sb(f"hid_hi{n}", [P, HID // P, TT], BF16) for n in range(3)]
        hid_lo = [sb(f"hid_lo{n}", [P, HID // P, TT], BF16) for n in range(3)]
        g = sb("g", [P, 2, TT])
        sl, sl2 = sb("sl", [P, TT]), sb("sl2", [P, TT])
        lg, pr, wt = (sb(n, [P, SUB, E1]) for n in ("lg", "pr", "wt"))
        gt, eq = sb("gt", [P, SUB, E1, E1]), sb("eq", [P, SUB, E1, E1])
        r1s = sb("r1", [P, 4, SUB])
        below = sb("below", [P, E1, E1])

        f_var, f_rstd, f_pool = count("f_var", 2), count("f_rstd", 2), count("f_pool", 7)
        b_var, b_rstd, b_pool = count("b_var", 1), count("b_rstd", 1), count("b_pool", 3)
        xn_ready, xnT, x_hi, x_lo = count("xn_ready", 3), count("xnT", 3 * KC), count("x_hi", 3 * KC), count("x_lo", 3 * KC)
        k_ps, r_ps, kv_ready, tr_ready = (count(n, KC) for n in ("k_ps", "r_ps", "kv_ready", "tr_ready"))
        arg_ready, z_ready, z_hi, z_lo = (count(n, KC) for n in ("arg_ready", "z_ready", "z_hi", "z_lo"))
        exp_ready = count("exp_ready", 2 * KC)
        o_ps, h2_ready = count("o_ps", 2), count("h2_ready", 2)
        qk_ps, v_ps, qk_sq, v_hi, v_lo, ss_ready, q_rstd, _, q_stack, k_stack = (
            count(n, SUB * m) for n, m in (("qk_ps", 1), ("v_ps", 1), ("qk_sq", 1), ("v_hi", 1), ("v_lo", 1),
                                           ("ss_ready", 1), ("q_rstd", 1), ("q_pool", 0), ("q_stack", 1), ("k_stack", 1)))
        qkT_ps, qkT_ready = count("qkT_ps", 2 * SUB), count("qkT_ready", 2 * SUB)
        S_ps, mx_ready = count("S_ps", 12 * SEQS), count("mx_ready", 12 * SEQS)
        np_ready, negT_ps, negT_ready = (count(n, SEQS) for n in ("np_ready", "negT_ps", "negT_ready"))
        P_ps, p_f, p_hi, pv_ps = (count(n, HEADS * SEQS) for n in ("P_ps", "p_f", "p_hi", "pv_ps"))
        p_lo_dve, p_lo_pool = count("p_lo_dve", SEQS * (HEADS // 3)), count("p_lo_pool", SEQS * (HEADS - HEADS // 3))

        def low_of(t, n):
            b, h = divmod(n, HEADS)
            k = (h + 1) // 3
            if h % 3 == 2:
                return p_lo_dve.sem, p_lo_dve.at(t, b * (HEADS // 3) + k)
            return p_lo_pool.sem, p_lo_pool.at(t, b * (HEADS - HEADS // 3) + h + 1 - k)
        ou_ready = count("ou_ready", 2 * SEQS)
        ao_ps, h3_ready = count("ao_ps", 2), count("h3_ready", 2)
        yn_ready, ynT, y_hi, y_lo = count("yn_ready", 1), count("ynT", KC), count("y_hi", KC), count("y_lo", KC)
        lg_ps, lg_ready, lg_shift, lg_exp = (count(n, 1) for n in ("lg_ps", "lg_ready", "lg_shift", "lg_exp"))
        f0_steps, f_steps, b_steps, b2_steps, g_steps = (
            count(n, m) for n, m in (("f0_steps", 6), ("f_steps", KF), ("b_steps", KB),
                                     ("b2_steps", KB2), ("g_steps", HID // P)))
        stored, set_up = count("stored", 16), count("set_up", 1)

        HC = HID // P
        UPS = {}
        for n, (name, src, ks_, dst, cs) in enumerate((
                ("e2_l1", None, KC, 0, HC), ("e0_up", None, KC, 2, HC), ("e2_l2", 0, HC, 1, HC),
                ("e2_l3", 1, HC, 0, HC), ("e3_down", None, KC, 2, KC), ("e3_up", 2, KC, 1, HC))):
            UPS[name] = (src, ks_, dst, cs)
        WORK = [("up", "e2_l1"), ("up", "e0_up"), ("up", "e2_l2"), ("down", "e0_down", 0, 2),
                ("up", "e3_down"), ("up", "e2_l3"), ("up", "e3_up"), ("down", "e2_l4", 2, 0),
                ("gated", None), ("down", "e3_out", 3, 1), ("down", "e1_down", 1, 0)]
        first_up, first_hid, first_down, nu, nh, nd = {}, {}, {}, 0, 0, 0
        hid_of = {}
        for w in WORK:
            if w[0] == "up":
                first_up[w[1]], first_hid[w[1]] = nu, nh
                nu, nh = nu + UPS[w[1]][3], nh + UPS[w[1]][3]
            elif w[0] == "gated":
                first_up["e1"], first_hid["e1"] = nu, nh
                nu, nh = nu + 2 * HC, nh + HC
            else:
                first_down[w[1]] = nd
                nd += 1
        NU, NH, ND = nu, nh, nd
        assert NU % 2 == 0
        maker = {"e0_down": "e0_up", "e2_l4": "e2_l3", "e3_out": "e3_up", "e1_down": "e1",
                 "e2_l2": "e2_l1", "e2_l3": "e2_l2", "e3_up": "e3_down"}
        up_ps = count("up_ps", NU)
        gate_th, gate_sl = count("gate_th", HC), count("gate_sl", HC)
        hi_ready, lo_ready = count("hi_ready", NH), count("lo_ready", NH)
        down_ps, down_used = count("down_ps", ND), count("down_used", ND * SUB)

        CHUNKS = [(w, k) for w in WORK for k in range(UPS[w[1]][3] if w[0] == "up" else HC)]

        def chunks(up=None, gated=None, down=None):
            steps = {}
            for n, (w, k) in enumerate(CHUNKS):
                if w[0] == "up" and up:
                    steps["w%d" % n] = lambda w=w, k=k: up(w[1], k)
                elif w[0] == "gated" and gated:
                    steps["w%d" % n] = lambda k=k: gated(k)
                elif w[0] == "down" and down:
                    steps["w%d" % n] = lambda w=w, k=k: down(*w[1:], k)
            return steps

        order = ORDER_C.split()
        assert sum(int(o) for o in order if o.isdigit()) == len(CHUNKS), len(CHUNKS)
        ORDER, n = [], 0
        for o in order:
            if o.isdigit():
                ORDER += ["w%d" % (n + j) for j in range(int(o))]
                n += int(o)
            else:
                ORDER.append(o)

        def braid(*stages):
            for o in ORDER:
                for stage in stages:
                    if o in stage:
                        stage[o]()

        def run(eng, front, back):
            FIRST, ROUTER = ("f0", "g0", "f1"), ("b0", "y0", "b1", "r1")

            def first(t):
                return {o: f for o, f in front(t).items() if o in FIRST}

            def rest(t):
                return {o: f for o, f in front(t).items() if o not in FIRST}

            def router(t):
                return {o: f for o, f in back(t).items() if o in ROUTER}

            def experts(t):
                return {o: f for o, f in back(t).items() if o not in ROUTER}
            braid(first(0))
            braid(rest(0), router(0), first(1))
            braid(experts(0), rest(1), router(1), first(2))
            with eng.Fori(1, TILES - 2) as t:
                braid(experts(t), rest(t + 1), router(t + 1), first(t + 2))
            braid(experts(TILES - 2), rest(TILES - 1), router(TILES - 1))
            braid(experts(TILES - 1))

        def group(n):
            if n < 8:
                return [4 * (n // 2) + n % 2 + 2 * j for j in range(2)]
            return [8 * ((n - 8) // 2) + n % 2 + 2 * j for j in range(4)]

        def W(part, name, k, lo, n):
            o, w = OFF_C[name]
            return part[:, o + k * w + lo:o + k * w + lo + n]

        block = x.enter_context(nc.Block())

        @block.sync
        def _(sp):
            with sp.Fori(0, TILES) as t:
                sp.wait_ge(down_used.sem, down_used.at(t))
                sp.dma_start(out[bass.ds(t * TT, TT), :].rearrange("(s p) d -> p s d", p=P),
                             c.h[:, bass.ds(t * SUB * D, SUB * D)].rearrange("p (s d) -> p s d", s=SUB)
                             ).then_inc(stored.sem, 16)
            sp.wait_ge(stored.sem, 16 * TILES)

        @block.gpsimd
        def _(pool):
            def rstd(mv, rs, var, ready, own, t, n, m, centred):
                pool.wait_ge(var.sem, var.at(t, n + 1))
                v = mv[:, :, 1]
                if not centred:
                    pool.tensor_tensor(rs[:, 0, :], mv[:, :, 0], mv[:, :, 0], ALU.mult).then_inc(own.sem, 1)
                    pool.wait_ge(own.sem, own.at(t, m + 1))
                    pool.tensor_tensor(rs[:, 1, :], rs[:, 0, :], v, ALU.add).then_inc(own.sem, 1)
                    pool.wait_ge(own.sem, own.at(t, m + 2))
                    v, m = rs[:, 1, :], m + 2
                pool.tensor_tensor(rs[:, 0, :], v, c.eps[:, 0:SUB] if centred else c.eps[:, 8:8 + SUB],
                                   ALU.add).then_inc(own.sem, 1)
                pool.wait_ge(own.sem, own.at(t, m + 1))
                pool.tensor_tensor(rs[:, 1, :], rs[:, 0, :], c.eps[:, 4:4 + SUB], ALU.pow).then_inc(ready.sem, 1)

            def front(t):
                def both_norms():
                    v, a, r1, b_, d_, r2 = (fmv[:, :, 1],) + tuple(frs[:, k, :] for k in range(5))
                    steps = ((a, v, c.eps[:, 0:SUB], ALU.add), (r1, a, c.eps[:, 4:4 + SUB], ALU.pow),
                             (b_, r1, r1, ALU.mult), (d_, b_, v, ALU.mult), (a, d_, c.eps[:, 8:8 + SUB], ALU.add))
                    pool.wait_ge(f_var.sem, f_var.at(t, 2))
                    for k, (o, p_, q, op) in enumerate(steps):
                        pool.tensor_tensor(o, p_, q, op).then_inc(f_pool.sem, 1)
                        pool.wait_ge(f_pool.sem, f_pool.at(t, k + 2))
                    pool.tensor_tensor(r2, a, c.eps[:, 4:4 + SUB], ALU.pow).then_inc(f_pool.sem, 1)
                    pool.wait_ge(f_pool.sem, f_pool.at(t))
                    pool.tensor_tensor(frs[:, 5, :], r1, r2, ALU.mult).then_inc(f_rstd.sem, 1)

                def low(n):
                    def f():
                        for k in range(KC):
                            pool.wait_ge(x_hi.sem, x_hi.at(t, n * KC + k + 1))
                            pool.tensor_tensor(xlo[:, k, :], xf[:, k, :], xhi[:, k, :],
                                               ALU.subtract).then_inc(x_lo.sem, 1)
                    return f

                def low_weights(n):
                    def f():
                        if n % HEADS % 3 == 2:
                            return
                        pool.wait_ge(p_hi.sem, p_hi.at(t, n + 1))
                        pool.tensor_tensor(pl[:, n % PB, :], pf[:, n % PB, :], ph[:, n % PB, :],
                                           ALU.subtract).then_inc(p_lo_pool.sem, 1)
                    return f
                return {"f0": lambda: rstd(fmv, frs, f_var, f_rstd, f_pool, t, 0, 0, True), "f1": low(0),
                        "f5": both_norms, "f6": low(1), "f13": low(2),
                        **{"S%d" % n: low_weights(n) for n in range(SEQS * HEADS)}}

            def back(t):
                def low(h, dst, k):
                    pool.wait_ge(hi_ready.sem, hi_ready.at(t, h + 1))
                    pool.tensor_tensor(hid_lo[dst][:, k, :], g[:, h % 2, :], hid_hi[dst][:, k, :],
                                       ALU.subtract).then_inc(lo_ready.sem, 1)

                def b1():
                    for k in range(KC):
                        pool.wait_ge(y_hi.sem, y_hi.at(t, k + 1))
                        pool.tensor_tensor(ylo[:, k, :], yf[:, k, :], yhi[:, k, :], ALU.subtract).then_inc(y_lo.sem, 1)
                return {"b0": lambda: rstd(bmv, brs, b_var, b_rstd, b_pool, t, 0, 0, False), "b1": b1,
                        **chunks(up=lambda name, k: low(first_hid[name] + k, UPS[name][2], k),
                                 gated=lambda k: low(first_hid["e1"] + k, 0, k))}
            run(pool, front, back)

        @block.scalar
        def _(act):
            def halves(src, f, hi, gain, psum_ready, ready, low_done, t, n, at_low):
                for k in range(KC):
                    act.wait_ge(psum_ready.sem, psum_ready.at(t, n * KC + k + 1))
                    act.wait_ge(low_done.sem, low_done.at(t, at_low))
                    scale = 1.0 if gain is None else c.vec[:, gain + k:gain + k + 1]
                    act.activation(f[:, k, :], src[k][:, :], ACT.Identity, scale=scale)
                    act.activation(hi[:, k, :], src[k][:, :], ACT.Identity, scale=scale).then_inc(ready.sem, 1)

            def front(t):
                def split(n, gain):
                    return lambda: halves(fb, xf, xhi, gain, xnT, x_hi, x_lo, t, n, n * KC)

                def evacuate(k):
                    def f():
                        b = (fb[2], fb[3]) if k == 0 else (fb[0], fb[1])
                        act.wait_ge(k_ps.sem, k_ps.at(t, k + 1))
                        act.activation(kk[:, k, :], b[0][:, :], ACT.Copy)
                        act.wait_ge(r_ps.sem, r_ps.at(t, k + 1))
                        act.activation(vv[:, k, :], b[1][:, :], ACT.Copy).then_inc(kv_ready.sem, 1)
                        act.activation(tr[:, k, :], b[1][:, :], ACT.Tanh, scale=0.5).then_inc(tr_ready.sem, 1)
                    return f

                def exps(k):
                    def f():
                        act.wait_ge(arg_ready.sem, arg_ready.at(t, k + 1))
                        for j in range(2):
                            act.activation(T[:, 2 * j:2 * j + 2, :], T[:, 2 * j:2 * j + 2, :],
                                           ACT.Exp).then_inc(exp_ready.sem, 1)
                    return f

                def f2():
                    evacuate(0)()
                    evacuate(1)()

                def zsplit(k):
                    def f():
                        act.wait_ge(z_ready.sem, z_ready.at(t, k + 1))
                        act.activation(xhi[:, k, :], z, ACT.Copy).then_inc(z_hi.sem, 1)
                    return f

                def qkv(s):
                    def f():
                        act.wait_ge(qk_ps.sem, qk_ps.at(t, s + 1))
                        if s > 0:
                            act.wait_ge(ss_ready.sem, ss_ready.at(t, s))
                        if s >= 2:
                            act.wait_ge(k_stack.sem, k_stack.at(t, s - 1))
                        act.activation(qkr[s % 2], fb[2][:, :], ACT.Copy)
                        act.activation(qsq, fb[2][:, :], ACT.Square).then_inc(qk_sq.sem, 1)
                        act.wait_ge(v_ps.sem, v_ps.at(t, s + 1))
                        act.wait_ge(v_lo.sem, v_lo.at(t, s))
                        act.activation(vf, fb[3][:, 0:D], ACT.Copy)
                        act.activation(vh[:, s % 2, :, 0:HD], fb[3][:, 0:D].rearrange("p (h d) -> p h d", h=HEADS),
                                       ACT.Copy).then_inc(v_hi.sem, 1)
                        act.wait_ge(ss_ready.sem, ss_ready.at(t, s + 1))
                        act.activation(qrs[:, s % 2, :], inv[:, s % 2, :], ACT.Sqrt).then_inc(q_rstd.sem, 1)
                    return f

                def stacks(s):
                    def f():
                        for j, dst in enumerate((qT, kT)):
                            act.wait_ge(qkT_ps.sem, qkT_ps.at(t, 2 * s + j + 1))
                            act.activation(dst[:, :, (s % 2) * P:(s % 2 + 1) * P],
                                           fb[j][:, :].bitcast(BF16).rearrange("p (h n) -> p h n", h=HEADS // 2),
                                           ACT.Copy).then_inc(qkT_ready.sem, 1)
                    return f

                def negated(b):
                    def f():
                        act.wait_ge(negT_ps.sem, negT_ps.at(t, b + 1))
                        act.activation(negT[:, :], fb[2][:, 0:P].bitcast(BF16), ACT.Copy).then_inc(negT_ready.sem, 1)
                    return f

                def weights(n):
                    def f():
                        act.wait_ge(P_ps.sem, P_ps.at(t, n + 1))
                        if n >= PB:
                            act.wait_ge(*low_of(t, n - PB))
                        act.activation(pf[:, n % PB, :], fb[n % 2][:, 0:3 * P], ACT.Exp).then_inc(p_f.sem, 1)
                    return f

                def output(b):
                    def f():
                        for q in range(2):
                            act.wait_ge(pv_ps.sem, pv_ps.at(t, (b + 1) * HEADS))
                            act.activation(ou[:, q, :, :], fb[2 + q][:, 0:HEADS * VW].rearrange("p (h d) -> p h d", h=HEADS),
                                           ACT.Copy).then_inc(ou_ready.sem, 1)
                    return f
                return {"f1": split(0, None), "f2": f2, "R0": exps(0), "Z0": zsplit(0), "R1": exps(1), "Z1": zsplit(1),
                        "f6": split(1, VEC["n1_w"]), "f13": split(2, None),
                        **{"Q%d" % s: qkv(s) for s in range(SUB)}, **{"T%d" % s: stacks(s) for s in range(SUB)},
                        **{"N%d" % b: negated(b) for b in range(SEQS)}, **{"O%d" % b: output(b) for b in range(SEQS)},
                        **{"S%d" % n: weights(n) for n in range(SEQS * HEADS)}}

            def back(t):
                def b1():
                    halves(bb[2:4], yf, yhi, VEC["n2_w"], ynT, y_hi, y_lo, t, 0, 0)

                def r1():
                    act.wait_ge(lg_shift.sem, lg_shift.at(t))
                    act.activation(pr[:, :, :], lg[:, :, :], ACT.Exp).then_inc(lg_exp.sem, 1)

                def gelu(name, k):
                    u, h, dst = first_up[name] + k, first_hid[name] + k, UPS[name][2]
                    act.wait_ge(up_ps.sem, up_ps.at(t, u + 1))
                    act.wait_ge(lo_ready.sem, lo_ready.at(t, max(h - 1, 0)))
                    act.activation(g[:, h % 2, :], bb[2 + u % 2][:, :], ACT.Gelu)
                    act.activation(hid_hi[dst][:, k, :], bb[2 + u % 2][:, :], ACT.Gelu).then_inc(hi_ready.sem, 1)

                def gated(k):
                    u, h = first_up["e1"] + 2 * k, first_hid["e1"] + k
                    act.wait_ge(up_ps.sem, up_ps.at(t, u + 1))
                    act.activation(sl[:, :], bb[2][:, :], ACT.Tanh, scale=0.5).then_inc(gate_th.sem, 1)
                    act.wait_ge(gate_sl.sem, gate_sl.at(t, k + 1))
                    act.activation(hid_hi[0][:, k, :], g[:, h % 2, :], ACT.Copy).then_inc(hi_ready.sem, 1)
                return {"b1": b1, "r1": r1, **chunks(up=gelu, gated=gated)}
            run(act, front, back)

        @block.vector
        def _(dve):
            F0, F, B, B2, G = (Steps(dve, q) for q in (f0_steps, f_steps, b_steps, b2_steps, g_steps))

            def stats(S, src, st, mv, var, scr):
                S.done(dve.tensor_copy(c.scr[:, scr:scr + 1], c.scr[:, 1:2]))
                for s in range(SUB):
                    S.done(dve.bn_stats(st[:, s, :], src(s)))
                S.settle()
                S.done(dve.tensor_copy(c.scr[:, scr:scr + 1], c.scr[:, 1:2]))
                for s in range(SUB):
                    i = dve.bn_aggr(mv[:, s, :], st[:, s, :])
                i.then_inc(var.sem, 1)

            def apply(dst, src, mv, rs, centred):
                for s in range(SUB):
                    a = (mv[:, s, 0:1], rs[:, s:s + 1], ALU.subtract, ALU.mult) if centred else \
                        (rs[:, s:s + 1], None, ALU.mult)
                    i = dve.tensor_scalar(dst[:, s * D:(s + 1) * D], src(s), *a)
                return i

            dve.memset(pp[:, :, 0:1], -1e38).then_inc(set_up.sem, 1)
            dve.memset(av[:, :, 0:1], 0.0).then_inc(set_up.sem, 1)
            dve.memset(bv[:, :, 0:1], 0.0).then_inc(set_up.sem, 1)
            dve.memset(vh[:, :, :, HD:VW], 1.0).then_inc(set_up.sem, 1)
            dve.memset(qs[:, :, 3 * HD:], 0.0).then_inc(set_up.sem, 1)
            dve.memset(ks[:, :, 3 * HD:], 0.0).then_inc(set_up.sem, 1)
            dve.memset(below[:, :, :], 0.0).then_inc(set_up.sem, 1)
            dve.memset(nstack[:, :, :], 0.0).then_inc(set_up.sem, 1)
            dve.wait_ge(set_up.sem, 8)
            for e in range(1, E1):
                dve.memset(below[:, e, 0:e], 1.0).then_inc(set_up.sem, 1)
            dve.wait_ge(set_up.sem, 8 + E1 - 1)

            def front(t):
                here = bass.ds(t * SUB * D, SUB * D)

                def h_rows(s):
                    return c.h[:, bass.ds(t * SUB * D + s * D, D)]

                def f0():
                    F0.begin(t)
                    dve.wait_ge(xn_ready.sem, xn_ready.at(t, 0))
                    stats(F0, h_rows, fst, fmv, f_var, 2)
                    F0.end()

                def g0():
                    dve.wait_ge(f_rstd.sem, f_rstd.at(t, 1))
                    apply(xn, h_rows, fmv, frs[:, 1, :], True).then_inc(xn_ready.sem, 1)

                def seqs(a, n=SEQ):
                    return a.rearrange("p (b n) -> p b n", b=SEQS)

                def recur_args(k):
                    def f():
                        w, u = c.dec[:, 4 + k:5 + k], c.vec[:, VEC["first1"] + k:VEC["first1"] + k + 1]
                        if k == 0:
                            F.begin(t)
                        dve.wait_ge(kv_ready.sem, kv_ready.at(t, k + 1))
                        for b in range(SEQS):
                            F.done(dve.tensor_tensor_scan(pp[:, b, 1:], w.to_broadcast([P, SEQ]),
                                                          kk[:, k, b * SEQ:(b + 1) * SEQ], -1e38, ALU.add, ALU.max))
                        F.settle()
                        before, now, K = pp[:, :, 0:SEQ], pp[:, :, 1:], seqs(kk[:, k, :])
                        F.done(dve.scalar_tensor_tensor(seqs(T[:, 0, :]), before, w, now, ALU.add, ALU.subtract))
                        F.done(dve.tensor_tensor(seqs(T[:, 1, :]), K, now, ALU.subtract))
                        F.done(dve.scalar_tensor_tensor(seqs(T[:, 4, :]), K, u, before, ALU.add, ALU.max))
                        F.settle()
                        F.done(dve.tensor_tensor(seqs(T[:, 2, :]), before, seqs(T[:, 4, :]), ALU.subtract))
                        dve.scalar_tensor_tensor(T[:, 3, :], kk[:, k, :], u, T[:, 4, :], ALU.add,
                                                 ALU.subtract).then_inc(arg_ready.sem, 1)
                    return f

                def recur(k):
                    def f():
                        V = vv[:, k, :]
                        dve.wait_ge(exp_ready.sem, exp_ready.at(t, 2 * k + 1))
                        F.done(dve.tensor_tensor(T[:, 4, :], T[:, 1, :], V, ALU.mult))
                        for b in range(SEQS):
                            q = slice(b * SEQ, (b + 1) * SEQ)
                            F.done(dve.tensor_tensor_scan(bv[:, b, 1:], T[:, 0, q], T[:, 1, q], 0.0, ALU.mult, ALU.add))
                        F.settle()
                        for b in range(SEQS):
                            q = slice(b * SEQ, (b + 1) * SEQ)
                            F.done(dve.tensor_tensor_scan(av[:, b, 1:], T[:, 0, q], T[:, 4, q], 0.0, ALU.mult, ALU.add))
                        F.settle()
                        dve.wait_ge(exp_ready.sem, exp_ready.at(t, 2 * k + 2))
                        F.done(dve.tensor_tensor(seqs(T[:, 0, :]), seqs(T[:, 2, :]), av[:, :, 0:SEQ], ALU.mult))
                        F.done(dve.tensor_tensor(T[:, 4, :], T[:, 3, :], V, ALU.mult))
                        F.done(dve.tensor_tensor(seqs(T[:, 1, :]), seqs(T[:, 2, :]), bv[:, :, 0:SEQ], ALU.mult))
                        F.settle()
                        F.done(dve.tensor_tensor(T[:, 0, :], T[:, 0, :], T[:, 4, :], ALU.add))
                        F.done(dve.tensor_tensor(T[:, 3, :], T[:, 1, :], T[:, 3, :], ALU.add))
                        F.settle()
                        F.done(dve.reciprocal(T[:, 2, :], T[:, 3, :]))
                        F.settle()
                        F.done(dve.scalar_tensor_tensor(T[:, 1, :], T[:, 0, :], 0.5, T[:, 2, :], ALU.mult, ALU.mult))
                        F.settle()
                        dve.wait_ge(tr_ready.sem, tr_ready.at(t, k + 1))
                        dve.scalar_tensor_tensor(z, tr[:, k, :], 1.0, T[:, 1, :], ALU.add,
                                                 ALU.mult).then_inc(z_ready.sem, 1)
                    return f

                def z_low(k):
                    def f():
                        dve.wait_ge(z_hi.sem, z_hi.at(t, k + 1))
                        dve.tensor_tensor(xlo[:, k, :], z, xhi[:, k, :], ALU.subtract).then_inc(z_lo.sem, 1)
                    return f

                def f5():
                    for j in range(2):
                        q = bass.ds(t * SUB * D + j * TT, TT)
                        dve.wait_ge(o_ps.sem, o_ps.at(t, j + 1))
                        dve.tensor_tensor(c.h[:, q], c.h[:, q], fb[2 + j][:, :], ALU.add).then_inc(h2_ready.sem, 1)
                    dve.wait_ge(h2_ready.sem, h2_ready.at(t))
                    stats(F, h_rows, fst, fmv, f_var, 3)

                def g5():
                    dve.wait_ge(f_rstd.sem, f_rstd.at(t, 2))
                    apply(xn, h_rows, fmv, frs[:, 5, :], True).then_inc(xn_ready.sem, 1)
                    F.done(apply(h2, h_rows, fmv, frs[:, 1, :], True))

                def heads_of(s):
                    return qkr[s % 2].rearrange("p (h d) -> p h d", h=2 * HEADS)

                def squares(s):
                    def f():
                        dve.wait_ge(qk_sq.sem, qk_sq.at(t, s + 1))
                        F.done(dve.tensor_reduce(ss[:, s % 2, :], qsq.rearrange("p (h d) -> p h d", h=2 * HEADS), AX.X,
                                                 ALU.add))
                        F.settle()
                        F.done(dve.tensor_scalar(ms[:, s % 2, :], ss[:, s % 2, :], 1.0 / HD, EPS1, ALU.mult, ALU.add))
                        F.settle()
                        dve.reciprocal(inv[:, s % 2, :], ms[:, s % 2, :]).then_inc(ss_ready.sem, 1)
                        dve.wait_ge(v_hi.sem, v_hi.at(t, s + 1))
                        dve.tensor_tensor(vl[:, s % 2, :, :], vf.rearrange("p (h d) -> p h d", h=HEADS),
                                          vh[:, s % 2, :, 0:HD], ALU.subtract).then_inc(v_lo.sem, 1)
                    return f

                def stack(s):
                    def f():
                        heads = heads_of(s)
                        dve.wait_ge(q_rstd.sem, q_rstd.at(t, s + 1))
                        F.done(dve.tensor_tensor(heads, heads, qrs[:, s % 2, :].unsqueeze(2).to_broadcast(
                            [P, 2 * HEADS, HD]), ALU.mult))
                        F.settle()
                        for j in range(2):
                            part = heads[:, j * HEADS:(j + 1) * HEADS, :]
                            F.done(dve.tensor_tensor(part, part, c.qkw2[:, j * HD:(j + 1) * HD].unsqueeze(1)
                                                     .to_broadcast([P, HEADS, HD]), ALU.mult))
                        F.settle()
                        if s > 0:
                            dve.wait_ge(qkT_ps.sem, qkT_ps.at(t, 2 * s))
                        qh, kh = heads[:, 0:HEADS, :], heads[:, HEADS:, :]
                        F.done(dve.tensor_copy(qs[:, :, 0:HD], qh))
                        F.done(dve.tensor_copy(qs[:, :, HD:2 * HD], qh))
                        F.done(dve.tensor_copy(ks[:, :, 0:HD], kh))
                        F.done(dve.tensor_copy(ks[:, :, 2 * HD:3 * HD], kh))
                        F.settle()
                        dve.tensor_tensor(qs[:, :, 2 * HD:3 * HD], qh, qs[:, :, 0:HD],
                                          ALU.subtract).then_inc(q_stack.sem, 1)
                        dve.tensor_tensor(ks[:, :, HD:2 * HD], kh, ks[:, :, 0:HD],
                                          ALU.subtract).then_inc(k_stack.sem, 1)
                    return f

                def maxima(b):
                    def f():
                        for n in range(12):
                            m = b * 12 + n
                            dve.wait_ge(S_ps.sem, S_ps.at(t, m + 1))
                            if n < 8:
                                o, w = mx[:, 1, group(n)[0]:group(n)[-1] + 1:2], SEQ
                            else:
                                o, w = mx[:, 0, group(n)[0]:group(n)[-1] + 1:2], P
                            dve.tensor_reduce(o, fb[n % 2][:, :].rearrange("p (h k) -> p h k", k=w), AX.X,
                                              ALU.max).then_inc(mx_ready.sem, 1)
                        dve.wait_ge(mx_ready.sem, mx_ready.at(t, (b + 1) * 12))
                        F.done(dve.tensor_scalar(npart[:, :, :, 0], mx[:, :, :], -1.0, None, ALU.mult))
                        F.settle()
                        F.done(dve.scalar_tensor_tensor(mr[:, 0, :, :], mx[:, :, :], -1.0, npart[:, :, :, 0], ALU.mult,
                                                        ALU.subtract))
                        F.settle()
                        F.done(dve.tensor_copy(npart[:, :, :, 1], mr[:, 0, :, :]))
                        F.settle()
                        dve.tensor_tensor(npart[:, :, :, 2], mr[:, 0, :, :], npart[:, :, :, 1],
                                          ALU.subtract).then_inc(np_ready.sem, 1)
                    return f

                def high_weights(n):
                    def f():
                        dve.wait_ge(p_f.sem, p_f.at(t, n + 1))
                        if n >= PB:
                            dve.wait_ge(pv_ps.sem, pv_ps.at(t, n - PB + 1))
                        dve.tensor_copy(ph[:, n % PB, :], pf[:, n % PB, :]).then_inc(p_hi.sem, 1)
                        if n % HEADS % 3 == 2:
                            dve.wait_ge(p_hi.sem, p_hi.at(t, n + 1))
                            dve.tensor_tensor(pl[:, n % PB, :], pf[:, n % PB, :], ph[:, n % PB, :],
                                              ALU.subtract).then_inc(p_lo_dve.sem, 1)
                    return f

                def output(b):
                    def f():
                        dve.wait_ge(ou_ready.sem, ou_ready.at(t, 2 * (b + 1)))
                        F.done(dve.reciprocal(den[:, :, :], ou[:, :, :, HD]))
                        F.settle()
                        for q in range(2):
                            o = xn[:, (2 * b + q) * D:(2 * b + q + 1) * D].rearrange("p (h d) -> p h d", h=HEADS)
                            i = dve.tensor_tensor(o, ou[:, q, :, 0:HD], den[:, q, :].unsqueeze(2).to_broadcast(
                                [P, HEADS, HD]), ALU.mult)
                            if q == 0 or b == 0:
                                F.done(i)
                        if b == SEQS - 1:
                            i.then_inc(xn_ready.sem, 1)
                    return f

                def f13():
                    F.settle()
                    for j in range(2):
                        dve.wait_ge(ao_ps.sem, ao_ps.at(t, j + 1))
                        q = h2[:, j * TT:(j + 1) * TT].rearrange("p (s d) -> p s d", s=2)[:, :, ZERO:]
                        dve.tensor_tensor(q, q, fb[2 + j][:, :].rearrange("p (s d) -> p s d", s=2)[:, :, 0:DZ],
                                          ALU.add).then_inc(h3_ready.sem, 1)
                    F.end()
                return {"f0": f0, "g0": g0, "g5": g5, "A0": recur_args(0), "R0": recur(0), "Z0": z_low(0), "A1": recur_args(1),
                        "R1": recur(1), "Z1": z_low(1), "f5": f5, "g13": f13,
                        **{"Q%d" % s: squares(s) for s in range(SUB)}, **{"K%d" % s: stack(s) for s in range(SUB)},
                        **{"M%d" % b: maxima(b) for b in range(SEQS)}, **{"O%d" % b: output(b) for b in range(SEQS)},
                        **{"S%d" % n: high_weights(n) for n in range(SEQS * HEADS)}}

            def back(t):
                def rows(s):
                    return h2[:, s * D:(s + 1) * D]

                def b0():
                    B.begin(t)
                    dve.wait_ge(h3_ready.sem, h3_ready.at(t))
                    stats(B, rows, bst, bmv, b_var, 0)
                    here = bass.ds(t * SUB * D, SUB * D)
                    B.done(dve.tensor_tensor(c.h[:, here], c.h[:, here], h2[:, :], ALU.add))

                def y0():
                    dve.wait_ge(b_rstd.sem, b_rstd.at(t))
                    apply(yn, rows, bmv, brs[:, 1, :], False).then_inc(yn_ready.sem, 1)

                def over(n):
                    return r1s[:, n, :].unsqueeze(2).to_broadcast([P, SUB, E1])

                def r1():
                    dve.wait_ge(lg_ps.sem, lg_ps.at(t))
                    dve.tensor_copy(pr[:, :, :], bb[0][:, 0:SUB * E1].rearrange("p (s e) -> p s e", s=SUB)
                                    ).then_inc(lg_ready.sem, 1)
                    dve.wait_ge(lg_ready.sem, lg_ready.at(t))
                    dve.wait_ge(down_used.sem, down_used.at(t, 0))
                    B.done(dve.memset(lg[:, :, :], 0.0))
                    B.settle()
                    B.done(dve.tensor_tensor(wt[:, :, :], pr[:, :, :], pr[:, :, :], ALU.is_equal))
                    B.settle()
                    B.done(dve.tensor_copy(c.scr[:, 0:1], c.scr[:, 1:2]))
                    B.done(dve.copy_predicated(lg[:, :, :], wt[:, :, :].bitcast(U32), pr[:, :, :]))
                    B.settle()
                    B.done(dve.tensor_scalar(lg[:, :, :], lg[:, :, :], -3.4028234e38, 3.4028234e38, ALU.max, ALU.min))
                    B.settle()
                    B.done(dve.tensor_reduce(r1s[:, 0, :], lg[:, :, :], AX.X, ALU.max))
                    B.settle()

                    dve.tensor_tensor(lg[:, :, :], lg[:, :, :], over(0), ALU.subtract).then_inc(lg_shift.sem, 1)
                    B.end()

                def r2():
                    B2.begin(t)
                    dve.wait_ge(lg_exp.sem, lg_exp.at(t))
                    B2.done(dve.tensor_reduce(r1s[:, 1, :], pr[:, :, :], AX.X, ALU.add))
                    B2.settle()
                    B2.done(dve.reciprocal(r1s[:, 2, :], r1s[:, 1, :]))
                    B2.settle()
                    B2.done(dve.tensor_tensor(pr[:, :, :], pr[:, :, :], over(2), ALU.mult))
                    B2.settle()
                    pj = pr[:, :, :].unsqueeze(2).to_broadcast([P, SUB, E1, E1])
                    pe_ = pr[:, :, :].unsqueeze(3).to_broadcast([P, SUB, E1, E1])
                    B2.done(dve.tensor_tensor(gt[:, :, :, :], pj, pe_, ALU.is_gt))
                    B2.done(dve.tensor_tensor(eq[:, :, :, :], pj, pe_, ALU.is_equal))
                    B2.settle()
                    B2.done(dve.tensor_tensor(eq[:, :, :, :], eq[:, :, :, :],
                                             below[:, :, :].unsqueeze(1).to_broadcast([P, SUB, E1, E1]), ALU.mult))
                    B2.settle()
                    B2.done(dve.tensor_tensor(gt[:, :, :, :], gt[:, :, :, :], eq[:, :, :, :], ALU.add))
                    B2.settle()
                    B2.done(dve.tensor_reduce(lg[:, :, :], gt[:, :, :, :], AX.X, ALU.add))
                    B2.settle()
                    B2.done(dve.scalar_tensor_tensor(wt[:, :, :], lg[:, :, :], 2.0, pr[:, :, :], ALU.is_lt, ALU.mult))
                    B2.settle()
                    B2.done(dve.tensor_reduce(r1s[:, 0, :], wt[:, :, :], AX.X, ALU.add))
                    B2.settle()
                    B2.done(dve.tensor_scalar(r1s[:, 1, :], r1s[:, 0, :], 1e-8, None, ALU.add))
                    B2.settle()
                    B2.done(dve.reciprocal(r1s[:, 3, :], r1s[:, 1, :]))
                    B2.settle()
                    B2.done(dve.tensor_tensor(wt[:, :, :], wt[:, :, :], over(3), ALU.mult))
                    B2.settle()
                    B2.end()

                def gated(k):
                    h, u = first_hid["e1"] + k, first_up["e1"] + 2 * k
                    if k == 0:
                        G.begin(t)
                    dve.wait_ge(gate_th.sem, gate_th.at(t, k + 1))
                    G.done(dve.scalar_tensor_tensor(sl2[:, :], sl[:, :], 1.0, bb[2][:, :], ALU.add, ALU.mult))
                    G.settle()
                    dve.wait_ge(up_ps.sem, up_ps.at(t, u + 2))
                    dve.wait_ge(lo_ready.sem, lo_ready.at(t, h - 1))
                    dve.scalar_tensor_tensor(g[:, h % 2, :], sl2[:, :], 0.5, bb[3][:, :], ALU.mult,
                                             ALU.mult).then_inc(gate_sl.sem, 1)
                    if k == HC - 1:
                        G.end()

                def down(name, e, src, k):
                    if k < HC - 1:
                        return
                    d = first_down[name]
                    dve.wait_ge(down_ps.sem, down_ps.at(t, d + 1))
                    dve.wait_ge(down_used.sem, down_used.at(t, d * SUB))
                    for s in range(SUB):
                        q = bass.ds((t * SUB + s) * D + ZERO, DZ)
                        dve.scalar_tensor_tensor(c.h[:, q], bb[s // 2][:, (s % 2) * D:(s % 2) * D + DZ],
                                                 wt[:, s, e:e + 1], c.h[:, q], ALU.mult,
                                                 ALU.add).then_inc(down_used.sem, 1)
                return {"b0": b0, "y0": y0, "r1": r1, "r2": r2, **chunks(gated=gated, down=down)}
            run(dve, front, back)

        @block.tensor
        def _(pe):
            PARTS = ((0, 0), (1, 0), (0, 1))
            WC = (c.WC_hi, c.WC_lo)

            def feature_major(bank, name, e, xs, kc=KC, lo_wait=None):
                for j, (wp, xp) in enumerate(PARTS):
                    if j == 2 and lo_wait is not None:
                        pe.wait_ge(*lo_wait)
                    for k in range(kc):
                        m = pe.matmul(bank[:, :], W(WC[wp], name, k, e * P, P), xs[xp][:, k, :],
                                      start=(j == 0 and k == 0), stop=(j == 2 and k == kc - 1))
                return m

            def token_major(o, name, s, xs, n):
                for j, (wp, xp) in enumerate(PARTS):
                    for k in range(KC):
                        m = pe.matmul(o, xs[xp][:, k, s * P:(s + 1) * P], W(WC[wp], name, k, 0, n),
                                      start=(j == 0 and k == 0), stop=(j == 2 and k == KC - 1))
                return m

            def transposes(src, banks, ready):
                for k in range(KC):
                    for s in range(SUB):
                        m = pe.transpose(banks[k][:, s * P:(s + 1) * P], src[:, s * D + k * P:s * D + (k + 1) * P],
                                         c.ident[:, :])
                    m.then_inc(ready.sem, 1)

            X = (xhi, xlo)

            def front(t):
                def f1():
                    pe.wait_ge(xn_ready.sem, xn_ready.at(t, 1))
                    pe.wait_ge(x_hi.sem, x_hi.at(t, 0))
                    transposes(xn, fb, xnT)

                def f2():
                    pe.wait_ge(x_hi.sem, x_hi.at(t, KC))
                    pe.wait_ge(h3_ready.sem, h3_ready.at(t, 0))
                    feature_major(fb[2], "Wk", 0, X, lo_wait=(x_lo.sem, x_lo.at(t, KC))).then_inc(k_ps.sem, 1)
                    feature_major(fb[3], "Wr", 0, X).then_inc(r_ps.sem, 1)
                    feature_major(fb[0], "Wk", 1, X).then_inc(k_ps.sem, 1)
                    feature_major(fb[1], "Wr", 1, X).then_inc(r_ps.sem, 1)

                def f5():
                    pe.wait_ge(z_hi.sem, z_hi.at(t))
                    pe.wait_ge(z_lo.sem, z_lo.at(t))
                    pe.wait_ge(tr_ready.sem, tr_ready.at(t))
                    for s in range(SUB):
                        m = token_major(fb[2 + s // 2][:, (s % 2) * D:(s % 2 + 1) * D], "Wo", s, X, D)
                        if s % 2:
                            m.then_inc(o_ps.sem, 1)

                def f6():
                    pe.wait_ge(xn_ready.sem, xn_ready.at(t, 2))
                    transposes(xn, fb, xnT)

                def qkv(s):
                    def f():
                        if s == 0:
                            pe.wait_ge(x_hi.sem, x_hi.at(t, 2 * KC))
                            pe.wait_ge(x_lo.sem, x_lo.at(t, 2 * KC))
                            pe.wait_ge(h2_ready.sem, h2_ready.at(t))
                        else:
                            pe.wait_ge(v_hi.sem, v_hi.at(t, s))
                        if s == 2:
                            pe.wait_ge(ou_ready.sem, ou_ready.at(t, 2))
                        token_major(fb[2][:, :], "wqk", s, X, 2 * D).then_inc(qk_ps.sem, 1)
                        token_major(fb[3][:, 0:D], "wv", s, X, D).then_inc(v_ps.sem, 1)
                    return f

                def stacks(s):
                    def f():
                        for j, (src, ready) in enumerate(((qs, q_stack), (ks, k_stack))):
                            pe.wait_ge(ready.sem, ready.at(t, s + 1))
                            if s > 0:
                                pe.wait_ge(qkT_ready.sem, qkT_ready.at(t, 2 * s + j - 1))
                            bank = fb[j][:, :].bitcast(BF16)
                            for h in range(HEADS // 2):
                                m = pe.transpose(bank[:, h * P:(h + 1) * P],
                                                 src[:, 2 * h:2 * h + 2, :].rearrange("p a d -> p (a d)"),
                                                 c.identb[:, :])
                            m.then_inc(qkT_ps.sem, 1)
                    return f

                def rows(h):
                    return slice(64 * (h % 2), 64 * (h % 2) + 64)

                def maxima(b):
                    def f():
                        pe.wait_ge(qkT_ready.sem, qkT_ready.at(t, 4 * (b + 1)))
                        for n in range(12):
                            m = b * 12 + n
                            if n >= 2:
                                pe.wait_ge(mx_ready.sem, mx_ready.at(t, m - 1))
                            bank = fb[n % 2]
                            if n < 8:
                                for j, h in enumerate(group(n)):
                                    q = j * SEQ
                                    pe.matmul(bank[:, q:q + SEQ], qT[rows(h), h // 2, P:2 * P], kT[rows(h), h // 2, :],
                                              start=True, stop=False, skip_group_check=True)
                                    i = pe.matmul(bank[:, q + P:q + SEQ], c.identb[:, :], c.mask[:, 0:P],
                                                  start=False, stop=True, skip_group_check=True)
                            else:
                                for j, h in enumerate(group(n)):
                                    q = j * P
                                    pe.matmul(bank[:, q:q + P], qT[rows(h), h // 2, 0:P], kT[rows(h), h // 2, 0:P],
                                              start=True, stop=False, skip_group_check=True)
                                    i = pe.matmul(bank[:, q:q + P], c.identb[:, :], c.mask[:, 0:P],
                                                  start=False, stop=True, skip_group_check=True)
                            i.then_inc(S_ps.sem, 1)
                    return f

                def scores(n):
                    def f():
                        h = n % HEADS
                        bank = fb[n % 2]
                        if h == 0:
                            pe.wait_ge(negT_ready.sem, negT_ready.at(t, n // HEADS + 1))
                        if h >= 2:
                            pe.wait_ge(p_f.sem, p_f.at(t, n - 1))
                        for lo, ks_, qs_ in ((0, 0, 0), (SEQ, P, P)):
                            w = SEQ - qs_
                            pe.matmul(bank[:, lo:lo + w], kT[rows(h), h // 2, ks_:ks_ + P], qT[rows(h), h // 2, qs_:SEQ],
                                      start=True, stop=False, skip_group_check=True)
                            pe.matmul(bank[:, lo:lo + P], c.identb[:, :], c.mask[:, P:2 * P],
                                      start=False, stop=False, skip_group_check=True)
                            i = pe.matmul(bank[:, lo:lo + w], c.sel[:, h, :], negT[:, qs_:SEQ],
                                          start=False, stop=True, skip_group_check=True)
                        i.then_inc(P_ps.sem, 1)
                    return f

                def values(n):
                    def f():
                        h = n % HEADS
                        if h == 0:
                            pe.wait_ge(v_lo.sem, v_lo.at(t, 2 * (n // HEADS + 1)))
                        pe.wait_ge(p_hi.sem, p_hi.at(t, n + 1))
                        pe.wait_ge(*low_of(t, n))
                        for q, blocks in ((0, ((0, 0),)), (1, ((P, 0), (SEQ, 1)))):
                            o = fb[2 + q][:, h * VW:(h + 1) * VW]
                            for a, (lo, kt) in enumerate(blocks):
                                last = a == len(blocks) - 1
                                hi_, lo_ = ph[:, n % PB, lo:lo + P], pl[:, n % PB, lo:lo + P]
                                pe.matmul(o, hi_, vh[:, kt, h, :], start=(a == 0), stop=False, skip_group_check=True)
                                pe.matmul(o[:, 0:HD], hi_, vl[:, kt, h, :], start=False, stop=False,
                                          skip_group_check=True)
                                i = pe.matmul(o, lo_, vh[:, kt, h, :], start=False, stop=last, skip_group_check=True)
                        i.then_inc(pv_ps.sem, 1)
                    return f

                def negated(b):
                    def f():
                        pe.wait_ge(np_ready.sem, np_ready.at(t, b + 1))
                        pe.wait_ge(v_hi.sem, v_hi.at(t, 2 * (b + 1)))
                        bank = fb[2][:, 0:P].bitcast(BF16)
                        for q in range(2):
                            m = pe.transpose(bank[:, q * P:(q + 1) * P], nstack[:, q, :],
                                             c.identb[:, :])
                        m.then_inc(negT_ps.sem, 1)
                    return f

                def f13():
                    pe.wait_ge(xn_ready.sem, xn_ready.at(t, 3))
                    transposes(xn, fb, xnT)

                def g13():
                    pe.wait_ge(x_hi.sem, x_hi.at(t, 3 * KC))
                    pe.wait_ge(x_lo.sem, x_lo.at(t, 3 * KC))
                    for s in range(SUB):
                        m = token_major(fb[2 + s // 2][:, (s % 2) * D:(s % 2) * D + DZ], "wo", s, X, DZ)
                        if s % 2:
                            m.then_inc(ao_ps.sem, 1)
                return {"f1": f1, "f2": f2, "f5": f5, "f6": f6, "f13": f13, "g13": g13,
                        **{"Q%d" % s: qkv(s) for s in range(SUB)}, **{"T%d" % s: stacks(s) for s in range(SUB)},
                        **{"M%d" % b: maxima(b) for b in range(SEQS)}, **{"N%d" % b: negated(b) for b in range(SEQS)},
                        **{"S%d" % n: scores(n) for n in range(SEQS * HEADS)},
                        **{"V%d" % n: values(n) for n in range(SEQS * HEADS)}}

            def back(t):
                def b1():
                    pe.wait_ge(yn_ready.sem, yn_ready.at(t))
                    pe.wait_ge(gate_sl.sem, gate_sl.at(t, 0))
                    transposes(yn, bb[2:4], ynT)

                def r1():
                    pe.wait_ge(y_hi.sem, y_hi.at(t))
                    pe.wait_ge(down_used.sem, down_used.at(t, 0))
                    pe.wait_ge(y_lo.sem, y_lo.at(t))
                    for s in range(SUB):
                        for n, (xp, p, k) in enumerate((xp, p, k) for xp, ps in ((yhi, 3), (ylo, 2))
                                                       for p in range(ps) for k in range(KC)):
                            m = pe.matmul(bb[0][:, s * E1:(s + 1) * E1], xp[:, k, s * P:(s + 1) * P],
                                          c.rw3[1][:, p, k * E1:(k + 1) * E1], start=(n == 0), stop=(n == 5 * KC - 1))
                    m.then_inc(lg_ps.sem, 1)

                def free(u):
                    v, g0 = u - 2, first_up["e1"]
                    if 0 <= v < g0:
                        pe.wait_ge(hi_ready.sem, hi_ready.at(t, v + 1))
                    elif v >= g0:
                        pe.wait_ge(gate_sl.sem, gate_sl.at(t, (v - g0) // 2 + 1))

                def up(name, k):
                    src, kc, dst, cs = UPS[name]
                    xs = (yhi, ylo) if src is None else (hid_hi[src], hid_lo[src])
                    if src is not None and k == 0:
                        h = first_hid[maker[name]] + kc
                        pe.wait_ge(hi_ready.sem, hi_ready.at(t, h))
                        pe.wait_ge(lo_ready.sem, lo_ready.at(t, h))
                    u = first_up[name] + k
                    free(u)
                    feature_major(bb[2 + u % 2], name, k, xs, kc).then_inc(up_ps.sem, 1)

                def gated(k):
                    for j, name in enumerate(("e1_w1", "e1_w2")):
                        u = first_up["e1"] + 2 * k + j
                        free(u)
                        feature_major(bb[2 + u % 2], name, k, (yhi, ylo)).then_inc(up_ps.sem, 1)

                def down(name, e, src, k):
                    d = first_down[name]
                    if k == 0 and d == 0:
                        pe.wait_ge(lg_ready.sem, lg_ready.at(t))
                    elif k == 0:
                        pe.wait_ge(down_used.sem, down_used.at(t, d * SUB))
                    h = first_hid[maker[name]] + k + 1
                    pe.wait_ge(hi_ready.sem, hi_ready.at(t, h))
                    pe.wait_ge(lo_ready.sem, lo_ready.at(t, h))
                    for s in range(SUB):
                        for j, (wp, xp) in enumerate(PARTS):
                            xs = (hid_hi[src], hid_lo[src])[xp]
                            m = pe.matmul(bb[s // 2][:, (s % 2) * D:(s % 2) * D + DZ], xs[:, k, s * P:(s + 1) * P],
                                          W(WC[wp], name, k, 0, DZ), start=(k == 0 and j == 0 and s % 2 == 0),
                                          stop=(k == HC - 1 and j == 2), skip_group_check=True)
                    if k == HC - 1:
                        m.then_inc(down_ps.sem, 1)
                return {"b1": b1, "r1": r1, **chunks(up=up, gated=gated, down=down)}
            run(pe, front, back)


def program(nc, ins, out, upto="c"):
    c = Chip()
    c.i = ins
    with ExitStack() as x:
        def sb(name, shape, dt=F32):
            return x.enter_context(nc.sbuf_tensor(name, shape, dt))
        c.h = sb("h", [P, TILES * SUB * D])
        c.w0 = sb("w0", [P, TILES * SUB * E0])
        c.vec, c.dec = sb("vec", [P, NVEC]), sb("dec", [P, 6])
        c.b1, c.br = sb("b1", [P, E0 * HC0]), sb("br", [P, E0])
        c.rw, c.rw_rest = ([sb(f"{n}{j}", [P, KC * e]) for j, e in enumerate((E0, E1))] for n in ("rw", "rw_rest"))
        c.rw3 = [sb(f"rw_parts{j}", [P, 3, KC * e], BF16) for j, e in enumerate((E0, E1))]
        c.qkw, c.qkw2 = sb("qkw", [P, 2 * HD]), sb("qkw2", [P, 2 * HD])
        c.ident, c.identb = sb("ident", [P, P]), sb("identb", [P, P], BF16)
        c.mask, c.sel = sb("mask", [P, 2 * P], BF16), sb("sel", [P, HEADS, P], BF16)
        c.ones, c.eps, c.scr = sb("ones", [1, P]), sb("eps", [P, 13]), sb("scr", [P, 5])
        c.xT_hi, c.xT_lo = sb("xT_hi", [P, KC * N], BF16), sb("xT_lo", [P, KC * N], BF16)
        with ExitStack() as a:
            def sa(name, shape, dt=F32):
                return a.enter_context(nc.sbuf_tensor(name, shape, dt))
            c.tok, c.idx, c.zero_i = sa("tok_s", [P, TILES * SUB], I32), sa("idx", [P, SUB], I32), sa("zero_i", [P, SUB], I32)
            c.zero_j = sa("zero_j", [P, 1], I32)
            c.WA_hi, c.WA_lo = sa("WA_hi", [P, COLS_A], BF16), sa("WA_lo", [P, COLS_A], BF16)
            c.idx_ready = a.enter_context(nc.semaphore("idx_ready"))
            phase_load(nc, c)
            phase_a(nc, c)
        if upto == "a":
            s = x.enter_context(nc.semaphore("dump"))
            with nc.Block() as block:
                @block.sync
                def _(sp):
                    sp.dma_start(out[0], c.h[:, :]).then_inc(s, 16)
                    sp.dma_start(out[1], c.w0[:, :]).then_inc(s, 16)
                    sp.wait_ge(s, 32)
            return

        c.WC_hi, c.WC_lo = sb("WC_hi", [P, COLS_C], BF16), sb("WC_lo", [P, COLS_C], BF16)
        phase_b(nc, c)
        if upto == "b":
            s = x.enter_context(nc.semaphore("dump"))
            with nc.Block() as block:
                @block.sync
                def _(sp):
                    sp.dma_start(out[0], c.h[:, :]).then_inc(s, 16)
                    sp.wait_ge(s, 16)
            return

        phase_c(nc, c, out)


def pack(np, m):
    k, n = m.shape
    return np.ascontiguousarray(m.reshape(k // P, P, n).transpose(1, 0, 2).reshape(P, -1))


def layout(inputs):
    import numpy as np
    g = {k: np.asarray(v) for k, v in inputs.items()}
    a = {}
    a["tok"] = np.ascontiguousarray(g["x"].reshape(TILES * SUB, P).T)
    a["emb"] = g["L0_tok_W_E"]
    L = "L0_attn_"
    a["WA"] = np.concatenate([pack(np, g[L + n].T) for n in ("Ww", "Wk", "Wv", "Wr", "Wo", "Wrec", "Wkey", "Wval")], 1)
    names = (L + "ln1_g", L + "ln1_b", L + "ln2_g", L + "ln2_b", L + "time_decay", "L1_attn_time_decay",
             "L1_attn_time_first", "L1_ffn_n1_w", "L1_ffn_n2_w")
    a["vec"] = np.concatenate([g[n].reshape(KC, P).T for n in names], 1)
    a["b1"] = np.ascontiguousarray(g["L0_ffn_b1"].reshape(E0 * HC0, P).T)
    a["b2"] = g["L0_ffn_b2"].reshape(E0 * D)
    a["Wrt"] = pack(np, g["L0_ffn_Wr"])
    a["br"] = g["L0_ffn_br"]
    a["gate"] = pack(np, g["L1_ffn_gate_w"].T)
    a["qn"], a["kn"] = g["L1_ffn_qn_w"], g["L1_ffn_kn_w"]
    w0 = np.stack([np.concatenate([pack(np, g["L0_ffn_W1"][e]), pack(np, g["L0_ffn_W2"][e])], 1)
                   for e in range(E0)])
    w0 = w0.reshape(E0, P, TILES, PIECE_E).transpose(0, 2, 1, 3).reshape(PIECES, P, PIECE_E)
    A, Fn = "L1_attn_", "L1_ffn_"
    m = {n: g[A + n].T for n in ("Wk", "Wr", "Wo")}
    m["wqk"] = np.concatenate([g[Fn + "wq"].T, g[Fn + "wk"].T], 1)
    m["wv"], m["wo"] = g[Fn + "wv"].T, g[Fn + "wo"].T[:, ZERO:]
    for n in OFF_C:
        if n[0] == "e":
            m[n] = g[Fn + n].T
            if OFF_C[n][1] == DZ:
                m[n] = m[n][:, ZERO:]
    wc = np.concatenate([pack(np, m[n]) for n in OFF_C], 1).reshape(P, PIECES, PIECE_C).transpose(1, 0, 2)
    a["WP"] = np.concatenate([w0, wc], 2)
    return {k: np.ascontiguousarray(v) for k, v in a.items()}


def kernel(**inputs):
    from concourse import bacc as _bacc
    from concourse.bass_utils import run_bass_kernel_spmd as _run

    arrays = layout(inputs)
    nc = _bacc.Bacc("TRN2", target_bir_lowering=False, num_devices=1)
    ins = {n: nc.dram_tensor(f"in_{n}", list(a.shape), mybir.dt.from_np(a.dtype), kind="ExternalInput").ap()
           for n, a in arrays.items()}
    out = nc.dram_tensor("out", [N, D], F32, kind="ExternalOutput").ap()
    program(nc, ins, out)
    r = _run(nc, [{f"in_{n}": a for n, a in arrays.items()}], core_ids=[0])
    return r.results[0]["out"].reshape(BATCH, SEQ, D)
```
